# Optimizing a Trainium2 kernel written in Bass

```python
import numpy as np
import jax
import jax.numpy as jnp

def _softmax(x, axis=-1):
    return jax.nn.softmax(x, axis=axis)

def _gelu(x):
    return jax.nn.gelu(x, approximate=True)

def _silu(x):
    return jax.nn.silu(x)

def _sigmoid(x):
    return jax.nn.sigmoid(x)

def _layernorm(x, axis=-1, eps=1e-05):
    m = jnp.mean(x, axis=axis, keepdims=True)
    v = jnp.var(x, axis=axis, keepdims=True)
    return (x - m) / jnp.sqrt(v + eps)

def _scatter_add(tgt, idx, src, axis=0):
    return tgt.at[idx].add(src)

def _segment_sum(src, seg, n):
    return jax.ops.segment_sum(src, seg, n)
kernel_name = 'mk_vit_tower_d2_tok_img768_r4_accd10'

def setup_inputs(seed: int=0):
    np.random.seed(seed)
    _w = jnp.asarray

    def _rec_inputs():
        import jax
        import jax.numpy as jnp
        _rk = jax.random.key(seed)
        x = -0.00100294 + 1.00044 * jax.random.normal(jax.random.fold_in(_rk, 1), (4, 3, 224, 224), jnp.float32)
        return x
    x = _rec_inputs()

    def _L0_tok_setup():
        import jax, jax.numpy as jnp
        import numpy as np
        IMAGE_SIZE = 64
        PATCH = 4
        EMBED = 192
        KDIM = 96
        VDIM = 96
        QDIM = 96
        IN_CH = 3
        BATCH = 8
        key = jax.random.key(seed)
        ks = jax.random.split(key, 10)
        s = 0.02
        x = jax.random.normal(ks[0], (BATCH, IN_CH, IMAGE_SIZE, IMAGE_SIZE), dtype=jnp.float32)
        conv_w = jax.random.normal(ks[1], (EMBED, IN_CH, PATCH, PATCH), dtype=jnp.float32) * s
        conv_b = jnp.zeros((EMBED,), dtype=jnp.float32)
        k_w = jax.random.normal(ks[2], (KDIM, EMBED), dtype=jnp.float32) * s
        k_b = jnp.zeros((KDIM,), dtype=jnp.float32)
        v_w = jax.random.normal(ks[3], (VDIM, EMBED), dtype=jnp.float32) * s
        v_b = jnp.zeros((VDIM,), dtype=jnp.float32)
        q_w = jax.random.normal(ks[4], (QDIM, EMBED), dtype=jnp.float32) * s
        q_b = jnp.zeros((QDIM,), dtype=jnp.float32)
        proj_w = jax.random.normal(ks[5], (EMBED, VDIM), dtype=jnp.float32) * s
        proj_b = jnp.zeros((EMBED,), dtype=jnp.float32)
        return {'x': x, 'conv_w': conv_w, 'conv_b': conv_b, 'k_w': k_w, 'k_b': k_b, 'v_w': v_w, 'v_b': v_b, 'q_w': q_w, 'q_b': q_b, 'proj_w': proj_w, 'proj_b': proj_b}
    _L0_tok_all = _L0_tok_setup()
    _L0_tok_in = {k: v for k, v in _L0_tok_all.items() if k in ('conv_w', 'conv_b', 'k_w', 'k_b', 'v_w', 'v_b', 'q_w', 'q_b', 'proj_w', 'proj_b')}
    del _L0_tok_all

    def _L0_attn_setup():
        import jax, jax.numpy as jnp
        import numpy as np
        B, L, D, M = (1, 512, 192, 64)
        key = jax.random.key(seed)
        ks = jax.random.split(key, 9)

        def w(k, shape):
            return jax.random.normal(k, shape, jnp.float32) * shape[0] ** (-0.5)
        x = jax.random.normal(ks[0], (B, L, D), jnp.float32)
        Wq = w(ks[1], (D, M))
        Wk = w(ks[2], (D, M))
        Wv = w(ks[3], (D, D))
        Wf = w(ks[4], (D, M))
        bf = jnp.zeros((M,), jnp.float32)
        Wo = w(ks[5], (D, D))
        gamma = jnp.ones((D,), jnp.float32)
        beta = jnp.zeros((D,), jnp.float32)
        return {'x': x, 'Wq': Wq, 'Wk': Wk, 'Wv': Wv, 'Wf': Wf, 'bf': bf, 'Wo': Wo, 'gamma': gamma, 'beta': beta}
    _L0_attn_all = _L0_attn_setup()
    _L0_attn_in = {k: v for k, v in _L0_attn_all.items() if k in ('Wq', 'Wk', 'Wv', 'Wf', 'bf', 'Wo', 'gamma', 'beta')}
    del _L0_attn_all

    def _L0_ffn_setup():
        import jax, jax.numpy as jnp
        import numpy as np
        B, S, H, D, E = (4, 512, 192, 256, 8)
        TOP_K = 2
        EPS = 1e-08
        LN_EPS = 1e-05

        def _gelu(t):
            return jax.nn.gelu(t, approximate=False)

        def _layer_norm(t, gamma, beta):
            mu = jnp.mean(t, axis=-1, keepdims=True)
            var = jnp.mean(jnp.square(t - mu), axis=-1, keepdims=True)
            return (t - mu) * jax.lax.rsqrt(var + LN_EPS) * gamma + beta
        key = jax.random.key(seed)
        ks = jax.random.split(key, 8)
        x = jax.random.normal(ks[0], (B, S, H), dtype=jnp.float32)
        w1 = jax.random.normal(ks[1], (H, H // 2), dtype=jnp.float32) * 0.02
        b1 = jnp.zeros((H // 2,), dtype=jnp.float32)
        w2 = jax.random.normal(ks[2], (H // 2, E), dtype=jnp.float32) * 0.02
        b2 = jnp.zeros((E,), dtype=jnp.float32)
        a_dn = float(np.sqrt(6.0 / (H + D)))
        a_up = float(np.sqrt(6.0 / (D + H)))
        down_w = jax.random.uniform(ks[3], (E, H, D), dtype=jnp.float32, minval=-a_dn, maxval=a_dn)
        down_b = jnp.zeros((E, D), dtype=jnp.float32)
        up_w = jax.random.uniform(ks[4], (E, D, H), dtype=jnp.float32, minval=-a_up, maxval=a_up)
        gamma = jnp.ones((H,), dtype=jnp.float32)
        beta = jnp.zeros((H,), dtype=jnp.float32)
        return {'x': x, 'w1': w1, 'b1': b1, 'w2': w2, 'b2': b2, 'down_w': down_w, 'down_b': down_b, 'up_w': up_w, 'gamma': gamma, 'beta': beta}
    _L0_ffn_all = _L0_ffn_setup()
    _L0_ffn_in = {k: v for k, v in _L0_ffn_all.items() if k in ('w1', 'b1', 'w2', 'b2', 'down_w', 'down_b', 'up_w', 'gamma', 'beta')}
    del _L0_ffn_all

    def _L1_attn_setup():
        import jax, jax.numpy as jnp
        import numpy as np
        DIM = 192
        HEADS = 12
        HEAD_DIM = DIM // HEADS
        EPS = 1e-12

        def _l1_normalize(t):
            denom = jnp.maximum(jnp.sum(jnp.abs(t), axis=-2, keepdims=True), EPS)
            return t / denom
        key = jax.random.key(seed)
        k1, k2, k3 = jax.random.split(key, 3)
        x = jax.random.normal(k1, (8, 1024, DIM), dtype=jnp.float32)
        s = 1.0 / np.sqrt(DIM)
        w_qkv = jax.random.uniform(k2, (3 * DIM, DIM), dtype=jnp.float32, minval=-s, maxval=s)
        w_proj = jax.random.uniform(k3, (DIM, DIM), dtype=jnp.float32, minval=-s, maxval=s)
        b_proj = jnp.zeros((DIM,), dtype=jnp.float32)
        return {'x': x, 'w_qkv': w_qkv, 'w_proj': w_proj, 'b_proj': b_proj}
    _L1_attn_all = _L1_attn_setup()
    _L1_attn_in = {k: v for k, v in _L1_attn_all.items() if k in ('w_qkv', 'w_proj', 'b_proj')}
    del _L1_attn_all

    def _L1_ffn_setup():
        import jax, jax.numpy as jnp
        import numpy as np
        EPS_NORM = 1e-06
        EPS_Q = 1e-05

        def rmsnorm(x, g):
            return x * jax.lax.rsqrt(jnp.mean(x * x, axis=-1, keepdims=True) + EPS_NORM) * g

        def activation_quant(x):
            scale = 127.0 / jnp.maximum(jnp.max(jnp.abs(x), axis=-1, keepdims=True), EPS_Q)
            return jnp.clip(jnp.round(x * scale), -128, 127) / scale

        def weight_quant(w):
            scale = 1.0 / jnp.maximum(jnp.mean(jnp.abs(w)), EPS_Q)
            return jnp.clip(jnp.round(w * scale), -1, 1) / scale

        def bitlinear(x, w, g):
            x_norm = rmsnorm(x, g)
            x_q = x_norm + jax.lax.stop_gradient(activation_quant(x_norm) - x_norm)
            w_q = w + jax.lax.stop_gradient(weight_quant(w) - w)
            return jnp.einsum('bsd,od->bso', x_q, w_q)
        key = jax.random.key(seed)
        k1, k2, k3 = jax.random.split(key, 3)
        B, S, D, H = (8, 1024, 192, 512)
        x = jax.random.normal(k1, (B, S, D), dtype=jnp.float32)
        w_in = jax.random.normal(k2, (2 * H, D), dtype=jnp.float32) * 0.002
        w_out = jax.random.normal(k3, (D, H), dtype=jnp.float32) * 0.002
        g_in = jnp.ones((D,), dtype=jnp.float32)
        g_out = jnp.ones((H,), dtype=jnp.float32)
        return {'x': x, 'w_in': w_in, 'g_in': g_in, 'w_out': w_out, 'g_out': g_out}
    _L1_ffn_all = _L1_ffn_setup()
    _L1_ffn_in = {k: v for k, v in _L1_ffn_all.items() if k in ('w_in', 'g_in', 'w_out', 'g_out')}
    del _L1_ffn_all
    return {'x': x, 'L0_tok_conv_w': _L0_tok_in['conv_w'], 'L0_tok_conv_b': _L0_tok_in['conv_b'], 'L0_tok_k_w': _L0_tok_in['k_w'], 'L0_tok_k_b': _L0_tok_in['k_b'], 'L0_tok_v_w': _L0_tok_in['v_w'], 'L0_tok_v_b': _L0_tok_in['v_b'], 'L0_tok_q_w': _L0_tok_in['q_w'], 'L0_tok_q_b': _L0_tok_in['q_b'], 'L0_tok_proj_w': _L0_tok_in['proj_w'], 'L0_tok_proj_b': _L0_tok_in['proj_b'], 'L0_attn_Wq': _L0_attn_in['Wq'], 'L0_attn_Wk': _L0_attn_in['Wk'], 'L0_attn_Wv': _L0_attn_in['Wv'], 'L0_attn_Wf': _L0_attn_in['Wf'], 'L0_attn_bf': _L0_attn_in['bf'], 'L0_attn_Wo': _L0_attn_in['Wo'], 'L0_attn_gamma': _L0_attn_in['gamma'], 'L0_attn_beta': _L0_attn_in['beta'], 'L0_ffn_w1': _L0_ffn_in['w1'], 'L0_ffn_b1': _L0_ffn_in['b1'], 'L0_ffn_w2': _L0_ffn_in['w2'], 'L0_ffn_b2': _L0_ffn_in['b2'], 'L0_ffn_down_w': _L0_ffn_in['down_w'], 'L0_ffn_down_b': _L0_ffn_in['down_b'], 'L0_ffn_up_w': _L0_ffn_in['up_w'], 'L0_ffn_gamma': _L0_ffn_in['gamma'], 'L0_ffn_beta': _L0_ffn_in['beta'], 'L1_attn_w_qkv': _L1_attn_in['w_qkv'], 'L1_attn_w_proj': _L1_attn_in['w_proj'], 'L1_attn_b_proj': _L1_attn_in['b_proj'], 'L1_ffn_w_in': _L1_ffn_in['w_in'], 'L1_ffn_g_in': _L1_ffn_in['g_in'], 'L1_ffn_w_out': _L1_ffn_in['w_out'], 'L1_ffn_g_out': _L1_ffn_in['g_out']}

def reference(x, L0_tok_conv_w, L0_tok_conv_b, L0_tok_k_w, L0_tok_k_b, L0_tok_v_w, L0_tok_v_b, L0_tok_q_w, L0_tok_q_b, L0_tok_proj_w, L0_tok_proj_b, L0_attn_Wq, L0_attn_Wk, L0_attn_Wv, L0_attn_Wf, L0_attn_bf, L0_attn_Wo, L0_attn_gamma, L0_attn_beta, L0_ffn_w1, L0_ffn_b1, L0_ffn_w2, L0_ffn_b2, L0_ffn_down_w, L0_ffn_down_b, L0_ffn_up_w, L0_ffn_gamma, L0_ffn_beta, L1_attn_w_qkv, L1_attn_w_proj, L1_attn_b_proj, L1_ffn_w_in, L1_ffn_g_in, L1_ffn_w_out, L1_ffn_g_out):
    import jax
    import jax.numpy as jnp

    def _L0_tok_ref(x, conv_w, conv_b, k_w, k_b, v_w, v_b, q_w, q_b, proj_w, proj_b):
        import jax, jax.numpy as jnp
        import numpy as np
        IMAGE_SIZE = 64
        PATCH = 4
        EMBED = 192
        KDIM = 96
        VDIM = 96
        QDIM = 96
        IN_CH = 3
        BATCH = 8
        h = jax.lax.conv_general_dilated(x, conv_w, window_strides=(PATCH, PATCH), padding='VALID', dimension_numbers=('NCHW', 'OIHW', 'NCHW'))
        h = h + conv_b[None, :, None, None]
        b, e, gh, gw = h.shape
        tokens = h.reshape(b, e, gh * gw).transpose(0, 2, 1)
        k = tokens @ k_w.T + k_b
        v = tokens @ v_w.T + v_b
        q = tokens @ q_w.T + q_b
        scores = jnp.einsum('bnd,bmd->bnm', q, k) / jnp.sqrt(jnp.float32(KDIM))
        attn = jax.nn.softmax(scores, axis=2)
        out = jnp.einsum('bnm,bmd->bnd', attn, v)
        out = out @ proj_w.T + proj_b
        return out

    def _L0_attn_ref(x, Wq, Wk, Wv, Wf, bf, Wo, gamma, beta):
        import jax, jax.numpy as jnp
        import numpy as np
        B, L, D, M = (1, 512, 192, 64)
        m_dim = Wq.shape[1]
        scale = m_dim ** (-0.5)
        q = (jax.nn.elu(x @ Wq) + 1.0) * scale
        k = jax.nn.elu(x @ Wk) + 1.0
        v = x @ Wv
        forget = jax.nn.sigmoid(x @ Wf + bf)
        log_f = jnp.log(jnp.clip(forget, 1e-06, None))
        log_f_cum = jnp.clip(jnp.cumsum(log_f, axis=1), -20.0, 20.0)
        exp_neg = jnp.exp(-log_f_cum)
        exp_pos = jnp.exp(log_f_cum)
        kv = k[..., :, None] * v[..., None, :]
        cum_kv = jnp.cumsum(exp_neg[..., None] * kv, axis=1)
        Mstate = exp_pos[..., None] * cum_kv
        z = exp_pos * jnp.cumsum(exp_neg * k, axis=1)
        numerator = jnp.einsum('blm,blmd->bld', q, Mstate)
        denominator = jnp.einsum('blm,blm->bl', q, z)[..., None] + 1e-06
        h = numerator / denominator
        mu = jnp.mean(h, axis=-1, keepdims=True)
        var = jnp.var(h, axis=-1, keepdims=True)
        normed = (h - mu) / jnp.sqrt(var + 1e-05) * gamma + beta
        return normed @ Wo

    def _L0_ffn_ref(x, w1, b1, w2, b2, down_w, down_b, up_w, gamma, beta):
        import jax, jax.numpy as jnp
        import numpy as np
        B, S, H, D, E = (4, 512, 192, 256, 8)
        TOP_K = 2
        EPS = 1e-08
        LN_EPS = 1e-05

        def _gelu(t):
            return jax.nn.gelu(t, approximate=False)

        def _layer_norm(t, gamma, beta):
            mu = jnp.mean(t, axis=-1, keepdims=True)
            var = jnp.mean(jnp.square(t - mu), axis=-1, keepdims=True)
            return (t - mu) * jax.lax.rsqrt(var + LN_EPS) * gamma + beta
        logits = _gelu(x @ w1 + b1) @ w2 + b2
        routing = jax.nn.softmax(logits, axis=-1)
        topv, topi = jax.lax.top_k(routing, TOP_K)
        sparse = jnp.sum(jax.nn.one_hot(topi, E, dtype=routing.dtype) * topv[..., None], axis=-2)
        sparse = sparse / (jnp.sum(sparse, axis=-1, keepdims=True) + EPS)
        z = _gelu(jnp.einsum('bsh,ehd->bsed', x, down_w) + down_b)
        expert_out = jnp.einsum('bsed,edh->bseh', z, up_w)
        moe_out = jnp.einsum('bseh,bse->bsh', expert_out, sparse)
        return _layer_norm(x + moe_out, gamma, beta)

    def _L1_attn_ref(x, w_qkv, w_proj, b_proj):
        import jax, jax.numpy as jnp
        import numpy as np
        DIM = 192
        HEADS = 12
        HEAD_DIM = DIM // HEADS
        EPS = 1e-12

        def _l1_normalize(t):
            denom = jnp.maximum(jnp.sum(jnp.abs(t), axis=-2, keepdims=True), EPS)
            return t / denom
        B, N, C = x.shape
        hd = C // HEADS
        qkv = x @ w_qkv.T
        qkv = qkv.reshape(B, N, 3, HEADS, hd).transpose(2, 0, 3, 1, 4)
        q, k, v = (qkv[0], qkv[1], qkv[2])
        q = _l1_normalize(q)
        k = _l1_normalize(k)
        if N < hd:
            out = jnp.einsum('bhnd,bhmd,bhme->bhne', q, k, v)
        else:
            kv = jnp.einsum('bhnd,bhne->bhde', k, v)
            out = jnp.einsum('bhnd,bhde->bhne', q, kv)
        out = out.transpose(0, 2, 1, 3).reshape(B, N, C)
        return out @ w_proj.T + b_proj

    def _L1_ffn_ref(x, w_in, g_in, w_out, g_out):
        import jax, jax.numpy as jnp
        import numpy as np
        EPS_NORM = 1e-06
        EPS_Q = 1e-05

        def rmsnorm(x, g):
            return x * jax.lax.rsqrt(jnp.mean(x * x, axis=-1, keepdims=True) + EPS_NORM) * g

        def activation_quant(x):
            scale = 127.0 / jnp.maximum(jnp.max(jnp.abs(x), axis=-1, keepdims=True), EPS_Q)
            return jnp.clip(jnp.round(x * scale), -128, 127) / scale

        def weight_quant(w):
            scale = 1.0 / jnp.maximum(jnp.mean(jnp.abs(w)), EPS_Q)
            return jnp.clip(jnp.round(w * scale), -1, 1) / scale

        def bitlinear(x, w, g):
            x_norm = rmsnorm(x, g)
            x_q = x_norm + jax.lax.stop_gradient(activation_quant(x_norm) - x_norm)
            w_q = w + jax.lax.stop_gradient(weight_quant(w) - w)
            return jnp.einsum('bsd,od->bso', x_q, w_q)
        h = bitlinear(x, w_in, g_in)
        up, gate = jnp.split(h, 2, axis=-1)
        y = jax.nn.silu(gate) * up
        return bitlinear(y, w_out, g_out)
    h = _L0_tok_ref(x, L0_tok_conv_w, L0_tok_conv_b, L0_tok_k_w, L0_tok_k_b, L0_tok_v_w, L0_tok_v_b, L0_tok_q_w, L0_tok_q_b, L0_tok_proj_w, L0_tok_proj_b)
    h = h + _L0_attn_ref(_layernorm(h, axis=-1), L0_attn_Wq, L0_attn_Wk, L0_attn_Wv, L0_attn_Wf, L0_attn_bf, L0_attn_Wo, L0_attn_gamma, L0_attn_beta)
    h = h + _L0_ffn_ref(_layernorm(h, axis=-1), L0_ffn_w1, L0_ffn_b1, L0_ffn_w2, L0_ffn_b2, L0_ffn_down_w, L0_ffn_down_b, L0_ffn_up_w, L0_ffn_gamma, L0_ffn_beta)
    h = h + _L1_attn_ref(_layernorm(h, axis=-1), L1_attn_w_qkv, L1_attn_w_proj, L1_attn_b_proj)
    h = h + _L1_ffn_ref(_layernorm(h, axis=-1), L1_ffn_w_in, L1_ffn_g_in, L1_ffn_w_out, L1_ffn_g_out)
    return h

_drawn_inputs = setup_inputs


def setup_inputs(seed=0):
    import zlib

    import numpy as np

    out = dict(_drawn_inputs(seed))
    spreads = {'L0_tok_conv_b': (0.0, 0.1),
     'L0_tok_k_b': (0.0, 2.0),
     'L0_tok_v_b': (0.0, 0.1),
     'L0_tok_q_b': (0.0, 0.8),
     'L0_tok_proj_b': (0.0, 0.1),
     'L0_attn_bf': (0.0, 2.0),
     'L0_attn_gamma': (1.0, 0.2),
     'L0_attn_beta': (0.0, 0.1),
     'L0_ffn_b1': (0.0, 0.8),
     'L0_ffn_b2': (0.0, 0.1),
     'L0_ffn_down_b': (0.0, 0.335),
     'L0_ffn_gamma': (1.0, 0.2),
     'L0_ffn_beta': (0.0, 0.1),
     'L1_attn_b_proj': (0.0, 0.1),
     'L1_ffn_g_in': (1.0, 0.6),
     'L1_ffn_g_out': (1.0, 0.6)}
    factors = {'x': 8.0,
     'L0_tok_conv_w': 8.0,
     'L0_tok_k_w': 8.0,
     'L0_tok_q_w': 8.0,
     'L0_attn_Wq': 8.0,
     'L0_attn_Wk': 8.0,
     'L0_attn_Wf': 27.664,
     'L0_ffn_w2': 8.0,
     'L1_attn_w_qkv': 43.513,
     'L1_attn_w_proj': 47.26,
     'L1_ffn_w_in': 8.0,
     'L1_ffn_w_out': 8.0}
    for name, (base, spread) in spreads.items():
        noise = np.random.default_rng([zlib.crc32(name.encode()), seed]).standard_normal(out[name].shape)
        drawn = base * np.exp(spread * noise) if base else spread * noise
        out[name] = jnp.asarray(drawn.astype(out[name].dtype))
    for name, factor in factors.items():
        out[name] = (out[name] * factor).astype(out[name].dtype)
    return out
```

```python
from contextlib import ExitStack

import concourse.bass as bass
from concourse import mybir

F32 = mybir.dt.float32
F32R = mybir.dt.float32r
BF16 = mybir.dt.bfloat16
ACT = mybir.ActivationFunctionType
ALU = mybir.AluOpType
AX = mybir.AxisListType

B = 4
TOK = 3136
D = 192
KC = 96
T = 112
TPI = TOK // T
NT = B * TPI
CH = 448
TPC = CH // T
CPI = TOK // CH
NC = B * CPI
X1 = 49
LO = 64
XS = LO + X1
KT = 25
KEYS = KT * 128
ZMIN = -13.815509557963773
SHIFT_SLOT = 11
PROJECT_SLOTS = (2, 4)
SLOTS = 13



def allocator(nc, ctx):
    def sb(name, shape, dt=F32):
        return ctx.enter_context(nc.sbuf_tensor(name, shape, dt))

    def ps(name, shape, dt=F32):
        return ctx.enter_context(nc.psum_tensor(name, shape, dt))

    def sem(name):
        return ctx.enter_context(nc.semaphore(name))
    return sb, ps, sem


def mixer_phase(nc, ins, h, bns, eye):
    with ExitStack() as ctx:
        sb, ps, sem = allocator(nc, ctx)
        conv = sb("conv", [KC, 2, X1])
        wqkv = sb("wqkv", [KC, 3, 2, 96])
        bqkv = sb("bqkv", [1, 3, 96])
        projT = sb("projT", [96, D + 1])
        projb = sb("projb", [1, D + 1])
        e48 = sb("e48", [1, 128])
        wT = sb("wT", [96, 3, 128])
        A2 = sb("A2", [X1, XS])
        W2 = sb("W2", [128, D + 1])
        eyer = sb("eyer", [T, T], F32R)
        x32 = [sb(f"x32_{i}", [XS, KEYS]) for i in range(2)]
        xhl = [sb(f"xhl_{i}", [XS, KEYS], F32R) for i in range(2)]
        xkey = [sb(f"xkey_{i}", [128, KT, LO]) for i in range(2)]
        y32 = sb("y32", [XS, CH])
        ysum = sb("ysum", [XS, CH])
        yh1 = sb("yh1", [XS, CH], F32R)
        yh = sb("yh", [XS, CH], F32R)
        yl = sb("yl", [XS, CH], F32R)
        pmax = sb("pmax", [T, TPC, CPI])
        negmax = sb("negmax", [T, TPC, XS], F32R)
        prob = [sb(f"prob{i}", [128, 2, CH]) for i in range(3)]
        oT = sb("oT", [128, CH])
        rden = sb("rden", [T, TPC, 1])

        pscore = [ps(f"pscore{i}", [128, 2, 512]) for i in range(2)]
        ppre = [ps(f"ppre{i}", [T, 512]) for i in range(2)]
        pout = ps("pout", [128, 512])
        pmisc = ps("pmisc", [128, 512])

        w_in = sem("w_in")
        x_in = [sem(f"x_in{i}") for i in range(2)]
        zeroed = sem("zeroed")
        x_split = sem("x_split")
        fold_mm = sem("fold_mm")
        folded = sem("folded")
        y_mm = sem("y_mm")
        y_out = sem("y_out")
        pre_mm = sem("pre_mm")
        pre_max = sem("pre_max")
        max_ready = sem("max_ready")
        shift_mm = sem("shift_mm")
        y_shifted = sem("y_shifted")
        scores = sem("scores")
        exped = sem("exped")
        pv = sem("pv")
        o_out = sem("o_out")
        proj_mm = sem("proj_mm")
        proj_out = sem("proj_out")
        dvec = sem("dvec")
        block = ctx.enter_context(nc.Block())

        @block.sync
        def _(sp):
            sp.dma_start(conv[:], ins["conv"]).then_inc(w_in, 16)
            sp.dma_start(wqkv[:], ins["wqkv"]).then_inc(w_in, 16)
            sp.dma_start(bqkv[:], ins["bqkv"]).then_inc(w_in, 16)
            sp.dma_start(projT[:], ins["projT"]).then_inc(w_in, 16)
            sp.dma_start(projb[:], ins["projb"]).then_inc(w_in, 16)
            sp.dma_start(e48[:], ins["e48"]).then_inc(w_in, 16)
            sp.dma_start(eye[:], ins["eye"]).then_inc(w_in, 16)
            for b in range(B):
                if b < 2:
                    sp.wait_ge(zeroed, b + 1)
                else:
                    sp.wait_ge(pv, SLOTS * CPI * (b - 1))
                sp.dma_start(x32[b % 2][0:X1, 0:TOK], ins["xT"][b]).then_inc(x_in[b % 2], 16)
                sp.dma_start(x32[b % 2][LO:XS, 0:TOK], ins["xT"][b]).then_inc(x_in[b % 2], 16)
                sp.dma_start(xkey[b % 2][:], ins["xkey"][b]).then_inc(x_in[b % 2], 16)

        @block.gpsimd
        def _(pool):
            nc.gpsimd.memset(x32[0][:], 0.0).then_inc(zeroed, 1)
            nc.gpsimd.memset(x32[1][:], 0.0).then_inc(zeroed, 1)
            nc.gpsimd.memset(negmax[:].bitcast(F32), 0.0).then_inc(zeroed, 1)
            nc.gpsimd.memset(wT[:], 0.0).then_inc(zeroed, 1)
            for b in range(B):
                pool.wait_ge(x_in[b % 2], 48 * (b // 2 + 1))
                pool.wait_ge(x_split, 2 * b) if b else pool.wait_ge(zeroed, 4)
                if b >= 2:
                    pool.wait_ge(pv, SLOTS * CPI * (b - 1))
                nc.gpsimd.tensor_copy(xhl[b % 2][:], x32[b % 2][:]).then_inc(x_split, 1)
                pool.wait_ge(x_split, 2 * b + 1)
                nc.gpsimd.tensor_tensor(xhl[b % 2][LO:XS, :], x32[b % 2][LO:XS, :],
                                        xhl[b % 2][LO:XS, :].bitcast(F32), ALU.subtract).then_inc(x_split, 1)

        @block.scalar
        def _(act):
            def slots(g):
                for j in range(SLOTS):
                    act.wait_ge(scores, g * SLOTS + j + 1)
                    if j >= 3:
                        act.wait_ge(pv, g * SLOTS + j - 2)
                    elif j == 0 and not (isinstance(g, int) and g == 0):
                        act.wait_ge(pv, g * SLOTS)
                    if j < SLOTS - 1:
                        nc.scalar.activation(prob[j % 3][:, :, :], pscore[j % 2][:, :, 0:CH],
                                             ACT.Exp).then_inc(exped, 1)
                    else:
                        nc.scalar.activation(prob[j % 3][:, 0, :], pscore[j % 2][:, 0, 0:CH],
                                             ACT.Exp).then_inc(exped, 1)

            nc.scalar.preload_act_table(ACT.Exp)
            slots(0)
            with act.Fori(1, NC) as g:
                slots(g)

        @block.tensor
        def _(pe):
            pe.wait_ge(w_in, 16 * 7)
            for i in range(3):
                for c in range(2):
                    pe.matmul(pmisc[0:96, i * 64:i * 64 + X1], wqkv[:, i, c, :], conv[:, c, :],
                              start=(c == 0), stop=False)
                pe.matmul(pmisc[0:96, i * 64:i * 64 + X1], bqkv[:, i, :], e48[:, 0:X1],
                          start=False, stop=True).then_inc(fold_mm, 1)
            pe.wait_ge(folded, 5)
            pe.matmul(ppre[0][0:X1, 0:XS], wT[:, 0, 0:X1], wT[:, 1, 0:XS], start=True, stop=True).then_inc(fold_mm, 1)
            pe.matmul(pout[:, 0:D + 1], wT[:, 2, :], projT[:], start=True, stop=False)
            pe.matmul(pout[:, 0:D + 1], e48[:], projb[:], start=False, stop=True).then_inc(fold_mm, 1)
            pe.wait_ge(folded, 8)

            def make_y(g, b, c):
                pe.matmul(pmisc[0:XS, 0:CH], A2[:], x32[b % 2][0:X1, bass.ds(c * CH, CH)],
                          start=True, stop=True).then_inc(y_mm, 1)

            def first_scores(g, b, k):
                q, kc = k // CPI, k % CPI
                pe.wait_ge(pre_max, g * TPC * CPI + k - 1) if k >= 2 else pe.wait_ge(pre_max, g * TPC * CPI)
                pe.matmul(ppre[k % 2][:, 0:CH], yh1[:, q * T:(q + 1) * T],
                          xhl[b % 2][:, kc * CH:(kc + 1) * CH], start=True, stop=True).then_inc(pre_mm, 1)

            def shift(g):
                pe.wait_ge(max_ready, (g + 1) * TPC)
                for q in range(TPC):
                    mm = pe.matmul(pmisc[0:XS, q * T:(q + 1) * T], negmax[:, q, :], eyer[:],
                                   start=True, stop=True)
                mm.then_inc(shift_mm, 1)

            def slot_scores(g, b, j, between=lambda: None):
                if j >= 2:
                    pe.wait_ge(exped, g * SLOTS + j - 1)
                elif j == 0:
                    pe.wait_ge(exped, g * SLOTS)
                for i in range(2 if j < SLOTS - 1 else 1):
                    k = 2 * j + i
                    out, keys = pscore[j % 2][:, i, 0:CH], xhl[b % 2][:, k * 128:(k + 1) * 128]
                    pe.matmul(out, keys, yh[:], start=True, stop=False)
                    mm = pe.matmul(out, keys, yl[:], start=False, stop=True)
                    if j == SLOTS - 1 or i == 1:
                        mm.then_inc(scores, 1)
                    between()

            def slot_pv(g, b, j):
                pe.wait_ge(exped, g * SLOTS + j + 1)
                if j == 0:
                    pe.wait_ge(o_out, g)
                if j < SLOTS - 1:
                    for i in range(2):
                        mm = pe.matmul(pout[i * LO:(i + 1) * LO, 0:CH], xkey[b % 2][:, 2 * j + i, :],
                                       prob[j % 3][:, i, :], start=(j == 0), stop=(i == 1 and j == SLOTS - 2),
                                       tile_position=(0, i * LO))
                else:
                    mm = pe.matmul(pout[0:LO, 0:CH], xkey[b % 2][:, 2 * j, :], prob[j % 3][:, 0, :],
                                   start=False, stop=True, tile_position=(0, 0))
                mm.then_inc(pv, 1)

            def project(g, r):
                for i in range(2):
                    q = 2 * r + i
                    mm = pe.matmul(pmisc[0:T, i * (D + 1):(i + 1) * (D + 1)], oT[:, q * T:(q + 1) * T], W2[:],
                                   start=True, stop=True, skip_group_check=True)
                mm.then_inc(proj_mm, 1)

            def chunk(g, b, nxt, first=False, last=False):
                pe.wait_ge(y_shifted, 2 * g + 2)
                todo = list(range(TPC * CPI)) if nxt is not None else []

                def first_pass():
                    if todo:
                        first_scores(g + 1, nxt[0], todo.pop(0))

                slot_scores(g, b, 0)
                for j in range(SLOTS):
                    if j == 1 and nxt is not None:
                        pe.wait_ge(y_out, 2 * (g + 2))
                    run = first_pass if 1 <= j < SHIFT_SLOT else lambda: None
                    if j < SLOTS - 1:
                        slot_scores(g, b, j + 1, run)
                    if j == 0 and nxt is not None:
                        if not first:
                            pe.wait_ge(y_shifted, 2 * g + 2)
                        if nxt[0] != b:
                            pe.wait_ge(x_split, 2 * (nxt[0] + 1))
                        make_y(g + 1, *nxt)
                    if j in PROJECT_SLOTS and not first:
                        if j == PROJECT_SLOTS[0]:
                            pe.wait_ge(o_out, g)
                            if nxt is not None:
                                pe.wait_ge(y_out, 2 * (g + 2))
                        else:
                            pe.wait_ge(proj_out, 4 * g - 2)
                        project(g - 1, PROJECT_SLOTS.index(j))
                    if j == SHIFT_SLOT and nxt is not None:
                        if not first:
                            pe.wait_ge(proj_out, 4 * g)
                        shift(g + 1)
                    slot_pv(g, b, j)
                    run()

            pe.wait_ge(x_split, 2)
            make_y(0, 0, 0)
            pe.wait_ge(y_out, 2)
            for k in range(TPC * CPI):
                first_scores(0, 0, k)
            shift(0)
            for b in range(B):
                chunk(b * CPI, b, (b, 1), first=(b == 0))
                with pe.Fori(1, CPI - 1) as c:
                    chunk(b * CPI + c, b, (b, c + 1))
                chunk(b * CPI + CPI - 1, b, (b + 1, 0) if b + 1 < B else None)
            pe.wait_ge(o_out, NC)
            project(NC - 1, 0)
            pe.wait_ge(proj_out, 4 * NC - 2)
            project(NC - 1, 1)

        @block.vector
        def _(dve):
            dve.wait_ge(w_in, 16 * 7)
            nc.vector.tensor_copy(eyer[:], eye[0:T, 0:T]).then_inc(folded, 1)
            dve.wait_ge(zeroed, 4)
            dve.wait_ge(fold_mm, 3)
            nc.vector.tensor_scalar(wT[:, 0, 0:X1], pmisc[0:96, 0:X1], 96 ** -0.5, None,
                                    ALU.mult).then_inc(folded, 1)
            nc.vector.tensor_copy(wT[:, 1:3, 0:X1],
                                  pmisc[0:96, 64:192].rearrange("p (i c) -> p i c", i=2)[:, :, 0:X1]).then_inc(folded, 1)
            nc.vector.tensor_copy(wT[:, 1, LO:XS], pmisc[0:96, 64:64 + X1]).then_inc(folded, 1)
            nc.vector.tensor_copy(wT[:, 2, LO:XS], pmisc[0:96, 128:128 + X1]).then_inc(folded, 1)
            dve.wait_ge(fold_mm, 5)
            nc.vector.tensor_copy(A2[:], ppre[0][0:X1, 0:XS]).then_inc(folded, 1)
            nc.vector.tensor_copy(W2[:], pout[:, 0:D + 1]).then_inc(folded, 1)
            nc.vector.memset(pmax[:], 0.0).then_inc(folded, 1)

            def take_y(g):
                dve.wait_ge(y_mm, g + 1)
                nc.vector.tensor_copy(yh1[:], pmisc[0:XS, 0:CH]).then_inc(y_out, 1)
                nc.vector.tensor_copy(y32[:], pmisc[0:XS, 0:CH]).then_inc(y_out, 1)

            def take_max(g, k):
                q, kc = k // CPI, k % CPI
                dve.wait_ge(pre_mm, g * TPC * CPI + k + 1)
                nc.vector.reduce_max(pmax[:, q, kc:kc + 1], ppre[k % 2][:, 0:CH], AX.X).then_inc(pre_max, 1)
                if kc == CPI - 1:
                    dve.wait_ge(pre_max, g * TPC * CPI + k + 1)
                    nc.vector.tensor_reduce(negmax[:, q, X1 - 1:XS:LO],
                                            pmax[:, q:q + 1, :].broadcast_to([T, 2, CPI]),
                                            AX.X, ALU.max, negate=True).then_inc(max_ready, 1)

            def shift_y(g, first=False):
                dve.wait_ge(shift_mm, g + 1)
                dve.wait_ge(y_out, 2 * (g + 1))
                nc.vector.tensor_tensor(ysum[:], y32[:], pmisc[0:XS, 0:CH], ALU.add).then_inc(dvec, 1)
                dve.wait_ge(dvec, g + 1)
                if not first:
                    dve.wait_ge(scores, g * SLOTS)
                nc.vector.tensor_copy(yh[:], ysum[:]).then_inc(y_shifted, 1)
                dve.wait_ge(y_shifted, 2 * g + 1)
                nc.vector.tensor_tensor(yl[:], ysum[:], yh[:].bitcast(F32), ALU.subtract).then_inc(y_shifted, 1)

            def take_o(g):
                dve.wait_ge(pv, (g + 1) * SLOTS)
                nc.vector.tensor_copy(oT[:], pout[:, 0:CH]).then_inc(o_out, 1)

            def take_projected(g, r):
                dve.wait_ge(proj_mm, 2 * g + r + 1)
                two = pmisc[0:T, 0:2 * (D + 1)].rearrange("p (i c) -> p i c", i=2)
                nc.vector.reciprocal(rden[:, 2 * r:2 * r + 2, :], two[:, :, D:D + 1]).then_inc(proj_rden, 1)
                dve.wait_ge(proj_rden, 2 * g + r + 1)
                for i in range(2):
                    nc.vector.tensor_scalar(h[:, g * TPC + 2 * r + i, :], two[:, i, 0:D], rden[:, 2 * r + i, :], None,
                                            ALU.mult).then_inc(proj_out, 1)

            def take_stats(g):
                for q in range(TPC):
                    nc.vector.bn_stats(bns[:, g * TPC + q, :], h[:, g * TPC + q, :]).then_inc(stat_out, 1)

            proj_rden, stat_out = sem("proj_rden"), sem("stat_out")

            def chunk(g, first=False, last=False):
                if not last:
                    take_y(g + 1)
                    for k in range(TPC * CPI):
                        if not first and k in (5, 11):
                            take_projected(g - 1, (5, 11).index(k))
                        if not first and k == 14:
                            dve.wait_ge(proj_out, 4 * g)
                        take_max(g + 1, k)
                        if not first and k == 14:
                            take_stats(g - 1)
                    shift_y(g + 1)
                else:
                    take_projected(g - 1, 0)
                    take_projected(g - 1, 1)
                    dve.wait_ge(proj_out, 4 * g)
                    take_stats(g - 1)
                take_o(g)

            take_y(0)
            for k in range(TPC * CPI):
                take_max(0, k)
            shift_y(0, first=True)
            chunk(0, first=True)
            with dve.Fori(1, NC - 1) as g:
                chunk(g)
            chunk(NC - 1, last=True)
            take_projected(NC - 1, 0)
            take_projected(NC - 1, 1)
            dve.wait_ge(proj_out, 4 * NC)
            take_stats(NC - 1)


def finish_stats(nc, name, bns, mean, rstd, vtok, eps):
    with ExitStack() as ctx:
        sb, ps, sem = allocator(nc, ctx)
        dif = sb(f"dif_{name}", [T, NT])
        var = sb(f"var_{name}", [T, NT])
        mhalf = sb(f"mhalf_{name}", [T, NT])
        done = sem(f"stats_{name}")
        ready = sem(f"var_{name}_ready")
        block = ctx.enter_context(nc.Block())

        @block.vector
        def _(dve):
            nc.vector.tensor_tensor(mean[:], bns[:, :, 1], bns[:, :, 4], ALU.add).then_inc(done, 1)
            nc.vector.tensor_tensor(dif[:], bns[:, :, 1], bns[:, :, 4], ALU.subtract).then_inc(done, 1)
            nc.vector.tensor_tensor(var[:], bns[:, :, 2], bns[:, :, 5], ALU.add).then_inc(done, 1)
            dve.wait_ge(done, 3)
            nc.vector.tensor_scalar(mean[:], mean[:], 0.5, None, ALU.mult).then_inc(done, 1)
            nc.vector.scalar_tensor_tensor(dif[:], dif[:], D / 4, dif[:], ALU.mult, ALU.mult).then_inc(done, 1)
            dve.wait_ge(done, 5)
            nc.vector.tensor_tensor(var[:], var[:], dif[:], ALU.add).then_inc(done, 1)
            dve.wait_ge(done, 6)
            nc.vector.tensor_scalar(vtok[:], var[:], 1.0 / D, None, ALU.mult).then_inc(done, 1)
            dve.wait_ge(done, 7)
            nc.vector.tensor_scalar(var[:], vtok[:], eps, None, ALU.add).then_inc(ready, 1)

        @block.gpsimd
        def _(pool):
            nc.gpsimd.memset(mhalf[:], -0.5).then_inc(ready, 1)
            pool.wait_ge(ready, 2)
            nc.gpsimd.tensor_tensor(rstd[:], var[:], mhalf[:], ALU.pow)


def retention_phase(nc, ins, h, bns, mean, rstd, eye):
    M = 64
    V1 = D + 1
    with ExitStack() as ctx:
        sb, ps, sem = allocator(nc, ctx)
        wqk = sb("wqk", [KC, 2, 128])
        wff = sb("wff", [KC, 2, 128])
        bff = sb("bff", [128, 1])
        wv = sb("wv", [KC, 2, D])
        wo = sb("wo", [KC + 1, 2, D])
        gam = sb("gam", [KC, 2])
        bet = sb("bet", [KC, 2])
        sgn = sb("sgn", [128, 1])
        mask = sb("mask", [T, T])
        ones = sb("ones_scan", [128, CH])
        eps5 = sb("eps5", [T, TPC])
        mhalf = sb("mhalf4", [T, TPC])
        xn = sb("xn2", [T, TPC, D])
        xT = sb("xT2", [KC, 2, CH])
        gate = sb("gate2", [128, CH])
        elu = sb("elu2", [128, CH])
        cum = sb("cum2", [128, CH])
        dec = sb("dec2", [128, CH])
        tail = sb("tail2", [128, 1])
        qt = sb("qt2", [M, CH])
        kt = sb("kt2", [M, CH])
        ktok = sb("ktok2", [T, TPC, M])
        vt = sb("vt2", [T, TPC, V1])
        at = sb("at2", [T, TPC, T])
        snap = sb("snap2", [M, TPC, V1])
        den = sb("den2", [T, TPC, 1])
        hh = sb("hh2", [T, TPC, D])
        bn = sb("bn2", [T, TPC, 6])
        agg = sb("agg2", [T, TPC, 2])
        veps = sb("veps2", [T, TPC])
        rst = sb("rst2", [T, TPC])
        nT = sb("nT2", [KC + 1, 2, CH])
        ptr = ps("ptr2", [KC, 2, 512])
        pqk = ps("pqk2", [128, 512])
        pff = ps("pff2", [128, 512])
        pvo = ps("pvo2", [T, 2, 512])
        pat = ps("pat2", [T, 512])
        pst = ps("pst2", [M, 512])

        names = ("w_in", "w_ready", "brow_mm", "xn_ready", "xtr_mm", "xT_out", "qk_mm", "ff_mm", "v_mm", "v_out",
                 "nrm_ready", "ntr_mm", "nT_out", "wo_mm", "h_out", "gate_in", "gate_out", "elu_in", "elu_out",
                 "cum_out", "dec_out", "qk_out", "ktr_mm", "ktok_out", "at_mm", "at_out", "st_mm", "snap_out",
                 "num_mm", "hhc", "hh_out", "agg_out", "rst_out", "dvec", "poolc")
        S = {n: sem(f"{n}_2") for n in names}
        block = ctx.enter_context(nc.Block())

        @block.sync
        def _(sp):
            for dst, name in ((wqk, "wqk"), (wff, "wff"), (bff, "bff"), (wv, "wv"), (gam, "gam2"),
                              (bet, "bet2"), (sgn, "sgn"), (mask, "mask")):
                sp.dma_start(dst[:], ins[name]).then_inc(S["w_in"], 16)
            sp.dma_start(wo[0:KC], ins["wo2"]).then_inc(S["w_in"], 16)

        @block.gpsimd
        def _(pool):
            for n, (buf, value) in enumerate(((ones[:], 1.0), (eps5[:], 1e-5), (mhalf[:], -0.5),
                                              (vt[:, :, D:V1], 1.0), (nT[KC:KC + 1], 1.0))):
                nc.gpsimd.memset(buf, value).then_inc(S["w_ready"], 1)
                pool.wait_ge(S["w_ready"], n + 1)

            def chunk(g, first=False):
                if not first:
                    pool.wait_ge(S["rst_out"], g)
                pool.wait_ge(S["agg_out"], g + 1)
                nc.gpsimd.tensor_tensor(veps[:], agg[:, :, 1], eps5[:], ALU.add).then_inc(S["poolc"], 1)
                pool.wait_ge(S["poolc"], g + 1)
                nc.gpsimd.tensor_tensor(rst[:], veps[:], mhalf[:], ALU.pow).then_inc(S["rst_out"], 1)

            chunk(0, first=True)
            with pool.Fori(1, NC) as g:
                chunk(g)

        @block.tensor
        def _(pe):
            pe.wait_ge(S["w_in"], 16 * 9)
            for c in range(2):
                mm = pe.matmul(pst[0:1, 0:D], bet[:, c:c + 1], wo[0:KC, c, :], start=(c == 0), stop=(c == 1))
            mm.then_inc(S["brow_mm"], 1)
            pe.wait_ge(S["w_ready"], 5 + 3)

            def front(g, first):
                pe.wait_ge(S["xn_ready"], g + 1)
                for q in range(TPC):
                    for c in range(2):
                        mm = pe.transpose(ptr[:, c, q * T:(q + 1) * T], xn[:, q, c * KC:(c + 1) * KC], eye[0:T, 0:T])
                mm.then_inc(S["xtr_mm"], 1)
                pe.wait_ge(S["xT_out"], g + 1)
                if not first:
                    pe.wait_ge(S["ktok_out"], g)
                for c in range(2):
                    mm = pe.matmul(pff[:, 0:CH], wff[:, c, :], xT[:, c, :], start=(c == 0), stop=(c == 1))
                mm.then_inc(S["ff_mm"], 1)
                for c in range(2):
                    mm = pe.matmul(pqk[:, 0:CH], wqk[:, c, :], xT[:, c, :], start=(c == 0), stop=(c == 1))
                mm.then_inc(S["qk_mm"], 1)
                if not first:
                    pe.wait_ge(S["hh_out"], g)
                for q in range(TPC):
                    for c in range(2):
                        mm = pe.matmul(pvo[:, q // 2, (q % 2) * V1:(q % 2) * V1 + D], xT[:, c, q * T:(q + 1) * T],
                                       wv[:, c, :], start=(c == 0), stop=(c == 1), skip_group_check=True)
                mm.then_inc(S["v_mm"], 1)

            def tail_out(g):
                pe.wait_ge(S["nrm_ready"], g + 1)
                for q in range(TPC):
                    for c in range(2):
                        mm = pe.transpose(ptr[:, c, q * T:(q + 1) * T], hh[:, q, c * KC:(c + 1) * KC], eye[0:T, 0:T])
                mm.then_inc(S["ntr_mm"], 1)
                pe.wait_ge(S["nT_out"], g + 1)

            def wo_out(g):
                for q in range(TPC):
                    for c in range(2):
                        k = KC + 1 if c == 0 else KC
                        mm = pe.matmul(pvo[:, q // 2, (q % 2) * V1:(q % 2) * V1 + D], nT[0:k, c, q * T:(q + 1) * T],
                                       wo[0:k, c, :], start=(c == 0), stop=(c == 1), skip_group_check=True)
                mm.then_inc(S["wo_mm"], 1)

            def attend(g, reset, first):
                pe.wait_ge(S["qk_out"], g + 1)
                for q in range(TPC):
                    mm = pe.matmul(pat[:, q * T:(q + 1) * T], kt[:, q * T:(q + 1) * T], qt[:, q * T:(q + 1) * T],
                                   start=True, stop=True)
                mm.then_inc(S["at_mm"], 1)
                for q in range(TPC):
                    mm = pe.transpose(pff[0:T, q * M:(q + 1) * M], kt[:, q * T:(q + 1) * T], eye[0:M, 0:M])
                mm.then_inc(S["ktr_mm"], 1)
                if not first:
                    pe.wait_ge(S["h_out"], g)
                pe.wait_ge(S["ktok_out"], g + 1)
                pe.wait_ge(S["at_out"], g + 1)
                for q in range(TPC):
                    if not (reset and q == 0):
                        pe.wait_ge(S["snap_out"], g * TPC + q)
                    num = pvo[:, q // 2, (q % 2) * V1:(q % 2 + 1) * V1]
                    pe.matmul(pst[:, 0:V1], ktok[:, q, :], vt[:, q, :], start=(reset and q == 0), stop=True,
                              skip_group_check=True).then_inc(S["st_mm"], 1)
                    mm = pe.matmul(num, at[:, q, :], vt[:, q, :], start=True, stop=(reset and q == 0),
                                   skip_group_check=True)
                    if not (reset and q == 0):
                        mm = pe.matmul(num, qt[:, q * T:(q + 1) * T], snap[:, q, :], start=False, stop=True,
                                       skip_group_check=True)
                mm.then_inc(S["num_mm"], 1)

            def chunk(g, reset=False, first=False):
                front(g, first)
                if not first:
                    tail_out(g - 1)
                pe.wait_ge(S["v_out"], g + 1)
                if not first:
                    wo_out(g - 1)
                attend(g, reset, first)

            chunk(0, reset=True, first=True)
            with pe.Fori(1, CPI) as c:
                chunk(c)
            with pe.Fori(1, B) as b:
                chunk(b * CPI, reset=True)
                with pe.Fori(1, CPI) as c:
                    chunk(b * CPI + c)
            tail_out(NC - 1)
            wo_out(NC - 1)

        @block.scalar
        def _(act):
            nc.scalar.preload_act_table_set("natural_log_exp_and_others")
            act.wait_ge(S["w_ready"], 5 + 3)

            def nT_copy(g):
                act.wait_ge(S["ntr_mm"], g + 1)
                nc.scalar.copy(nT[0:KC, :, :], ptr[:, :, 0:CH]).then_inc(S["nT_out"], 1)

            def chunk(g, reset=False, first=False):
                act.wait_ge(S["xtr_mm"], g + 1)
                nc.scalar.copy(xT[:, :, :], ptr[:, :, 0:CH]).then_inc(S["xT_out"], 1)
                act.wait_ge(S["gate_in"], g + 1)
                nc.scalar.activation(gate[:], gate[:], ACT.Exp, scale=-1.0).then_inc(S["gate_out"], 1)
                act.wait_ge(S["gate_out"], 2 * g + 1)
                nc.scalar.activation(gate[:], gate[:], ACT.Ln, bias=1.0).then_inc(S["gate_out"], 1)
                act.wait_ge(S["elu_in"], g + 1)
                nc.scalar.activation(elu[:], elu[:], ACT.Exp).then_inc(S["elu_out"], 1)
                act.wait_ge(S["v_mm"], g + 1)
                for i in range(2):
                    cp = nc.scalar.copy(vt[:, 2 * i:2 * i + 2, 0:D],
                                        pvo[:, i, 0:2 * V1].rearrange("p (q v) -> p q v", q=2)[:, :, 0:D])
                cp.then_inc(S["v_out"], 1)
                act.wait_ge(S["cum_out"], g + 1)
                nc.scalar.activation(dec[:], cum[:], ACT.Exp, scale=sgn[:]).then_inc(S["dec_out"], 1)
                if not first:
                    nT_copy(g - 1)
                act.wait_ge(S["ktr_mm"], g + 1)
                nc.scalar.copy(ktok[:, :, :], pff[0:T, 0:TPC * M].rearrange("p (q m) -> p q m", q=TPC)).then_inc(
                    S["ktok_out"], 1)
                for q in range(TPC):
                    act.wait_ge(S["st_mm"], g * TPC + q + 1)
                    nc.scalar.copy(snap[:, (q + 1) % TPC, :], pst[:, 0:V1]).then_inc(S["snap_out"], 1)

            chunk(0, reset=True, first=True)
            with act.Fori(1, NC) as g:
                chunk(g)
            nT_copy(NC - 1)

        @block.vector
        def _(dve):
            dve.wait_ge(S["w_in"], 16 * 9)
            dve.wait_ge(S["w_ready"], 5)
            dve.wait_ge(S["brow_mm"], 1)
            nc.vector.tensor_copy(wo[KC:KC + 1, 0, :], pst[0:1, 0:D]).then_inc(S["w_ready"], 1)
            nc.vector.tensor_copy(wo[KC:KC + 1, 1, :], pst[0:1, 0:D]).then_inc(S["w_ready"], 1)
            for c in range(2):
                ts = nc.vector.tensor_scalar(wo[0:KC, c, :], wo[0:KC, c, :], gam[:, c:c + 1], None, ALU.mult)
            ts.then_inc(S["w_ready"], 1)

            def normalise(g):
                for q in range(TPC):
                    t = g * TPC + q
                    ts = nc.vector.tensor_scalar(xn[:, q, :], h[:, t, :], mean[:, bass.ds(t, 1)], rstd[:, bass.ds(t, 1)],
                                                 ALU.subtract, ALU.mult)
                ts.then_inc(S["xn_ready"], 1)

            def sums_out(g):
                dve.wait_ge(S["num_mm"], g + 1)
                step = [g * 3]

                def link(ins):
                    step[0] = step[0] + 1
                    ins.then_inc(S["hhc"], 1)
                    dve.wait_ge(S["hhc"], step[0])

                two = [pvo[:, i, 0:2 * V1].rearrange("p (q v) -> p q v", q=2) for i in range(2)]
                for i in range(2):
                    ts = nc.vector.tensor_scalar(den[:, 2 * i:2 * i + 2, :], two[i][:, :, D:V1], 1e-6, None, ALU.add)
                link(ts)
                link(nc.vector.reciprocal(den[:], den[:]))
                for q in range(TPC):
                    ts = nc.vector.tensor_scalar(hh[:, q, :], two[q // 2][:, q % 2, 0:D], den[:, q, :], None, ALU.mult)
                ts.then_inc(S["hh_out"], 1)
                dve.wait_ge(S["hh_out"], g + 1)
                for q in range(TPC):
                    bs = nc.vector.bn_stats(bn[:, q, :], hh[:, q, :])
                bs.then_inc(S["hhc"], 1)

            def sums_aggr(g):
                for q in range(TPC):
                    ag = nc.vector.bn_aggr(agg[:, q, :], bn[:, q, :])
                ag.then_inc(S["agg_out"], 1)

            def sums_norm(g):
                dve.wait_ge(S["rst_out"], g + 1)
                for q in range(TPC):
                    ts = nc.vector.tensor_scalar(hh[:, q, :], hh[:, q, :], agg[:, q, 0:1], rst[:, q:q + 1],
                                                 ALU.subtract, ALU.mult)
                ts.then_inc(S["nrm_ready"], 1)

            def gates(g, reset):
                dve.wait_ge(S["ff_mm"], g + 1)
                nc.vector.tensor_scalar(gate[:], pff[:, 0:CH], bff[:], ZMIN, ALU.add, ALU.max).then_inc(S["gate_in"], 1)
                dve.wait_ge(S["qk_mm"], g + 1)
                nc.vector.tensor_scalar(elu[:], pqk[:, 0:CH], 0.0, None, ALU.min).then_inc(S["elu_in"], 1)
                return

            def decay(g, reset, first):
                dve.wait_ge(S["gate_out"], 2 * g + 2)
                if not first:
                    dve.wait_ge(S["hhc"], g * 3)
                nc.vector.tensor_tensor_scan(cum[:], ones[:], gate[:], 0.0 if reset else tail[:],
                                             ALU.mult, ALU.subtract).then_inc(S["dvec"], 1)
                if not first:
                    sums_aggr(g - 1)
                dve.wait_ge(S["dvec"], 3 * g + 1)
                nc.vector.tensor_copy(tail[:], cum[:, CH - 1:CH]).then_inc(S["dvec"], 1)
                dve.wait_ge(S["dvec"], 3 * g + 2)
                nc.vector.tensor_scalar(cum[:], cum[:], -20.0, 20.0, ALU.max, ALU.min).then_inc(S["cum_out"], 1)
                dve.wait_ge(S["elu_out"], g + 1)
                nc.vector.scalar_tensor_tensor(elu[:], pqk[:, 0:CH], 0.0, elu[:], ALU.max, ALU.add).then_inc(S["dvec"], 1)
                dve.wait_ge(S["dvec"], 3 * g + 3)
                dve.wait_ge(S["dec_out"], g + 1)
                nc.vector.scalar_tensor_tensor(qt[:], elu[0:M, :], M ** -0.5, dec[0:M, :], ALU.mult, ALU.mult)
                nc.vector.tensor_tensor(kt[:], elu[M:128, :], dec[M:128, :], ALU.mult).then_inc(S["qk_out"], 1)

            def add_out(g):
                dve.wait_ge(S["wo_mm"], g + 1)
                for q in range(TPC):
                    t = g * TPC + q
                    tt = nc.vector.tensor_tensor(h[:, t, :], h[:, t, :], pvo[:, q // 2, (q % 2) * V1:(q % 2) * V1 + D],
                                                 ALU.add)
                tt.then_inc(S["h_out"], 1)

            def take_stats(g):
                for q in range(TPC):
                    nc.vector.bn_stats(bns[:, g * TPC + q, :], h[:, g * TPC + q, :])

            def chunk(g, reset=False, first=False, last=False):
                gates(g, reset)
                if not first:
                    sums_out(g - 1)
                decay(g, reset, first)
                if not first:
                    sums_norm(g - 1)
                    add_out(g - 1)
                    dve.wait_ge(S["h_out"], g)
                dve.wait_ge(S["at_mm"], g + 1)
                nc.vector.tensor_tensor(at[:, :, :], pat[:, 0:CH].rearrange("p (q t) -> p q t", q=TPC),
                                        mask[:, :].unsqueeze(1).broadcast_to([T, TPC, T]), ALU.mult).then_inc(S["at_out"], 1)
                if not first:
                    take_stats(g - 1)
                if not last:
                    normalise(g + 1)

            normalise(0)
            chunk(0, reset=True, first=True)
            with dve.Fori(1, CPI) as c:
                chunk(c)
            with dve.Fori(1, B - 1) as b:
                chunk(b * CPI, reset=True)
                with dve.Fori(1, CPI) as c:
                    chunk(b * CPI + c)
            chunk((B - 1) * CPI, reset=True)
            with dve.Fori((B - 1) * CPI + 1, NC - 1) as g:
                chunk(g)
            chunk(NC - 1, last=True)
            sums_out(NC - 1)
            dve.wait_ge(S["hhc"], 3 * NC)
            sums_aggr(NC - 1)
            sums_norm(NC - 1)
            add_out(NC - 1)
            dve.wait_ge(S["h_out"], NC)
            take_stats(NC - 1)


def expert_phase(nc, ins, h, bns, mean, rstd, eye):
    E, HID = 8, 256
    with ExitStack() as ctx:
        sb, ps, sem = allocator(nc, ctx)
        w1 = sb("w1_3", [KC, 2, KC])
        b1 = sb("b1_3", [KC, 1])
        w2 = sb("w2_3", [KC + 1, E])
        down = sb("down", [KC, E, 2, HID])
        downb = sb("downb", [128, 2 * E])
        up = sb("up", [128, E, 2, D])
        gam = sb("gam3", [T, D])
        bet = sb("bet3", [T, D])
        tri = sb("tri", [T, E, E])
        eps5 = sb("eps5_3", [T, TPC])
        mhalf = sb("mhalf_3", [T, TPC])
        xn = sb("xn3", [T, TPC, D])
        xT = sb("xT3", [KC, 2, CH])
        r1 = sb("r1", [KC + 1, CH])
        lg = sb("lg", [T, TPC, E])
        ex = sb("ex", [T, TPC, E])
        small = sb("small3", [T, TPC, 1])
        gt = sb("gt3", [T, TPC * E, E])
        eq = sb("eq3", [T, TPC * E, E])
        gates = sb("gates", [T, TPC, E])
        z = [[sb(f"z{i}{m}", [128, CH]) for m in range(2)] for i in range(2)]
        acc = sb("acc3", [T, TPC, D])
        yf = sb("yf3", [T, TPC, D])
        bn = sb("bn3", [T, TPC, 6])
        agg = sb("agg3", [T, TPC, 2])
        veps = sb("veps3", [T, TPC])
        rst = sb("rst3", [T, TPC])
        ptr = ps("ptr3", [KC, 2, 512])
        prt = ps("prt3", [KC, 512])
        plg = ps("plg3", [T, TPC * E])
        pz = [ps(f"pz{m}", [128, 512]) for m in range(2)]
        py = ps("py3", [T, 2, 512])
        names = ("w_in", "w_ready", "xn_ready", "xtr_mm", "xT_out", "r1_mm", "r1_out", "lg_mm", "dvec", "lg_out",
                 "ex_out", "gates_out", "down_mm", "z_out", "up_mm", "acc_out", "stat_out", "agg_out", "rst_out",
                 "nrm_out", "poolc", "yf_out", "h_out")
        S = {n: sem(f"{n}_3") for n in names}
        block = ctx.enter_context(nc.Block())
        NW = 9

        @block.sync
        def _(sp):
            for dst, name in ((w1[:], "w1"), (b1[:], "b1"), (w2[:], "w2"), (down[:], "down"), (downb[:], "downb"),
                              (up[:], "up"), (gam[:], "gam3"), (bet[:], "bet3"), (tri[:], "tri")):
                sp.dma_start(dst, ins[name]).then_inc(S["w_in"], 16)

        @block.gpsimd
        def _(pool):
            for n, (buf, value) in enumerate(((eps5[:], 1e-5), (mhalf[:], -0.5), (r1[KC:KC + 1], 1.0))):
                nc.gpsimd.memset(buf, value).then_inc(S["w_ready"], 1)
                pool.wait_ge(S["w_ready"], n + 1)
            pool.wait_ge(S["w_in"], 16 * NW)

            def chunk(g, first=False):
                if not first:
                    pool.wait_ge(S["yf_out"], g)
                pool.wait_ge(S["agg_out"], g + 1)
                nc.gpsimd.tensor_tensor(veps[:], agg[:, :, 1], eps5[:], ALU.add).then_inc(S["poolc"], 1)
                pool.wait_ge(S["poolc"], 2 * g + 1)
                nc.gpsimd.tensor_tensor(rst[:], veps[:], mhalf[:], ALU.pow).then_inc(S["rst_out"], 1)
                pool.wait_ge(S["rst_out"], g + 1)
                pool.wait_ge(S["nrm_out"], g + 1)
                nc.gpsimd.tensor_tensor(yf[:], yf[:], gam[:].unsqueeze(1).broadcast_to([T, TPC, D]),
                                        ALU.mult).then_inc(S["poolc"], 1)
                pool.wait_ge(S["poolc"], 2 * g + 2)
                nc.gpsimd.tensor_tensor(yf[:], yf[:], bet[:].unsqueeze(1).broadcast_to([T, TPC, D]),
                                        ALU.add).then_inc(S["yf_out"], 1)

            chunk(0, first=True)
            with pool.Fori(1, NC) as g:
                chunk(g)

        @block.tensor
        def _(pe):
            pe.wait_ge(S["w_in"], 16 * NW)
            pe.wait_ge(S["w_ready"], 3)

            def front(g):
                pe.wait_ge(S["xn_ready"], g + 1)
                for q in range(TPC):
                    for c in range(2):
                        mm = pe.transpose(ptr[:, c, q * T:(q + 1) * T], xn[:, q, c * KC:(c + 1) * KC], eye[0:T, 0:T])
                mm.then_inc(S["xtr_mm"], 1)

            def router(g):
                pe.wait_ge(S["xT_out"], g + 1)
                for c in range(2):
                    mm = pe.matmul(prt[:, 0:CH], w1[:, c, :], xT[:, c, :], start=(c == 0), stop=(c == 1))
                mm.then_inc(S["r1_mm"], 1)

            def logits(g):
                pe.wait_ge(S["r1_out"], g + 1)
                for q in range(TPC):
                    mm = pe.matmul(plg[:, q * E:(q + 1) * E], r1[:, q * T:(q + 1) * T], w2[:], start=True, stop=True,
                                   skip_group_check=True)
                mm.then_inc(S["lg_mm"], 1)

            def down_e(g, e, first):
                if e >= 1 or not first:
                    pe.wait_ge(S["z_out"], 2 * (g * E + e))
                for m in range(2):
                    for c in range(2):
                        mm = pe.matmul(pz[m][:, 0:CH], down[:, e, c, m * 128:(m + 1) * 128], xT[:, c, :],
                                       start=(c == 0), stop=(c == 1))
                    mm.then_inc(S["down_mm"], 1)

            def up_e(g, e, first):
                pe.wait_ge(S["z_out"], 2 * (g * E + e) + 2)
                for q in range(TPC):
                    if q % 2 == 0 and (e >= 1 or not first):
                        pe.wait_ge(S["acc_out"], 2 * (g * E + e) - 1 + q // 2)
                    for m in range(2):
                        mm = pe.matmul(py[:, q // 2, (q % 2) * D:(q % 2 + 1) * D], z[e % 2][m][:, q * T:(q + 1) * T],
                                       up[:, e, m, :], start=(m == 0), stop=(m == 1), skip_group_check=True)
                    if q % 2 == 1:
                        mm.then_inc(S["up_mm"], 1)

            def chunk(g, first=False, last=False):
                down_e(g, 0, first)
                logits(g)
                for e in range(1, E):
                    down_e(g, e, first)
                    if e == E - 1 and not last:
                        front(g + 1)
                    up_e(g, e - 1, first)
                if not last:
                    router(g + 1)
                up_e(g, E - 1, first)

            front(0)
            router(0)
            chunk(0, first=True)
            with pe.Fori(1, NC - 1) as g:
                chunk(g)
            chunk(NC - 1, last=True)

        @block.scalar
        def _(act):
            def take_x(g):
                act.wait_ge(S["xtr_mm"], g + 1)
                nc.scalar.copy(xT[:, :, :], ptr[:, :, 0:CH]).then_inc(S["xT_out"], 1)

            def take_r1(g):
                act.wait_ge(S["r1_mm"], g + 1)
                nc.scalar.activation(r1[0:KC], prt[:, 0:CH], ACT.Gelu, bias=b1[:]).then_inc(S["r1_out"], 1)

            def gelu_e(g, e, first):
                if e >= 2 or not first:
                    act.wait_ge(S["up_mm"], 2 * (g * E + e) - 2)
                for m in range(2):
                    act.wait_ge(S["down_mm"], 2 * (g * E + e) + m + 1)
                    nc.scalar.activation(z[e % 2][m][:], pz[m][:, 0:CH], ACT.Gelu,
                                         bias=downb[:, 2 * e + m:2 * e + m + 1]).then_inc(S["z_out"], 1)

            def chunk(g, first=False, last=False):
                gelu_e(g, 0, first)
                gelu_e(g, 1, first)
                act.wait_ge(S["lg_out"], g + 1)
                nc.scalar.activation(ex[:], lg[:], ACT.Exp).then_inc(S["ex_out"], 1)
                for e in range(2, E):
                    gelu_e(g, e, first)
                if not last:
                    take_x(g + 1)
                    take_r1(g + 1)

            act.wait_ge(S["w_in"], 16 * NW)
            take_x(0)
            take_r1(0)
            chunk(0, first=True)
            with act.Fori(1, NC - 1) as g:
                chunk(g)
            chunk(NC - 1, last=True)

        @block.vector
        def _(dve):
            dve.wait_ge(S["w_in"], 16 * NW)
            CHAIN = 12

            def normalise(g):
                for q in range(TPC):
                    t = g * TPC + q
                    ts = nc.vector.tensor_scalar(xn[:, q, :], h[:, t, :], mean[:, bass.ds(t, 1)],
                                                 rstd[:, bass.ds(t, 1)], ALU.subtract, ALU.mult)
                ts.then_inc(S["xn_ready"], 1)

            def softmax_top2(g, first):
                step = [g * CHAIN]

                def link(ins):
                    step[0] = step[0] + 1
                    ins.then_inc(S["dvec"], 1)
                    dve.wait_ge(S["dvec"], step[0])

                logit = plg[:].rearrange("p (q e) -> p q e", q=TPC)
                dve.wait_ge(S["lg_mm"], g + 1)
                if not first:
                    dve.wait_ge(S["stat_out"], g)
                mx = nc.vector.tensor_reduce(small[:, :, 0], logit, AX.X, ALU.max)
                if not first:
                    aggregate(g - 1)
                link(mx)
                nc.vector.tensor_tensor(lg[:], logit, small[:].broadcast_to([T, TPC, E]),
                                        ALU.subtract).then_inc(S["lg_out"], 1)
                dve.wait_ge(S["ex_out"], g + 1)
                link(nc.vector.tensor_reduce(small[:, :, 0], ex[:], AX.X, ALU.add))
                link(nc.vector.reciprocal(small[:], small[:]))
                link(nc.vector.tensor_tensor(ex[:], ex[:], small[:].broadcast_to([T, TPC, E]), ALU.mult))
                pe_ = ex[:].unsqueeze(3).broadcast_to([T, TPC, E, E])
                pj = ex[:].unsqueeze(2).broadcast_to([T, TPC, E, E])
                nc.vector.tensor_tensor(gt[:].rearrange("p (q e) j -> p q e j", q=TPC), pj, pe_, ALU.is_gt)
                link(nc.vector.tensor_tensor(eq[:].rearrange("p (q e) j -> p q e j", q=TPC), pj, pe_, ALU.is_equal))
                link(nc.vector.tensor_tensor(eq[:].rearrange("p (q e) j -> p q (e j)", q=TPC),
                                             eq[:].rearrange("p (q e) j -> p q (e j)", q=TPC),
                                             tri[:].rearrange("p e j -> p (e j)").unsqueeze(1).broadcast_to(
                                                 [T, TPC, E * E]), ALU.mult))
                link(nc.vector.tensor_tensor(gt[:], gt[:], eq[:], ALU.add))
                link(nc.vector.tensor_reduce(lg[:].rearrange("p q e -> p (q e)"), gt[:], AX.X, ALU.add))
                link(nc.vector.scalar_tensor_tensor(ex[:], lg[:], 2.0, ex[:], ALU.is_lt, ALU.mult))
                link(nc.vector.tensor_reduce(small[:, :, 0], ex[:], AX.X, ALU.add))
                link(nc.vector.tensor_scalar(small[:], small[:], 1e-8, None, ALU.add))
                link(nc.vector.reciprocal(small[:], small[:]))
                nc.vector.tensor_tensor(gates[:], ex[:], small[:].broadcast_to([T, TPC, E]),
                                        ALU.mult).then_inc(S["gates_out"], 1)
                dve.wait_ge(S["gates_out"], g + 1)

            def combine(g, e, first):
                if e >= 1:
                    dve.wait_ge(S["acc_out"], 2 * (g * E + e))
                elif not first:
                    dve.wait_ge(S["nrm_out"], g)
                for q in range(TPC):
                    if q % 2 == 0:
                        dve.wait_ge(S["up_mm"], 2 * (g * E + e) + 1 + q // 2)
                    src = xn if e == 0 else acc
                    st = nc.vector.scalar_tensor_tensor(acc[:, q, :], py[:, q // 2, (q % 2) * D:(q % 2 + 1) * D],
                                                        gates[:, q, e:e + 1], src[:, q, :], ALU.mult, ALU.add)
                    if q % 2 == 1:
                        st.then_inc(S["acc_out"], 1)

            def stat(g):
                dve.wait_ge(S["acc_out"], 2 * E * (g + 1))
                for q in range(TPC):
                    bs = nc.vector.bn_stats(bn[:, q, :], acc[:, q, :])
                bs.then_inc(S["stat_out"], 1)

            def aggregate(g):
                for q in range(TPC):
                    ag = nc.vector.bn_aggr(agg[:, q, :], bn[:, q, :])
                ag.then_inc(S["agg_out"], 1)

            def norm_out(g):
                dve.wait_ge(S["rst_out"], g + 1)
                for q in range(TPC):
                    ts = nc.vector.tensor_scalar(yf[:, q, :], acc[:, q, :], agg[:, q, 0:1], rst[:, q:q + 1],
                                                 ALU.subtract, ALU.mult)
                ts.then_inc(S["nrm_out"], 1)

            def add_out(g):
                dve.wait_ge(S["yf_out"], g + 1)
                hs = h[:, bass.ds(g * TPC, TPC), :]
                nc.vector.tensor_tensor(hs, hs, yf[:], ALU.add).then_inc(S["h_out"], 1)

            def take_stats(g):
                for q in range(TPC):
                    nc.vector.bn_stats(bns[:, g * TPC + q, :], h[:, g * TPC + q, :])

            def chunk(g, first=False, last=False):
                softmax_top2(g, first)
                if not first:
                    norm_out(g - 1)
                combine(g, 0, first)
                if not last:
                    dve.wait_ge(S["acc_out"], 2 * g * E + 2)
                    normalise(g + 1)
                combine(g, 1, first)
                combine(g, 2, first)
                if not first:
                    add_out(g - 1)
                    dve.wait_ge(S["h_out"], g)
                combine(g, 3, first)
                if not first:
                    take_stats(g - 1)
                for e in range(4, E):
                    combine(g, e, first)
                stat(g)

            normalise(0)
            chunk(0, first=True)
            with dve.Fori(1, NC - 1) as g:
                chunk(g)
            chunk(NC - 1, last=True)
            dve.wait_ge(S["stat_out"], NC)
            aggregate(NC - 1)
            norm_out(NC - 1)
            add_out(NC - 1)
            dve.wait_ge(S["h_out"], NC)
            take_stats(NC - 1)


def linear_attention_phase(nc, ins, h, bns, mean, rstd, eye):
    with ExitStack() as ctx:
        sb, ps, sem = allocator(nc, ctx)
        wT = sb("wT4", [KC, 2, 3 * D])
        wq = sb("wq4", [KC, 2, D])
        wpT = sb("wpT4", [KC, 2, D])
        heads = sb("heads4", [KC, KC])
        xn = [sb(f"xn4_{i}", [T, TPC, D]) for i in range(2)]
        xT = sb("xT4", [KC + 1, 2, TOK])
        junk = sb("junk4", [KC, CH])
        sums = sb("sums4", [KC, 4, CPI])
        nrm = sb("nrm4", [KC, 4])
        scale = sb("scale4", [KC, 2])
        gsb = sb("gsb4", [KC, 2, D])
        t2 = sb("t2_4", [KC, 2, D])
        kvT = sb("kvT4", [KC, 2, D])
        m1 = sb("m1_4", [KC, 2, D])
        wimg = sb("wimg4", [KC + 1, 2, D])
        ptr = ps("ptr4", [KC, 2, 512])
        pqk = [ps(f"pqk4_{i}", [KC, 512]) for i in range(2)]
        pg = [ps(f"pg4_{i}", [KC, 512]) for i in range(2)]
        po = ps("po4", [T, 2, 512])
        names = ("w_in", "w_ready", "xn_ready", "xtr_mm", "xT_out", "qk_mm", "k_sum", "q_sum", "g_mm", "g_out",
                 "t2_mm", "t2_out", "kv_mm", "kv_out", "m1_mm", "m1_out", "wi_mm", "wi_out", "o_mm", "h_out", "dvec")
        S = {n: sem(f"{n}_4") for n in names}
        block = ctx.enter_context(nc.Block())
        NW = 5

        @block.sync
        def _(sp):
            for dst, name in ((wT[:], "wT4"), (wq[:], "wq4"), (wpT[:], "wpT4"), (heads[:], "heads"),
                              (wimg[KC:KC + 1, 0, :], "bproj4")):
                sp.dma_start(dst, ins[name]).then_inc(S["w_in"], 16)

        @block.gpsimd
        def _(pool):
            nc.gpsimd.memset(xT[KC:KC + 1], 1.0).then_inc(S["w_ready"], 1)

        @block.tensor
        def _(pe):
            pe.wait_ge(S["w_in"], 16 * NW)
            pe.wait_ge(S["w_ready"], 1)
            pe.sem_inc(S["o_mm"], 1)

            def gather(b, c):
                g = b * CPI + c
                pe.wait_ge(S["xn_ready"], g + 1)
                for q in range(TPC):
                    for i in range(2):
                        mm = pe.transpose(ptr[:, i, q * T:(q + 1) * T], xn[c % 2][:, q, i * KC:(i + 1) * KC],
                                          eye[0:T, 0:T])
                mm.then_inc(S["xtr_mm"], 1)
                for q in range(TPC):
                    for i in range(2):
                        mm = pe.matmul(pg[i][:, 0:D], xn[c % 2][:, q, i * KC:(i + 1) * KC], xn[c % 2][:, q, :],
                                       start=(c == 0 and q == 0), stop=(c == CPI - 1 and q == TPC - 1),
                                       skip_group_check=True)
                mm.then_inc(S["g_mm"], 1)
                pe.wait_ge(S["xT_out"], g + 1)
                for m in range(4):
                    if m == 0:
                        pe.wait_ge(S["q_sum"], 2 * g + 1)
                    elif m == 1:
                        pe.wait_ge(S["k_sum"], 2 * g + 1)
                    elif m == 2:
                        pe.wait_ge(S["q_sum"], 2 * g + 2)
                    else:
                        pe.wait_ge(S["k_sum"], 2 * g + 2)
                    piece = (0, 2, 1, 3)[m]
                    for i in range(2):
                        mm = pe.matmul(pqk[m % 2][:, 0:CH], wT[:, i, piece * KC:(piece + 1) * KC],
                                       xT[0:KC, i, c * CH:(c + 1) * CH], start=(i == 0), stop=(i == 1))
                    mm.then_inc(S["qk_mm"], 1)

            def square(dst, lhs, rhs):
                for i in range(2):
                    for c in range(2):
                        mm = pe.matmul(dst[i][:, 0:D], lhs(c, i), rhs(c), start=(c == 0), stop=(c == 1))
                return mm

            def image(b):
                for c in range(CPI):
                    gather(b, c)
                pe.wait_ge(S["g_out"], b + 1)
                pe.wait_ge(S["k_sum"], 2 * CPI * (b + 1) + 1)
                pe.wait_ge(S["q_sum"], 2 * CPI * (b + 1) + 1)
                square(pqk, lambda c, i: gsb[:, c, i * KC:(i + 1) * KC],
                       lambda c: wT[:, c, D:2 * D]).then_inc(S["t2_mm"], 1)
                pe.wait_ge(S["t2_out"], b + 1)
                square(pg, lambda c, i: wT[:, c, 2 * D + i * KC:2 * D + (i + 1) * KC],
                       lambda c: t2[:, c, :]).then_inc(S["kv_mm"], 1)
                pe.wait_ge(S["kv_out"], b + 1)
                square(pqk, lambda c, i: kvT[:, c, i * KC:(i + 1) * KC],
                       lambda c: wpT[:, c, :]).then_inc(S["m1_mm"], 1)
                pe.wait_ge(S["m1_out"], b + 1)
                square(pg, lambda c, i: wq[:, c, i * KC:(i + 1) * KC],
                       lambda c: m1[:, c, :]).then_inc(S["wi_mm"], 1)
                pe.wait_ge(S["wi_out"], b + 1)
                for t in range(TPI):
                    if t % 2 == 0:
                        pe.wait_ge(S["h_out"], TPI // 2 * b + t // 2 + 1)
                    for i in range(2):
                        k = KC + 1 if i == 0 else KC
                        mm = pe.matmul(po[:, (t // 2) % 2, (t % 2) * D:(t % 2 + 1) * D], xT[0:k, i, t * T:(t + 1) * T],
                                       wimg[0:k, i, :], start=(i == 0), stop=(i == 1), skip_group_check=True)
                    if t % 2 == 1:
                        mm.then_inc(S["o_mm"], 1)

            with pe.Fori(0, B) as b:
                image(b)

        @block.scalar
        def _(act):
            act.wait_ge(S["w_in"], 16 * NW)
            nc.scalar.preload_act_table(ACT.Abs)
            act.sem_inc(S["q_sum"], 1)

            def image(b):
                for c in range(CPI):
                    g = b * CPI + c
                    act.wait_ge(S["xtr_mm"], g + 1)
                    if c == 0:
                        act.wait_ge(S["o_mm"], TPI // 2 * b + 1)
                    nc.scalar.copy(xT[0:KC, :, c * CH:(c + 1) * CH], ptr[:, :, 0:CH]).then_inc(S["xT_out"], 1)
                    for m in range(2):
                        act.wait_ge(S["qk_mm"], 4 * g + 2 * m + 1)
                        nc.scalar.activation(junk[:], pqk[0][:, 0:CH], ACT.Abs,
                                             accum_out=sums[:, m, c:c + 1]).then_inc(S["q_sum"], 1)
                act.wait_ge(S["g_mm"], CPI * (b + 1))
                for i in range(2):
                    cp = nc.scalar.copy(gsb[:, i, :], pg[i][:, 0:D])
                cp.then_inc(S["g_out"], 1)

            with act.Fori(0, B) as b:
                image(b)

        @block.vector
        def _(dve):
            dve.wait_ge(S["w_in"], 16 * NW)
            dve.sem_inc(S["k_sum"], 1)
            dve.sem_inc(S["h_out"], 2)

            def normalise(b, c):
                g = b * CPI + c
                if c >= 2:
                    dve.wait_ge(S["g_mm"], g - 1)
                for q in range(TPC):
                    t = g * TPC + q
                    ts = nc.vector.tensor_scalar(xn[c % 2][:, q, :], h[:, t, :],
                                                 mean[:, bass.ds(t, 1)], rstd[:, bass.ds(t, 1)],
                                                 ALU.subtract, ALU.mult)
                ts.then_inc(S["xn_ready"], 1)

            def image(b):
                normalise(b, 0)
                for c in range(CPI):
                    g = b * CPI + c
                    if c + 1 < CPI:
                        normalise(b, c + 1)
                    for m in range(2):
                        dve.wait_ge(S["qk_mm"], 4 * g + 2 * m + 2)
                        nc.vector.tensor_reduce(sums[:, 2 + m, c:c + 1], pqk[1][:, 0:CH], AX.X, ALU.add,
                                                apply_absolute_value=True).then_inc(S["k_sum"], 1)
                dve.wait_ge(S["k_sum"], 2 * CPI * (b + 1) + 1)
                dve.wait_ge(S["q_sum"], 2 * CPI * (b + 1) + 1)
                step = [4 * b]

                def link(ins):
                    step[0] = step[0] + 1
                    ins.then_inc(S["dvec"], 1)
                    dve.wait_ge(S["dvec"], step[0])

                link(nc.vector.tensor_reduce(nrm[:], sums[:], AX.X, ALU.add))
                link(nc.vector.tensor_scalar(nrm[:], nrm[:], 1e-12, None, ALU.max))
                link(nc.vector.reciprocal(nrm[:], nrm[:]))
                link(nc.vector.tensor_tensor(scale[:], nrm[:, 0:2], nrm[:, 2:4], ALU.mult))
                dve.wait_ge(S["t2_mm"], b + 1)
                for i in range(2):
                    cp = nc.vector.tensor_copy(t2[:, i, :], pqk[i][:, 0:D])
                cp.then_inc(S["t2_out"], 1)
                dve.wait_ge(S["kv_mm"], b + 1)
                for i in range(2):
                    nc.vector.tensor_tensor(kvT[:, i, i * KC:(i + 1) * KC], pg[i][:, i * KC:(i + 1) * KC], heads[:],
                                            ALU.mult)
                    ms = nc.vector.memset(kvT[:, i, (1 - i) * KC:(2 - i) * KC], 0.0)
                ms.then_inc(S["kv_out"], 1)
                dve.wait_ge(S["m1_mm"], b + 1)
                for i in range(2):
                    ts = nc.vector.tensor_scalar(m1[:, i, :], pqk[i][:, 0:D], scale[:, i:i + 1], None, ALU.mult)
                ts.then_inc(S["m1_out"], 1)
                dve.wait_ge(S["wi_mm"], b + 1)
                for i in range(2):
                    cp = nc.vector.tensor_copy(wimg[0:KC, i, :], pg[i][:, 0:D])
                cp.then_inc(S["wi_out"], 1)
                for p in range(TPI // 2):
                    n = TPI // 2 * b + p
                    t = b * TPI + 2 * p
                    dve.wait_ge(S["o_mm"], n + 2)
                    if p >= 1:
                        dve.wait_ge(S["h_out"], n + 2)
                    two = h[:, bass.ds(t, 2), :]
                    nc.vector.tensor_tensor(two, two, po[:, p % 2, 0:2 * D].rearrange("p (q d) -> p q d", q=2),
                                            ALU.add).then_inc(S["h_out"], 1)
                    if p >= 1:
                        stats_of(t - 2)
                dve.wait_ge(S["h_out"], TPI // 2 * (b + 1) + 2)
                nc.vector.tensor_copy(scale[:], nrm[:, 0:2])
                stats_of(b * TPI + TPI - 2)

            def stats_of(t):
                for q in range(2):
                    nc.vector.bn_stats(bns[:, t + q, :],
                                       h[:, t + q, :])

            with dve.Fori(0, B) as b:
                image(b)


def bit_ffn_phase(nc, ins, h, bns, mean, rstd, var, eye, out):
    HID = 512
    MAGIC = 12582912.0
    with ExitStack() as ctx:
        sb, ps, sem = allocator(nc, ctx)
        win = sb("win5", [KC, 2, 2 * HID])
        wout = sb("wout5", [128, 4, D])
        winq = sb("winq5", [KC, 2, 2 * HID], BF16)
        woutq = sb("woutq5", [128, 4, D], BF16)
        gin = sb("gin5", [T, D])
        gout = sb("gout5", [T, HID])
        ones = sb("ones5", [128, 128])
        eyeb = sb("eyeb5", [128, 128], BF16)
        wsum = sb("wsum5", [128, 4])
        wsc = sb("wsc5", [128, 4])
        mhalf = sb("mhalf5", [T, NT])
        fac = sb("fac5", [T, NT])
        tmp = sb("tmp5", [T, NT])
        xg = sb("xg5", [T, TPC, D])
        xr = sb("xr5", [T, TPC, D])
        xq = sb("xq5", [T, TPC, D], BF16)
        xT = sb("xT5", [KC, 2, CH], BF16)
        am = sb("am5", [T, TPC])
        sx = sb("sx5", [T, TPC])
        dx = sb("dx5", [T, TPC])
        sg = [sb(f"sg5_{i}", [T, HID]) for i in range(2)]
        junk = sb("junk5", [T, HID])
        y = sb("y5", [T, TPC, HID])
        yg = sb("yg5", [T, TPC, HID])
        yr = sb("yr5", [T, TPC, HID])
        yq = sb("yq5", [T, TPC, HID], BF16)
        yT = sb("yT5", [128, 4, CH], BF16)
        ssq = sb("ssq5", [T, TPC])
        am2 = sb("am2_5", [T, TPC])
        ms2 = sb("ms2_5", [T, TPC])
        r2 = sb("r2_5", [T, TPC])
        s2 = sb("s2_5", [T, TPC])
        d2 = sb("d2_5", [T, TPC])
        ho = sb("ho5", [T, TPC, D])
        pxt = ps("pxt5", [KC, 2, CH], BF16)
        pyt = ps("pyt5", [128, 2, 1024], BF16)
        pup = [ps(f"pup5_{i}", [128, 512]) for i in range(2)]
        pga = [ps(f"pga5_{i}", [128, 512]) for i in range(2)]
        po = ps("po5", [T, 512])
        names = ("w_in", "w_ready", "wc", "wsum_mm", "xq_out", "xtr_mm", "xT_out", "in_mm", "sg_out", "y_out", "yg_out",
                 "ssq_out", "r2_in", "r2_out", "yq_out", "ytr_mm", "yT_out", "o_mm", "o_out", "stored", "dvec",
                 "dvec2", "fac_in", "fac_out", "poolc", "d2_out", "dx_out", "xr_out", "yr_out")
        S = {n: sem(f"{n}_5") for n in names}
        block = ctx.enter_context(nc.Block())
        NW = 4
        out_t = out.rearrange("b (t p) d -> p (b t) d", p=T)

        @block.sync
        def _(sp):
            for dst, name in ((win[:], "win5"), (wout[:], "wout5"), (gin[:], "gin5"), (gout[:], "gout5")):
                sp.dma_start(dst, ins[name]).then_inc(S["w_in"], 16)

            def store(g):
                sp.wait_ge(S["o_out"], 2 * g + 2)
                sp.dma_start(out_t[:, bass.ds(g * TPC, TPC), :], ho[:]).then_inc(S["stored"], 16)

            with sp.Fori(0, NC) as g:
                store(g)
            sp.wait_ge(S["stored"], 16 * NC)

        @block.gpsimd
        def _(pool):
            nc.gpsimd.memset(ones[:], 1.0).then_inc(S["w_ready"], 1)
            pool.wait_ge(S["w_ready"], 1)
            nc.gpsimd.memset(mhalf[:], -0.5).then_inc(S["w_ready"], 1)
            pool.wait_ge(S["w_ready"], 2)
            pool.wait_ge(S["fac_in"], 1)
            nc.gpsimd.tensor_tensor(fac[:], tmp[:], mhalf[:], ALU.pow).then_inc(S["fac_out"], 1)
            pool.wait_ge(S["w_in"], 16 * NW)
            pool.wait_ge(S["fac_out"], 1)

            def chunk(g, first=False):
                for q in range(TPC):
                    if q == 0 and not first:
                        pool.wait_ge(S["r2_out"], g)
                        pool.wait_ge(S["yr_out"], g)
                    elif q:
                        pool.wait_ge(S["yg_out"], g * TPC + q)
                    pool.wait_ge(S["y_out"], g * TPC + q + 1)
                    nc.gpsimd.tensor_tensor(yg[:, q, :], y[:, q, :], gout[:], ALU.mult).then_inc(S["yg_out"], 1)
                pool.wait_ge(S["yg_out"], (g + 1) * TPC)
                pool.wait_ge(S["r2_in"], g + 1)
                nc.gpsimd.tensor_tensor(r2[:], ms2[:], mhalf[:, 0:TPC], ALU.pow).then_inc(S["r2_out"], 1)

            chunk(0, first=True)
            with pool.Fori(1, NC) as g:
                chunk(g)

        @block.tensor
        def _(pe):
            pe.wait_ge(S["w_ready"], 2)
            pe.wait_ge(S["wc"], 1)
            pe.matmul(pup[0][:, 0:1], ones[:], wsum[:, 1:2], start=True, stop=True)
            pe.matmul(pga[0][:, 0:1], ones[:], wsum[:, 0:1], start=True, stop=True).then_inc(
                S["wsum_mm"], 1)
            pe.wait_ge(S["w_ready"], 2 + 3)

            def transpose_in(g):
                pe.wait_ge(S["xq_out"], g + 1)
                for q in range(TPC):
                    for c in range(2):
                        mm = pe.transpose(pxt[:, c, q * T:(q + 1) * T], xq[:, q, c * KC:(c + 1) * KC], eyeb[0:T, 0:T])
                mm.then_inc(S["xtr_mm"], 1)

            def into(g, q, first=False):
                if not first:
                    pe.wait_ge(S["y_out"], g * TPC + q - 1)
                for dst, o in ((pga, HID), (pup, 0)):
                    for c in range(2):
                        mm = pe.matmul(dst[q % 2][0:T], xT[:, c, q * T:(q + 1) * T], winq[:, c, o:o + HID],
                                       start=(c == 0), stop=(c == 1))
                mm.then_inc(S["in_mm"], 1)

            def transpose_y(g):
                pe.wait_ge(S["yq_out"], 2 * g + 2)
                for half in range(2):
                    for k in range(2):
                        for q in range(TPC):
                            mm = pe.transpose(pyt[:, half, k * CH + q * T:k * CH + (q + 1) * T],
                                              yq[:, q, (2 * half + k) * 128:(2 * half + k + 1) * 128], eyeb[0:T, 0:T])
                    mm.then_inc(S["ytr_mm"], 1)

            def enter(g, first=False):
                pe.wait_ge(S["xT_out"], g + 1)
                into(g, 0, first)
                into(g, 1, first)

            def outof(g, pair):
                if pair or not isinstance(g, int) or g > 0:
                    pe.wait_ge(S["o_out"], 2 * g + pair)
                pe.wait_ge(S["yT_out"], 2 * g + 2)
                for i in range(2):
                    q = 2 * pair + i
                    for k in range(4):
                        mm = pe.matmul(po[:, i * D:(i + 1) * D], yT[:, k, q * T:(q + 1) * T], woutq[:, k, :],
                                       start=(k == 0), stop=(k == 3), skip_group_check=True)
                mm.then_inc(S["o_mm"], 1)

            def step(g, first=False, last=False):
                into(g, 2)
                into(g, 3)
                if not first:
                    transpose_y(g - 1)
                    outof(g - 1, 0)
                if not last:
                    transpose_in(g + 1)
                if not first:
                    outof(g - 1, 1)
                if not last:
                    enter(g + 1)

            transpose_in(0)
            enter(0, first=True)
            step(0, first=True)
            with pe.Fori(1, NC - 1) as g:
                step(g)
            step(NC - 1, last=True)
            transpose_y(NC - 1)
            outof(NC - 1, 0)
            outof(NC - 1, 1)

        @block.scalar
        def _(act):
            nc.scalar.preload_act_table(ACT.Silu)
            act.wait_ge(S["w_ready"], 2 + 3)

            def take_x(g):
                act.wait_ge(S["xtr_mm"], g + 1)
                nc.scalar.copy(xT[:, :, :], pxt[:, :, :]).then_inc(S["xT_out"], 1)

            def silu(g, q):
                act.wait_ge(S["in_mm"], g * TPC + q + 1)
                nc.scalar.activation(sg[q % 2][:], pga[q % 2][0:T], ACT.Silu, scale=dx[:, q:q + 1]).then_inc(
                    S["sg_out"], 1)

            def squares(g, q, first=False):
                if q or not first:
                    act.wait_ge(S["ssq_out"], g * TPC + q)
                if q == 0 and not first:
                    act.wait_ge(S["r2_in"], g)
                act.wait_ge(S["y_out"], g * TPC + q + 1)
                nc.scalar.activation(junk[:], y[:, q, :], ACT.Square, accum_out=ssq[:, q:q + 1]).then_inc(
                    S["ssq_out"], 1)

            def whole_y(g, pair):
                act.wait_ge(S["yr_out"], g + 1)
                nc.scalar.activation(yq[:, 2 * pair:2 * pair + 2, :], yr[:, 2 * pair:2 * pair + 2, :],
                                     ACT.Copy, bias=-MAGIC).then_inc(S["yq_out"], 1)

            def take_y(g):
                for half in range(2):
                    act.wait_ge(S["ytr_mm"], 2 * g + half + 1)
                    nc.scalar.copy(yT[:, 2 * half:2 * half + 2, :],
                                   pyt[:, half, 0:2 * CH].rearrange("p (k c) -> p k c", k=2)).then_inc(S["yT_out"], 1)

            def step(g, first=False, last=False):
                if not first:
                    whole_y(g - 1, 0)
                silu(g, 2)
                if not first:
                    whole_y(g - 1, 1)
                silu(g, 3)
                for q in (0, 1):
                    squares(g, q, first)
                if not first:
                    take_y(g - 1)
                for q in (2, 3):
                    squares(g, q)
                if not last:
                    take_x(g + 1)
                    silu(g + 1, 0)
                    silu(g + 1, 1)

            take_x(0)
            silu(0, 0)
            silu(0, 1)
            step(0, first=True)
            with act.Fori(1, NC - 1) as g:
                step(g)
            step(NC - 1, last=True)
            whole_y(NC - 1, 0)
            whole_y(NC - 1, 1)
            take_y(NC - 1)

        @block.vector
        def _(dve):
            step = [0]

            def link(ins):
                step[0] = step[0] + 1
                ins.then_inc(S["dvec"], 1)
                dve.wait_ge(S["dvec"], step[0])

            dve.wait_ge(S["w_in"], 16 * NW)
            link(nc.vector.memset(wsum[:], 0.0))
            link(nc.vector.tensor_reduce(wsum[0:KC, 0:1], win[:], AX.XY, ALU.add, apply_absolute_value=True))
            nc.vector.tensor_reduce(wsum[:, 1:2], wout[:], AX.XY, ALU.add, apply_absolute_value=True).then_inc(S["wc"], 1)
            link(nc.vector.tensor_copy(eyeb[:], eye[:]))
            dve.wait_ge(S["wsum_mm"], 1)
            nc.vector.tensor_scalar(wsc[:, 0:1], pga[0][:, 0:1], 1.0 / (2 * HID * D), 1e-5, ALU.mult, ALU.max)
            link(nc.vector.tensor_scalar(wsc[:, 1:2], pup[0][:, 0:1], 1.0 / (HID * D), 1e-5, ALU.mult, ALU.max))
            link(nc.vector.reciprocal(wsc[:, 2:4], wsc[:, 0:2]))
            link(nc.vector.tensor_scalar(win[:], win[:], wsc[0:KC, 2:3], MAGIC, ALU.mult, ALU.add))
            link(nc.vector.tensor_scalar(win[:], win[:], MAGIC, 1.0, ALU.subtract, ALU.min))
            nc.vector.tensor_scalar(winq[:], win[:], -1.0, None, ALU.max).then_inc(S["w_ready"], 1)
            link(nc.vector.tensor_scalar(wout[:], wout[:], wsc[:, 3:4], MAGIC, ALU.mult, ALU.add))
            link(nc.vector.tensor_scalar(wout[:], wout[:], MAGIC, 1.0, ALU.subtract, ALU.min))
            nc.vector.tensor_scalar(woutq[:], wout[:], -1.0, None, ALU.max).then_inc(S["w_ready"], 1)
            link(nc.vector.tensor_tensor(tmp[:], var[:], rstd[:], ALU.mult))
            link(nc.vector.tensor_tensor(tmp[:], tmp[:], rstd[:], ALU.mult))
            link(nc.vector.tensor_scalar(tmp[:], tmp[:], 1e-6, None, ALU.add))
            dve.sem_inc(S["fac_in"], 1)
            dve.wait_ge(S["fac_out"], 1)
            nc.vector.tensor_tensor(fac[:], fac[:], rstd[:], ALU.mult).then_inc(S["w_ready"], 1)
            dve.wait_ge(S["w_ready"], 5)

            L1, L2 = 6, 5

            def quant_in(g):
                st = [g * L1]

                def link(ins):
                    st[0] = st[0] + 1
                    ins.then_inc(S["poolc"], 1)
                    dve.wait_ge(S["poolc"], st[0])

                for q in range(TPC):
                    t = g * TPC + q
                    ins_ = nc.vector.scalar_tensor_tensor(xg[:, q, :], h[:, t, :], mean[:, bass.ds(t, 1)], gin[:],
                                                          ALU.subtract, ALU.mult)
                link(ins_)
                link(nc.vector.tensor_reduce(am[:], xg[:], AX.X, ALU.max, apply_absolute_value=True))
                link(nc.vector.tensor_tensor(am[:], am[:], fac[:, bass.ds(g * TPC, TPC)], ALU.mult))
                link(nc.vector.tensor_scalar(am[:], am[:], 1e-5, 1.0 / 127, ALU.max, ALU.mult))
                nc.vector.tensor_scalar(dx[:], am[:], wsc[0:T, 0:1], None, ALU.mult).then_inc(S["dx_out"], 1)
                link(nc.vector.reciprocal(sx[:], am[:]))
                link(nc.vector.tensor_tensor(sx[:], sx[:], fac[:, bass.ds(g * TPC, TPC)], ALU.mult))
                for q in range(TPC):
                    ins_ = nc.vector.tensor_scalar(xr[:, q, :], xg[:, q, :], sx[:, q:q + 1], MAGIC, ALU.mult, ALU.add)
                ins_.then_inc(S["xr_out"], 1)
                dve.wait_ge(S["xr_out"], g + 1)
                nc.vector.tensor_scalar(xq[:], xr[:], MAGIC, None, ALU.subtract).then_inc(S["xq_out"], 1)

            def gated(g, q, first=False):
                if not first:
                    dve.wait_ge(S["yg_out"], (g - 1) * TPC + q + 1)
                dve.wait_ge(S["sg_out"], g * TPC + q + 1)
                nc.vector.scalar_tensor_tensor(y[:, q, :], pup[q % 2][0:T], dx[:, q:q + 1], sg[q % 2][:],
                                               ALU.mult, ALU.mult).then_inc(S["y_out"], 1)

            def mean_square(g):
                dve.wait_ge(S["ssq_out"], (g + 1) * TPC)
                nc.vector.tensor_scalar(ms2[:], ssq[:], 1.0 / HID, 1e-6, ALU.mult, ALU.add).then_inc(S["r2_in"], 1)

            def quant_y(g, first=False):
                st = [g * L2]

                def link(ins):
                    st[0] = st[0] + 1
                    ins.then_inc(S["dvec2"], 1)
                    dve.wait_ge(S["dvec2"], st[0])

                dve.wait_ge(S["yg_out"], (g + 1) * TPC)
                nc.vector.tensor_reduce(am2[:], yg[:], AX.X, ALU.max, apply_absolute_value=True)
                if not first:
                    result(g - 1, 1)
                dve.wait_ge(S["r2_out"], g + 1)
                dve.wait_ge(S["r2_in"], g + 1)
                link(nc.vector.tensor_copy(s2[:], r2[:]))
                link(nc.vector.tensor_tensor(am2[:], am2[:], r2[:], ALU.mult))
                if not first:
                    dve.wait_ge(S["o_out"], 2 * g)
                link(nc.vector.tensor_scalar(am2[:], am2[:], 1e-5, 1.0 / 127, ALU.max, ALU.mult))
                link(nc.vector.reciprocal(s2[:], am2[:]))
                nc.vector.tensor_scalar(d2[:], am2[:], wsc[0:T, 1:2], None, ALU.mult).then_inc(S["d2_out"], 1)
                link(nc.vector.tensor_tensor(s2[:], s2[:], r2[:], ALU.mult))
                if not first:
                    dve.wait_ge(S["yq_out"], 2 * g)
                for q in range(TPC):
                    ins_ = nc.vector.tensor_scalar(yr[:, q, :], yg[:, q, :], s2[:, q:q + 1], MAGIC, ALU.mult, ALU.add)
                ins_.then_inc(S["yr_out"], 1)

            def result(g, pair):
                if pair == 0 and (not isinstance(g, int) or g > 0):
                    dve.wait_ge(S["stored"], 16 * g)
                dve.wait_ge(S["d2_out"], g + 1)
                dve.wait_ge(S["o_mm"], 2 * g + pair + 1)
                for i in range(2):
                    q = 2 * pair + i
                    st = nc.vector.scalar_tensor_tensor(ho[:, q, :], po[:, i * D:(i + 1) * D], d2[:, q:q + 1],
                                                        h[:, g * TPC + q, :], ALU.mult, ALU.add)
                st.then_inc(S["o_out"], 1)

            def step(g, first=False, last=False):
                for q in range(TPC):
                    gated(g, q, first)
                if not last:
                    quant_in(g + 1)
                mean_square(g)
                if not first:
                    result(g - 1, 0)
                quant_y(g, first)

            quant_in(0)
            step(0, first=True)
            with dve.Fori(1, NC - 1) as g:
                step(g)
            step(NC - 1, last=True)
            result(NC - 1, 0)
            result(NC - 1, 1)


def vit_tower(nc, ins, out):
    with ExitStack() as ctx:
        sb, ps, sem = allocator(nc, ctx)
        h = sb("h", [T, NT, D])
        bns = sb("bns", [T, NT, 6])
        eye = sb("eye", [128, 128])
        mean = sb("mean", [T, NT])
        rstd = sb("rstd", [T, NT])
        var = sb("var", [T, NT])
        mixer_phase(nc, ins, h, bns, eye)
        finish_stats(nc, "ln1", bns, mean, rstd, var, 1e-5)
        retention_phase(nc, ins, h, bns, mean, rstd, eye)
        finish_stats(nc, "ln2", bns, mean, rstd, var, 1e-5)
        expert_phase(nc, ins, h, bns, mean, rstd, eye)
        finish_stats(nc, "ln3", bns, mean, rstd, var, 1e-5)
        linear_attention_phase(nc, ins, h, bns, mean, rstd, eye)
        finish_stats(nc, "ln4", bns, mean, rstd, var, 1e-5)
        bit_ffn_phase(nc, ins, h, bns, mean, rstd, var, eye, out)


def kernel(**inputs):
    import numpy as np
    import concourse.bacc as bacc
    from concourse.bass_utils import run_bass_kernel_spmd as run

    f = {k: np.ascontiguousarray(v) for k, v in inputs.items()}
    lay = {}
    x = f["x"].reshape(B, 3, 56, 4, 56, 4).transpose(0, 1, 3, 5, 2, 4).reshape(B, 48, TOK)
    x1 = np.ones((B, X1, TOK), np.float32)
    x1[:, 0:48] = x
    lay["xT"] = x1
    keys = np.zeros((B, KT * 128, LO), np.float32)
    keys[:, 0:TOK, 0:X1] = x1.transpose(0, 2, 1)
    lay["xkey"] = keys.reshape(B, KT, 128, LO).transpose(0, 2, 1, 3)
    conv = np.zeros((D, X1), np.float32)
    conv[:, 0:48] = f["L0_tok_conv_w"].reshape(D, 48)
    conv[:, 48] = f["L0_tok_conv_b"]
    lay["conv"] = conv.reshape(2, KC, X1).transpose(1, 0, 2)
    w = np.stack([f["L0_tok_q_w"].T, f["L0_tok_k_w"].T, f["L0_tok_v_w"].T])
    lay["wqkv"] = w.reshape(3, 2, KC, 96).transpose(2, 0, 1, 3)
    lay["bqkv"] = np.stack([f["L0_tok_q_b"], f["L0_tok_k_b"], f["L0_tok_v_b"]])[None]
    projT = np.zeros((96, D + 1), np.float32)
    projT[:, 0:D] = f["L0_tok_proj_w"].T
    lay["projT"] = projT
    projb = np.ones((1, D + 1), np.float32)
    projb[0, 0:D] = f["L0_tok_proj_b"]
    lay["projb"] = projb
    e48 = np.zeros((1, 128), np.float32)
    e48[0, 48] = e48[0, LO + 48] = 1.0
    lay["e48"] = e48
    lay["eye"] = np.eye(128, dtype=np.float32)

    def pieces(w, n=2):
        return w.reshape(n, w.shape[0] // n, -1).transpose(1, 0, 2)

    lay["wqk"] = pieces(np.concatenate([f["L0_attn_Wq"], f["L0_attn_Wk"]], 1))
    lay["wff"] = pieces(np.concatenate([f["L0_attn_Wf"], f["L0_attn_Wf"]], 1))
    lay["bff"] = np.concatenate([f["L0_attn_bf"], f["L0_attn_bf"]])[:, None]
    lay["wv"] = pieces(f["L0_attn_Wv"])
    lay["wo2"] = pieces(f["L0_attn_Wo"])
    lay["gam2"] = f["L0_attn_gamma"].reshape(2, KC).T
    lay["bet2"] = f["L0_attn_beta"].reshape(2, KC).T
    lay["sgn"] = np.repeat(np.float32([1.0, -1.0]), 64)[:, None]
    lay["mask"] = np.triu(np.ones((T, T), np.float32))

    E = 8
    lay["w1"] = pieces(f["L0_ffn_w1"])
    lay["b1"] = f["L0_ffn_b1"][:, None]
    lay["w2"] = np.concatenate([f["L0_ffn_w2"], f["L0_ffn_b2"][None]], 0)
    lay["down"] = f["L0_ffn_down_w"].reshape(E, 2, KC, 256).transpose(2, 0, 1, 3)
    lay["downb"] = f["L0_ffn_down_b"].reshape(E * 2, 128).T
    lay["up"] = f["L0_ffn_up_w"].reshape(E, 2, 128, D).transpose(2, 0, 1, 3)
    lay["gam3"] = np.broadcast_to(f["L0_ffn_gamma"], (T, D))
    lay["bet3"] = np.broadcast_to(f["L0_ffn_beta"], (T, D))
    lay["tri"] = np.broadcast_to(np.tril(np.ones((E, E), np.float32), -1), (T, E, E))
    lay["wT4"] = pieces(f["L1_attn_w_qkv"].T)
    lay["wq4"] = pieces(f["L1_attn_w_qkv"][0:D])
    lay["wpT4"] = pieces(f["L1_attn_w_proj"].T)
    lay["heads"] = np.kron(np.eye(6, dtype=np.float32), np.ones((16, 16), np.float32))
    lay["bproj4"] = f["L1_attn_b_proj"][None]
    lay["win5"] = pieces(f["L1_ffn_w_in"].T)
    lay["wout5"] = pieces(f["L1_ffn_w_out"].T, 4)
    lay["gin5"] = np.broadcast_to(f["L1_ffn_g_in"], (T, D))
    lay["gout5"] = np.broadcast_to(f["L1_ffn_g_out"], (T, 512))

    nc = bacc.Bacc("TRN2", target_bir_lowering=False, num_devices=1)
    arrays, ins = {}, {}
    for name, a in lay.items():
        a = np.ascontiguousarray(a)
        arrays[f"in_{name}"] = a
        ins[name] = nc.dram_tensor(f"in_{name}", a.shape, mybir.dt.from_np(a.dtype), kind="ExternalInput").ap()
    out = nc.dram_tensor("out_0", (B, TOK, D), F32, kind="ExternalOutput").ap()
    vit_tower(nc, ins, out)
    r = run(nc, [arrays], core_ids=[0])
    return r.results[0]["out_0"]
```

```python
from contextlib import ExitStack

import concourse.bass as bass
from concourse import mybir

F32 = mybir.dt.float32
F32R = mybir.dt.float32r
BF16 = mybir.dt.bfloat16
ACT = mybir.ActivationFunctionType
ALU = mybir.AluOpType
AX = mybir.AxisListType

B = 4
TOK = 3136
D = 192
KC = 96
T = 112
TPI = TOK // T
NT = B * TPI
CH = 448
TPC = CH // T
CPI = TOK // CH
NC = B * CPI
X1 = 49
LO = 64
XS = LO + X1
KT = 25
KEYS = KT * 128
ZMIN = -13.815509557963773
SHIFT_SLOT = 11
PROJECT_SLOTS = (2, 4)
SLOTS = 13



def allocator(nc, ctx):
    def sb(name, shape, dt=F32):
        return ctx.enter_context(nc.sbuf_tensor(name, shape, dt))

    def ps(name, shape, dt=F32):
        return ctx.enter_context(nc.psum_tensor(name, shape, dt))

    def sem(name):
        return ctx.enter_context(nc.semaphore(name))
    return sb, ps, sem


def mixer_phase(nc, ins, h, bns, eye):
    with ExitStack() as ctx:
        sb, ps, sem = allocator(nc, ctx)
        conv = sb("conv", [KC, 2, X1])
        wqkv = sb("wqkv", [KC, 3, 2, 96])
        bqkv = sb("bqkv", [1, 3, 96])
        projT = sb("projT", [96, D + 1])
        projb = sb("projb", [1, D + 1])
        e48 = sb("e48", [1, 128])
        wT = sb("wT", [96, 3, 128])
        A2 = sb("A2", [X1, XS])
        W2 = sb("W2", [128, D + 1])
        eyer = sb("eyer", [T, T], F32R)
        x32 = [sb(f"x32_{i}", [XS, KEYS]) for i in range(2)]
        xhl = [sb(f"xhl_{i}", [XS, KEYS], F32R) for i in range(2)]
        xkey = [sb(f"xkey_{i}", [128, KT, LO]) for i in range(2)]
        y32 = sb("y32", [XS, CH])
        ysum = sb("ysum", [XS, CH])
        yh1 = sb("yh1", [XS, CH], F32R)
        yh = sb("yh", [XS, CH], F32R)
        yl = sb("yl", [XS, CH], F32R)
        pmax = sb("pmax", [T, TPC, CPI])
        negmax = sb("negmax", [T, TPC, XS], F32R)
        prob = [sb(f"prob{i}", [128, 2, CH]) for i in range(3)]
        oT = sb("oT", [128, CH])
        rden = sb("rden", [T, TPC, 1])

        pscore = [ps(f"pscore{i}", [128, 2, 512]) for i in range(2)]
        ppre = [ps(f"ppre{i}", [T, 512]) for i in range(2)]
        pout = ps("pout", [128, 512])
        pmisc = ps("pmisc", [128, 512])

        w_in = sem("w_in")
        x_in = [sem(f"x_in{i}") for i in range(2)]
        zeroed = sem("zeroed")
        x_split = sem("x_split")
        fold_mm = sem("fold_mm")
        folded = sem("folded")
        y_mm = sem("y_mm")
        y_out = sem("y_out")
        pre_mm = sem("pre_mm")
        pre_max = sem("pre_max")
        max_ready = sem("max_ready")
        shift_mm = sem("shift_mm")
        y_shifted = sem("y_shifted")
        scores = sem("scores")
        exped = sem("exped")
        pv = sem("pv")
        o_out = sem("o_out")
        proj_mm = sem("proj_mm")
        proj_out = sem("proj_out")
        dvec = sem("dvec")
        block = ctx.enter_context(nc.Block())

        @block.sync
        def _(sp):
            sp.dma_start(conv[:], ins["conv"]).then_inc(w_in, 16)
            sp.dma_start(wqkv[:], ins["wqkv"]).then_inc(w_in, 16)
            sp.dma_start(bqkv[:], ins["bqkv"]).then_inc(w_in, 16)
            sp.dma_start(projT[:], ins["projT"]).then_inc(w_in, 16)
            sp.dma_start(projb[:], ins["projb"]).then_inc(w_in, 16)
            sp.dma_start(e48[:], ins["e48"]).then_inc(w_in, 16)
            sp.dma_start(eye[:], ins["eye"]).then_inc(w_in, 16)
            for b in range(B):
                if b < 2:
                    sp.wait_ge(zeroed, b + 1)
                else:
                    sp.wait_ge(pv, SLOTS * CPI * (b - 1))
                sp.dma_start(x32[b % 2][0:X1, 0:TOK], ins["xT"][b]).then_inc(x_in[b % 2], 16)
                sp.dma_start(x32[b % 2][LO:XS, 0:TOK], ins["xT"][b]).then_inc(x_in[b % 2], 16)
                sp.dma_start(xkey[b % 2][:], ins["xkey"][b]).then_inc(x_in[b % 2], 16)

        @block.gpsimd
        def _(pool):
            nc.gpsimd.memset(x32[0][:], 0.0).then_inc(zeroed, 1)
            nc.gpsimd.memset(x32[1][:], 0.0).then_inc(zeroed, 1)
            nc.gpsimd.memset(negmax[:].bitcast(F32), 0.0).then_inc(zeroed, 1)
            nc.gpsimd.memset(wT[:], 0.0).then_inc(zeroed, 1)
            for b in range(B):
                pool.wait_ge(x_in[b % 2], 48 * (b // 2 + 1))
                pool.wait_ge(x_split, 2 * b) if b else pool.wait_ge(zeroed, 4)
                if b >= 2:
                    pool.wait_ge(pv, SLOTS * CPI * (b - 1))
                nc.gpsimd.tensor_copy(xhl[b % 2][:], x32[b % 2][:]).then_inc(x_split, 1)
                pool.wait_ge(x_split, 2 * b + 1)
                nc.gpsimd.tensor_tensor(xhl[b % 2][LO:XS, :], x32[b % 2][LO:XS, :],
                                        xhl[b % 2][LO:XS, :].bitcast(F32), ALU.subtract).then_inc(x_split, 1)

        @block.scalar
        def _(act):
            def slots(g):
                for j in range(SLOTS):
                    act.wait_ge(scores, g * SLOTS + j + 1)
                    if j >= 3:
                        act.wait_ge(pv, g * SLOTS + j - 2)
                    elif j == 0 and not (isinstance(g, int) and g == 0):
                        act.wait_ge(pv, g * SLOTS)
                    if j < SLOTS - 1:
                        nc.scalar.activation(prob[j % 3][:, :, :], pscore[j % 2][:, :, 0:CH],
                                             ACT.Exp).then_inc(exped, 1)
                    else:
                        nc.scalar.activation(prob[j % 3][:, 0, :], pscore[j % 2][:, 0, 0:CH],
                                             ACT.Exp).then_inc(exped, 1)

            nc.scalar.preload_act_table(ACT.Exp)
            slots(0)
            with act.Fori(1, NC) as g:
                slots(g)

        @block.tensor
        def _(pe):
            pe.wait_ge(w_in, 16 * 7)
            for i in range(3):
                for c in range(2):
                    pe.matmul(pmisc[0:96, i * 64:i * 64 + X1], wqkv[:, i, c, :], conv[:, c, :],
                              start=(c == 0), stop=False)
                pe.matmul(pmisc[0:96, i * 64:i * 64 + X1], bqkv[:, i, :], e48[:, 0:X1],
                          start=False, stop=True).then_inc(fold_mm, 1)
            pe.wait_ge(folded, 5)
            pe.matmul(ppre[0][0:X1, 0:XS], wT[:, 0, 0:X1], wT[:, 1, 0:XS], start=True, stop=True).then_inc(fold_mm, 1)
            pe.matmul(pout[:, 0:D + 1], wT[:, 2, :], projT[:], start=True, stop=False)
            pe.matmul(pout[:, 0:D + 1], e48[:], projb[:], start=False, stop=True).then_inc(fold_mm, 1)
            pe.wait_ge(folded, 8)

            def make_y(g, b, c):
                pe.matmul(pmisc[0:XS, 0:CH], A2[:], x32[b % 2][0:X1, bass.ds(c * CH, CH)],
                          start=True, stop=True).then_inc(y_mm, 1)

            def first_scores(g, b, k):
                q, kc = k // CPI, k % CPI
                pe.wait_ge(pre_max, g * TPC * CPI + k - 1) if k >= 2 else pe.wait_ge(pre_max, g * TPC * CPI)
                pe.matmul(ppre[k % 2][:, 0:CH], yh1[:, q * T:(q + 1) * T],
                          xhl[b % 2][:, kc * CH:(kc + 1) * CH], start=True, stop=True).then_inc(pre_mm, 1)

            def shift(g):
                pe.wait_ge(max_ready, (g + 1) * TPC)
                for q in range(TPC):
                    mm = pe.matmul(pmisc[0:XS, q * T:(q + 1) * T], negmax[:, q, :], eyer[:],
                                   start=True, stop=True)
                mm.then_inc(shift_mm, 1)

            def slot_scores(g, b, j, between=lambda: None):
                if j >= 2:
                    pe.wait_ge(exped, g * SLOTS + j - 1)
                elif j == 0:
                    pe.wait_ge(exped, g * SLOTS)
                for i in range(2 if j < SLOTS - 1 else 1):
                    k = 2 * j + i
                    out, keys = pscore[j % 2][:, i, 0:CH], xhl[b % 2][:, k * 128:(k + 1) * 128]
                    pe.matmul(out, keys, yh[:], start=True, stop=False)
                    mm = pe.matmul(out, keys, yl[:], start=False, stop=True)
                    if j == SLOTS - 1 or i == 1:
                        mm.then_inc(scores, 1)
                    between()

            def slot_pv(g, b, j):
                pe.wait_ge(exped, g * SLOTS + j + 1)
                if j == 0:
                    pe.wait_ge(o_out, g)
                if j < SLOTS - 1:
                    for i in range(2):
                        mm = pe.matmul(pout[i * LO:(i + 1) * LO, 0:CH], xkey[b % 2][:, 2 * j + i, :],
                                       prob[j % 3][:, i, :], start=(j == 0), stop=(i == 1 and j == SLOTS - 2),
                                       tile_position=(0, i * LO))
                else:
                    mm = pe.matmul(pout[0:LO, 0:CH], xkey[b % 2][:, 2 * j, :], prob[j % 3][:, 0, :],
                                   start=False, stop=True, tile_position=(0, 0))
                mm.then_inc(pv, 1)

            def project(g, r):
                for i in range(2):
                    q = 2 * r + i
                    mm = pe.matmul(pmisc[0:T, i * (D + 1):(i + 1) * (D + 1)], oT[:, q * T:(q + 1) * T], W2[:],
                                   start=True, stop=True, skip_group_check=True)
                mm.then_inc(proj_mm, 1)

            def chunk(g, b, nxt, first=False, last=False):
                pe.wait_ge(y_shifted, 2 * g + 2)
                todo = list(range(TPC * CPI)) if nxt is not None else []

                def first_pass():
                    if todo:
                        first_scores(g + 1, nxt[0], todo.pop(0))

                slot_scores(g, b, 0)
                for j in range(SLOTS):
                    if j == 1 and nxt is not None:
                        pe.wait_ge(y_out, 2 * (g + 2))
                    run = first_pass if 1 <= j < SHIFT_SLOT else lambda: None
                    if j < SLOTS - 1:
                        slot_scores(g, b, j + 1, run)
                    if j == 0 and nxt is not None:
                        if not first:
                            pe.wait_ge(y_shifted, 2 * g + 2)
                        if nxt[0] != b:
                            pe.wait_ge(x_split, 2 * (nxt[0] + 1))
                        make_y(g + 1, *nxt)
                    if j in PROJECT_SLOTS and not first:
                        if j == PROJECT_SLOTS[0]:
                            pe.wait_ge(o_out, g)
                            if nxt is not None:
                                pe.wait_ge(y_out, 2 * (g + 2))
                        else:
                            pe.wait_ge(proj_out, 4 * g - 2)
                        project(g - 1, PROJECT_SLOTS.index(j))
                    if j == SHIFT_SLOT and nxt is not None:
                        if not first:
                            pe.wait_ge(proj_out, 4 * g)
                        shift(g + 1)
                    slot_pv(g, b, j)
                    run()

            pe.wait_ge(x_split, 2)
            make_y(0, 0, 0)
            pe.wait_ge(y_out, 2)
            for k in range(TPC * CPI):
                first_scores(0, 0, k)
            shift(0)
            for b in range(B):
                chunk(b * CPI, b, (b, 1), first=(b == 0))
                with pe.Fori(1, CPI - 1) as c:
                    chunk(b * CPI + c, b, (b, c + 1))
                chunk(b * CPI + CPI - 1, b, (b + 1, 0) if b + 1 < B else None)
            pe.wait_ge(o_out, NC)
            project(NC - 1, 0)
            pe.wait_ge(proj_out, 4 * NC - 2)
            project(NC - 1, 1)

        @block.vector
        def _(dve):
            dve.wait_ge(w_in, 16 * 7)
            nc.vector.tensor_copy(eyer[:], eye[0:T, 0:T]).then_inc(folded, 1)
            dve.wait_ge(zeroed, 4)
            dve.wait_ge(fold_mm, 3)
            nc.vector.tensor_scalar(wT[:, 0, 0:X1], pmisc[0:96, 0:X1], 96 ** -0.5, None,
                                    ALU.mult).then_inc(folded, 1)
            nc.vector.tensor_copy(wT[:, 1:3, 0:X1],
                                  pmisc[0:96, 64:192].rearrange("p (i c) -> p i c", i=2)[:, :, 0:X1]).then_inc(folded, 1)
            nc.vector.tensor_copy(wT[:, 1, LO:XS], pmisc[0:96, 64:64 + X1]).then_inc(folded, 1)
            nc.vector.tensor_copy(wT[:, 2, LO:XS], pmisc[0:96, 128:128 + X1]).then_inc(folded, 1)
            dve.wait_ge(fold_mm, 5)
            nc.vector.tensor_copy(A2[:], ppre[0][0:X1, 0:XS]).then_inc(folded, 1)
            nc.vector.tensor_copy(W2[:], pout[:, 0:D + 1]).then_inc(folded, 1)
            nc.vector.memset(pmax[:], 0.0).then_inc(folded, 1)

            def take_y(g):
                dve.wait_ge(y_mm, g + 1)
                nc.vector.tensor_copy(yh1[:], pmisc[0:XS, 0:CH]).then_inc(y_out, 1)
                nc.vector.tensor_copy(y32[:], pmisc[0:XS, 0:CH]).then_inc(y_out, 1)

            def take_max(g, k):
                q, kc = k // CPI, k % CPI
                dve.wait_ge(pre_mm, g * TPC * CPI + k + 1)
                nc.vector.reduce_max(pmax[:, q, kc:kc + 1], ppre[k % 2][:, 0:CH], AX.X).then_inc(pre_max, 1)
                if kc == CPI - 1:
                    dve.wait_ge(pre_max, g * TPC * CPI + k + 1)
                    nc.vector.tensor_reduce(negmax[:, q, X1 - 1:XS:LO],
                                            pmax[:, q:q + 1, :].broadcast_to([T, 2, CPI]),
                                            AX.X, ALU.max, negate=True).then_inc(max_ready, 1)

            def shift_y(g, first=False):
                dve.wait_ge(shift_mm, g + 1)
                dve.wait_ge(y_out, 2 * (g + 1))
                nc.vector.tensor_tensor(ysum[:], y32[:], pmisc[0:XS, 0:CH], ALU.add).then_inc(dvec, 1)
                dve.wait_ge(dvec, g + 1)
                if not first:
                    dve.wait_ge(scores, g * SLOTS)
                nc.vector.tensor_copy(yh[:], ysum[:]).then_inc(y_shifted, 1)
                dve.wait_ge(y_shifted, 2 * g + 1)
                nc.vector.tensor_tensor(yl[:], ysum[:], yh[:].bitcast(F32), ALU.subtract).then_inc(y_shifted, 1)

            def take_o(g):
                dve.wait_ge(pv, (g + 1) * SLOTS)
                nc.vector.tensor_copy(oT[:], pout[:, 0:CH]).then_inc(o_out, 1)

            def take_projected(g, r):
                dve.wait_ge(proj_mm, 2 * g + r + 1)
                two = pmisc[0:T, 0:2 * (D + 1)].rearrange("p (i c) -> p i c", i=2)
                nc.vector.reciprocal(rden[:, 2 * r:2 * r + 2, :], two[:, :, D:D + 1]).then_inc(proj_rden, 1)
                dve.wait_ge(proj_rden, 2 * g + r + 1)
                for i in range(2):
                    nc.vector.tensor_scalar(h[:, g * TPC + 2 * r + i, :], two[:, i, 0:D], rden[:, 2 * r + i, :], None,
                                            ALU.mult).then_inc(proj_out, 1)

            def take_stats(g):
                for q in range(TPC):
                    nc.vector.bn_stats(bns[:, g * TPC + q, :], h[:, g * TPC + q, :]).then_inc(stat_out, 1)

            proj_rden, stat_out = sem("proj_rden"), sem("stat_out")

            def chunk(g, first=False, last=False):
                if not last:
                    take_y(g + 1)
                    for k in range(TPC * CPI):
                        if not first and k in (5, 11):
                            take_projected(g - 1, (5, 11).index(k))
                        if not first and k == 14:
                            dve.wait_ge(proj_out, 4 * g)
                        take_max(g + 1, k)
                        if not first and k == 14:
                            take_stats(g - 1)
                    shift_y(g + 1)
                else:
                    take_projected(g - 1, 0)
                    take_projected(g - 1, 1)
                    dve.wait_ge(proj_out, 4 * g)
                    take_stats(g - 1)
                take_o(g)

            take_y(0)
            for k in range(TPC * CPI):
                take_max(0, k)
            shift_y(0, first=True)
            chunk(0, first=True)
            with dve.Fori(1, NC - 1) as g:
                chunk(g)
            chunk(NC - 1, last=True)
            take_projected(NC - 1, 0)
            take_projected(NC - 1, 1)
            dve.wait_ge(proj_out, 4 * NC)
            take_stats(NC - 1)


def finish_stats(nc, name, bns, mean, rstd, vtok, eps):
    with ExitStack() as ctx:
        sb, ps, sem = allocator(nc, ctx)
        dif = sb(f"dif_{name}", [T, NT])
        var = sb(f"var_{name}", [T, NT])
        mhalf = sb(f"mhalf_{name}", [T, NT])
        done = sem(f"stats_{name}")
        ready = sem(f"var_{name}_ready")
        block = ctx.enter_context(nc.Block())

        @block.vector
        def _(dve):
            nc.vector.tensor_tensor(mean[:], bns[:, :, 1], bns[:, :, 4], ALU.add).then_inc(done, 1)
            nc.vector.tensor_tensor(dif[:], bns[:, :, 1], bns[:, :, 4], ALU.subtract).then_inc(done, 1)
            nc.vector.tensor_tensor(var[:], bns[:, :, 2], bns[:, :, 5], ALU.add).then_inc(done, 1)
            dve.wait_ge(done, 3)
            nc.vector.tensor_scalar(mean[:], mean[:], 0.5, None, ALU.mult).then_inc(done, 1)
            nc.vector.scalar_tensor_tensor(dif[:], dif[:], D / 4, dif[:], ALU.mult, ALU.mult).then_inc(done, 1)
            dve.wait_ge(done, 5)
            nc.vector.tensor_tensor(var[:], var[:], dif[:], ALU.add).then_inc(done, 1)
            dve.wait_ge(done, 6)
            nc.vector.tensor_scalar(vtok[:], var[:], 1.0 / D, None, ALU.mult).then_inc(done, 1)
            dve.wait_ge(done, 7)
            nc.vector.tensor_scalar(var[:], vtok[:], eps, None, ALU.add).then_inc(ready, 1)

        @block.gpsimd
        def _(pool):
            nc.gpsimd.memset(mhalf[:], -0.5).then_inc(ready, 1)
            pool.wait_ge(ready, 2)
            nc.gpsimd.tensor_tensor(rstd[:], var[:], mhalf[:], ALU.pow)


def retention_phase(nc, ins, h, bns, mean, rstd, eye):
    M = 64
    V1 = D + 1
    with ExitStack() as ctx:
        sb, ps, sem = allocator(nc, ctx)
        wqk = sb("wqk", [KC, 2, 128])
        wff = sb("wff", [KC, 2, 128])
        bff = sb("bff", [128, 1])
        wv = sb("wv", [KC, 2, D])
        wo = sb("wo", [KC + 1, 2, D])
        gam = sb("gam", [KC, 2])
        bet = sb("bet", [KC, 2])
        sgn = sb("sgn", [128, 1])
        mask = sb("mask", [T, T])
        ones = sb("ones_scan", [128, CH])
        eps5 = sb("eps5", [T, TPC])
        mhalf = sb("mhalf4", [T, TPC])
        xn = sb("xn2", [T, TPC, D])
        xT = sb("xT2", [KC, 2, CH])
        gate = sb("gate2", [128, CH])
        elu = sb("elu2", [128, CH])
        cum = sb("cum2", [128, CH])
        dec = sb("dec2", [128, CH])
        tail = sb("tail2", [128, 1])
        qt = sb("qt2", [M, CH])
        kt = sb("kt2", [M, CH])
        ktok = sb("ktok2", [T, TPC, M])
        vt = sb("vt2", [T, TPC, V1])
        at = sb("at2", [T, TPC, T])
        snap = sb("snap2", [M, TPC, V1])
        den = sb("den2", [T, TPC, 1])
        hh = sb("hh2", [T, TPC, D])
        bn = sb("bn2", [T, TPC, 6])
        agg = sb("agg2", [T, TPC, 2])
        veps = sb("veps2", [T, TPC])
        rst = sb("rst2", [T, TPC])
        nT = sb("nT2", [KC + 1, 2, CH])
        ptr = ps("ptr2", [KC, 2, 512])
        pqk = ps("pqk2", [128, 512])
        pff = ps("pff2", [128, 512])
        pvo = ps("pvo2", [T, 2, 512])
        pat = ps("pat2", [T, 512])
        pst = ps("pst2", [M, 512])

        names = ("w_in", "w_ready", "brow_mm", "xn_ready", "xtr_mm", "xT_out", "qk_mm", "ff_mm", "v_mm", "v_out",
                 "nrm_ready", "ntr_mm", "nT_out", "wo_mm", "h_out", "gate_in", "gate_out", "elu_in", "elu_out",
                 "cum_out", "dec_out", "qk_out", "ktr_mm", "ktok_out", "at_mm", "at_out", "st_mm", "snap_out",
                 "num_mm", "hhc", "hh_out", "agg_out", "rst_out", "dvec", "poolc")
        S = {n: sem(f"{n}_2") for n in names}
        block = ctx.enter_context(nc.Block())

        @block.sync
        def _(sp):
            for dst, name in ((wqk, "wqk"), (wff, "wff"), (bff, "bff"), (wv, "wv"), (gam, "gam2"),
                              (bet, "bet2"), (sgn, "sgn"), (mask, "mask")):
                sp.dma_start(dst[:], ins[name]).then_inc(S["w_in"], 16)
            sp.dma_start(wo[0:KC], ins["wo2"]).then_inc(S["w_in"], 16)

        @block.gpsimd
        def _(pool):
            for n, (buf, value) in enumerate(((ones[:], 1.0), (eps5[:], 1e-5), (mhalf[:], -0.5),
                                              (vt[:, :, D:V1], 1.0), (nT[KC:KC + 1], 1.0))):
                nc.gpsimd.memset(buf, value).then_inc(S["w_ready"], 1)
                pool.wait_ge(S["w_ready"], n + 1)

            def chunk(g, first=False):
                if not first:
                    pool.wait_ge(S["rst_out"], g)
                pool.wait_ge(S["agg_out"], g + 1)
                nc.gpsimd.tensor_tensor(veps[:], agg[:, :, 1], eps5[:], ALU.add).then_inc(S["poolc"], 1)
                pool.wait_ge(S["poolc"], g + 1)
                nc.gpsimd.tensor_tensor(rst[:], veps[:], mhalf[:], ALU.pow).then_inc(S["rst_out"], 1)

            chunk(0, first=True)
            with pool.Fori(1, NC) as g:
                chunk(g)

        @block.tensor
        def _(pe):
            pe.wait_ge(S["w_in"], 16 * 9)
            for c in range(2):
                mm = pe.matmul(pst[0:1, 0:D], bet[:, c:c + 1], wo[0:KC, c, :], start=(c == 0), stop=(c == 1))
            mm.then_inc(S["brow_mm"], 1)
            pe.wait_ge(S["w_ready"], 5 + 3)

            def transpose_x(g):
                pe.wait_ge(S["xn_ready"], g + 1)
                for q in range(TPC):
                    for c in range(2):
                        mm = pe.transpose(ptr[:, c, q * T:(q + 1) * T], xn[:, q, c * KC:(c + 1) * KC], eye[0:T, 0:T])
                mm.then_inc(S["xtr_mm"], 1)

            def project(g):
                pe.wait_ge(S["xT_out"], g + 1)
                for dst, w, done in ((pff, wff, "ff_mm"), (pqk, wqk, "qk_mm")):
                    for c in range(2):
                        mm = pe.matmul(dst[:, 0:CH], w[:, c, :], xT[:, c, :], start=(c == 0), stop=(c == 1))
                    mm.then_inc(S[done], 1)

            def values(g, first=False):
                if not first:
                    pe.wait_ge(S["hh_out"], g)
                for q in range(TPC):
                    for c in range(2):
                        mm = pe.matmul(pvo[:, q // 2, (q % 2) * V1:(q % 2) * V1 + D], xT[:, c, q * T:(q + 1) * T],
                                       wv[:, c, :], start=(c == 0), stop=(c == 1), skip_group_check=True)
                mm.then_inc(S["v_mm"], 1)

            def weights(g):
                pe.wait_ge(S["qk_out"], g + 1)
                for q in range(TPC):
                    mm = pe.matmul(pat[:, q * T:(q + 1) * T], kt[:, q * T:(q + 1) * T], qt[:, q * T:(q + 1) * T],
                                   start=True, stop=True)
                mm.then_inc(S["at_mm"], 1)
                for q in range(TPC):
                    mm = pe.transpose(pff[0:T, q * M:(q + 1) * M], kt[:, q * T:(q + 1) * T], eye[0:M, 0:M])
                mm.then_inc(S["ktr_mm"], 1)

            def attend(g, reset, first):
                if not first:
                    pe.wait_ge(S["h_out"], g)
                pe.wait_ge(S["v_out"], g + 1)
                pe.wait_ge(S["ktok_out"], g + 1)
                pe.wait_ge(S["at_out"], g + 1)
                for q in range(TPC):
                    if not (reset and q == 0):
                        pe.wait_ge(S["snap_out"], g * TPC + q)
                    num = pvo[:, q // 2, (q % 2) * V1:(q % 2 + 1) * V1]
                    pe.matmul(pst[:, 0:V1], ktok[:, q, :], vt[:, q, :], start=(reset and q == 0), stop=True,
                              skip_group_check=True).then_inc(S["st_mm"], 1)
                    mm = pe.matmul(num, at[:, q, :], vt[:, q, :], start=True, stop=(reset and q == 0),
                                   skip_group_check=True)
                    if not (reset and q == 0):
                        mm = pe.matmul(num, qt[:, q * T:(q + 1) * T], snap[:, q, :], start=False, stop=True,
                                       skip_group_check=True)
                mm.then_inc(S["num_mm"], 1)

            def transpose_n(g):
                pe.wait_ge(S["nrm_ready"], g + 1)
                for q in range(TPC):
                    for c in range(2):
                        mm = pe.transpose(ptr[:, c, q * T:(q + 1) * T], hh[:, q, c * KC:(c + 1) * KC], eye[0:T, 0:T])
                mm.then_inc(S["ntr_mm"], 1)

            def wo_out(g, last=False):
                pe.wait_ge(S["nT_out"], g + 1)
                if not last:
                    pe.wait_ge(S["v_out"], g + 2)
                for q in range(TPC):
                    for c in range(2):
                        k = KC + 1 if c == 0 else KC
                        mm = pe.matmul(pvo[:, q // 2, (q % 2) * V1:(q % 2) * V1 + D], nT[0:k, c, q * T:(q + 1) * T],
                                       wo[0:k, c, :], start=(c == 0), stop=(c == 1), skip_group_check=True)
                    if q % 2 == 1:
                        mm.then_inc(S["wo_mm"], 1)

            def chunk(g, reset=False, first=False, last=False):
                weights(g)
                if not last:
                    transpose_x(g + 1)
                attend(g, reset, first)
                if not last:
                    project(g + 1)
                    values(g + 1)
                transpose_n(g)
                wo_out(g, last)

            transpose_x(0)
            project(0)
            values(0, first=True)
            chunk(0, reset=True, first=True)
            with pe.Fori(1, CPI) as c:
                chunk(c)
            with pe.Fori(1, B - 1) as b:
                chunk(b * CPI, reset=True)
                with pe.Fori(1, CPI) as c:
                    chunk(b * CPI + c)
            chunk((B - 1) * CPI, reset=True)
            with pe.Fori((B - 1) * CPI + 1, NC - 1) as g:
                chunk(g)
            chunk(NC - 1, last=True)

        @block.scalar
        def _(act):
            nc.scalar.preload_act_table_set("natural_log_exp_and_others")
            act.wait_ge(S["w_ready"], 5 + 3)

            def gate_and_values(g):
                act.wait_ge(S["gate_in"], g + 1)
                nc.scalar.activation(gate[:], gate[:], ACT.Exp, scale=-1.0).then_inc(S["gate_out"], 1)
                act.wait_ge(S["gate_out"], 2 * g + 1)
                nc.scalar.activation(gate[:], gate[:], ACT.Ln, bias=1.0).then_inc(S["gate_out"], 1)
                act.wait_ge(S["elu_in"], g + 1)
                nc.scalar.activation(elu[:], elu[:], ACT.Exp).then_inc(S["elu_out"], 1)
                act.wait_ge(S["v_mm"], g + 1)
                for i in range(2):
                    cp = nc.scalar.copy(vt[:, 2 * i:2 * i + 2, 0:D],
                                        pvo[:, i, 0:2 * V1].rearrange("p (q v) -> p q v", q=2)[:, :, 0:D])
                cp.then_inc(S["v_out"], 1)
                act.wait_ge(S["cum_out"], g + 1)
                nc.scalar.activation(dec[:], cum[:], ACT.Exp, scale=sgn[:]).then_inc(S["dec_out"], 1)

            def chunk(g, last=False):
                act.wait_ge(S["ktr_mm"], g + 1)
                nc.scalar.copy(ktok[:, :, :], pff[0:T, 0:TPC * M].rearrange("p (q m) -> p q m", q=TPC)).then_inc(
                    S["ktok_out"], 1)
                for q in range(TPC):
                    act.wait_ge(S["st_mm"], g * TPC + q + 1)
                    nc.scalar.copy(snap[:, (q + 1) % TPC, :], pst[:, 0:V1]).then_inc(S["snap_out"], 1)
                if not last:
                    gate_and_values(g + 1)
                act.wait_ge(S["ntr_mm"], g + 1)
                nc.scalar.copy(nT[0:KC, :, :], ptr[:, :, 0:CH]).then_inc(S["nT_out"], 1)

            gate_and_values(0)
            with act.Fori(0, NC - 1) as g:
                chunk(g)
            chunk(NC - 1, last=True)

        @block.vector
        def _(dve):
            dve.wait_ge(S["w_in"], 16 * 9)
            dve.wait_ge(S["w_ready"], 5)
            dve.wait_ge(S["brow_mm"], 1)
            nc.vector.tensor_copy(wo[KC:KC + 1, 0, :], pst[0:1, 0:D]).then_inc(S["w_ready"], 1)
            nc.vector.tensor_copy(wo[KC:KC + 1, 1, :], pst[0:1, 0:D]).then_inc(S["w_ready"], 1)
            for c in range(2):
                ts = nc.vector.tensor_scalar(wo[0:KC, c, :], wo[0:KC, c, :], gam[:, c:c + 1], None, ALU.mult)
            ts.then_inc(S["w_ready"], 1)

            def normalise(g):
                for q in range(TPC):
                    t = g * TPC + q
                    ts = nc.vector.tensor_scalar(xn[:, q, :], h[:, t, :], mean[:, bass.ds(t, 1)], rstd[:, bass.ds(t, 1)],
                                                 ALU.subtract, ALU.mult)
                ts.then_inc(S["xn_ready"], 1)

            def take_x(g):
                dve.wait_ge(S["xtr_mm"], g + 1)
                nc.vector.tensor_copy(xT[:, :, :], ptr[:, :, 0:CH]).then_inc(S["xT_out"], 1)

            def sums_out(g):
                dve.wait_ge(S["num_mm"], g + 1)
                step = [g * 3]

                def link(ins):
                    step[0] = step[0] + 1
                    ins.then_inc(S["hhc"], 1)
                    dve.wait_ge(S["hhc"], step[0])

                two = [pvo[:, i, 0:2 * V1].rearrange("p (q v) -> p q v", q=2) for i in range(2)]
                for i in range(2):
                    ts = nc.vector.tensor_scalar(den[:, 2 * i:2 * i + 2, :], two[i][:, :, D:V1], 1e-6, None, ALU.add)
                link(ts)
                link(nc.vector.reciprocal(den[:], den[:]))
                for q in range(TPC):
                    ts = nc.vector.tensor_scalar(hh[:, q, :], two[q // 2][:, q % 2, 0:D], den[:, q, :], None, ALU.mult)
                ts.then_inc(S["hh_out"], 1)
                dve.wait_ge(S["hh_out"], g + 1)
                for q in range(TPC):
                    bs = nc.vector.bn_stats(bn[:, q, :], hh[:, q, :])
                bs.then_inc(S["hhc"], 1)
                dve.wait_ge(S["hhc"], 3 * g + 3)

            def sums_aggr(g):
                for q in range(TPC):
                    ag = nc.vector.bn_aggr(agg[:, q, :], bn[:, q, :])
                ag.then_inc(S["agg_out"], 1)

            def sums_norm(g):
                dve.wait_ge(S["rst_out"], g + 1)
                for q in range(TPC):
                    ts = nc.vector.tensor_scalar(hh[:, q, :], hh[:, q, :], agg[:, q, 0:1], rst[:, q:q + 1],
                                                 ALU.subtract, ALU.mult)
                ts.then_inc(S["nrm_ready"], 1)

            def gate_in(g):
                dve.wait_ge(S["ff_mm"], g + 1)
                nc.vector.tensor_scalar(gate[:], pff[:, 0:CH], bff[:], ZMIN, ALU.add, ALU.max).then_inc(S["gate_in"], 1)

            def elu_in(g):
                dve.wait_ge(S["qk_mm"], g + 1)
                nc.vector.tensor_scalar(elu[:], pqk[:, 0:CH], 0.0, None, ALU.min).then_inc(S["elu_in"], 1)

            def scan(g, reset):
                dve.wait_ge(S["gate_out"], 2 * g + 2)
                nc.vector.tensor_tensor_scan(cum[:], ones[:], gate[:], 0.0 if reset else tail[:],
                                             ALU.mult, ALU.subtract).then_inc(S["dvec"], 1)
                dve.wait_ge(S["dvec"], 3 * g + 1)
                nc.vector.tensor_copy(tail[:], cum[:, CH - 1:CH]).then_inc(S["dvec"], 1)
                dve.wait_ge(S["dvec"], 3 * g + 2)
                nc.vector.tensor_scalar(cum[:], cum[:], -20.0, 20.0, ALU.max, ALU.min).then_inc(S["cum_out"], 1)

            def q_and_k(g):
                dve.wait_ge(S["elu_out"], g + 1)
                nc.vector.scalar_tensor_tensor(elu[:], pqk[:, 0:CH], 0.0, elu[:], ALU.max, ALU.add).then_inc(S["dvec"], 1)
                dve.wait_ge(S["dvec"], 3 * g + 3)
                dve.wait_ge(S["dec_out"], g + 1)
                nc.vector.scalar_tensor_tensor(qt[:], elu[0:M, :], M ** -0.5, dec[0:M, :], ALU.mult, ALU.mult)
                nc.vector.tensor_tensor(kt[:], elu[M:128, :], dec[M:128, :], ALU.mult).then_inc(S["qk_out"], 1)

            def add_out(g):
                for r in range(2):
                    dve.wait_ge(S["wo_mm"], 2 * g + r + 1)
                    hs = h[:, bass.ds(g * TPC + 2 * r, 2), :]
                    tt = nc.vector.tensor_tensor(
                        hs, hs, pvo[:, r, 0:2 * V1].rearrange("p (q v) -> p q v", q=2)[:, :, 0:D], ALU.add)
                tt.then_inc(S["h_out"], 1)

            def take_stats(g):
                for q in range(TPC):
                    nc.vector.bn_stats(bns[:, g * TPC + q, :], h[:, g * TPC + q, :])

            def chunk(g, reset_next=False, first=False, last=False, enter=True):
                if not first:
                    dve.wait_ge(S["h_out"], g)
                dve.wait_ge(S["at_mm"], g + 1)
                nc.vector.tensor_tensor(at[:, :, :], pat[:, 0:CH].rearrange("p (q t) -> p q t", q=TPC),
                                        mask[:, :].unsqueeze(1).broadcast_to([T, TPC, T]), ALU.mult).then_inc(S["at_out"], 1)
                if not last:
                    take_x(g + 1)
                if not first:
                    take_stats(g - 1)
                if enter:
                    normalise(g + 2)
                sums_out(g)
                if last:
                    sums_aggr(g)
                else:
                    gate_in(g + 1)
                    sums_aggr(g)
                    elu_in(g + 1)
                    scan(g + 1, reset_next)
                sums_norm(g)
                if not last:
                    q_and_k(g + 1)
                add_out(g)

            normalise(0)
            take_x(0)
            normalise(1)
            gate_in(0)
            elu_in(0)
            scan(0, True)
            q_and_k(0)
            chunk(0, first=True)
            with dve.Fori(1, CPI - 1) as c:
                chunk(c)
            chunk(CPI - 1, reset_next=True)
            with dve.Fori(1, B - 1) as b:
                with dve.Fori(0, CPI - 1) as c:
                    chunk(b * CPI + c)
                chunk(b * CPI + CPI - 1, reset_next=True)
            with dve.Fori((B - 1) * CPI, NC - 2) as g:
                chunk(g)
            chunk(NC - 2, enter=False)
            chunk(NC - 1, last=True, enter=False)
            dve.wait_ge(S["h_out"], NC)
            take_stats(NC - 1)


def expert_phase(nc, ins, h, bns, mean, rstd, eye):
    E, HID = 8, 256
    with ExitStack() as ctx:
        sb, ps, sem = allocator(nc, ctx)
        w1h = sb("w1h", [128, 2, KC], F32R)
        w1l = sb("w1l", [128, 2, KC], F32R)
        w1s = sb("w1s", [128, 2, KC])
        b1 = sb("b1_3", [KC, 1])
        w2 = sb("w2_3", [KC + 1, E])
        downh = sb("downh", [128, 2, E, HID], F32R)
        downl = sb("downl", [128, 2, E, HID], F32R)
        downb = sb("downb", [128, 2 * E])
        uph = sb("uph", [128, E, 2, D], F32R)
        upl = sb("upl", [128, E, 2, D], F32R)
        gam = sb("gam3", [T, D])
        bet = sb("bet3", [T, D])
        tri = sb("tri", [T, E, E])
        eps5 = sb("eps5_3", [T, TPC])
        mhalf = sb("mhalf_3", [T, TPC])
        xth = sb("xth3", [128, 2, CH], F32R)
        xtl = sb("xtl3", [128, CH], F32R)
        r1 = sb("r1", [KC + 1, CH])
        lg = sb("lg", [T, TPC, E])
        ex = sb("ex", [T, TPC, E])
        small = sb("small3", [T, TPC, 1])
        gt = sb("gt3", [T, TPC * E, E])
        eq = sb("eq3", [T, TPC * E, E])
        gates = sb("gates", [T, TPC, E])
        zh = [[sb(f"zh{i}{m}", [128, CH], F32R) for m in range(2)] for i in range(2)]
        zl = [[sb(f"zl{i}{m}", [128, CH], F32R) for m in range(2)] for i in range(2)]
        stage = sb("stage3", [128, 2, 2048])
        z = [stage[:, 0, m * CH:(m + 1) * CH] for m in range(2)]
        acc = stage[0:T, 0, 1024:1024 + TPC * D].rearrange("p (q d) -> p q d", q=TPC)
        xn = stage[0:T, 1, 0:1024].rearrange("p (q d) -> p q d", q=TPC)
        yf = stage[0:T, 1, 1024:1024 + TPC * D].rearrange("p (q d) -> p q d", q=TPC)
        bn = sb("bn3", [T, TPC, 6])
        agg = sb("agg3", [T, TPC, 2])
        veps = sb("veps3", [T, TPC])
        rst = sb("rst3", [T, TPC])
        ptr = ps("ptr3", [128, 2, 512])
        prt = ps("prt3", [KC, 512])
        plg = ps("plg3", [T, TPC * E])
        pz = [ps(f"pz{m}", [128, 512]) for m in range(2)]
        py = ps("py3", [T, 2, 512])
        names = ("w_in", "w_ready", "xn_ready", "xtr_mm", "xT_out", "r1_mm", "r1_out", "lg_mm", "dvec", "lg_out",
                 "ex_out", "gates_out", "down_mm", "z_out", "zl_out", "xL_out", "split", "stage_in", "veps_out", "gam_out", "mx_out", "up_mm", "acc_out", "stat_out", "agg_out", "rst_out",
                 "nrm_out", "poolc", "yf_out", "h_out")
        S = {n: sem(f"{n}_3") for n in names}
        block = ctx.enter_context(nc.Block())
        NW = 7
        UPH = E // 2 * 2 * D

        @block.sync
        def _(sp):
            for half in range(2):
                sp.dma_start(stage[:, half, :], ins["down"][:, half].rearrange("p e d -> p (e d)")).then_inc(
                    S["stage_in"], 16)
            for dst, name in ((w1s[:], "w1"), (b1[:], "b1"), (w2[:], "w2"), (downb[:], "downb"), (gam[:], "gam3"),
                              (bet[:], "bet3"), (tri[:], "tri")):
                sp.dma_start(dst, ins[name]).then_inc(S["w_in"], 16)
            for half in range(2):
                sp.wait_ge(S["split"], 2 * half + 2)
                sp.dma_start(stage[:, half, 0:UPH],
                             ins["up"][:, half * E // 2:(half + 1) * E // 2].rearrange("p e m d -> p (e m d)")
                             ).then_inc(S["stage_in"], 16)

        @block.gpsimd
        def _(pool):
            for n, (buf, value) in enumerate(((eps5[:], 1e-5), (mhalf[:], -0.5), (r1[KC:KC + 1], 1.0))):
                nc.gpsimd.memset(buf, value).then_inc(S["w_ready"], 1)
                pool.wait_ge(S["w_ready"], n + 1)
            pool.wait_ge(S["w_in"], 16 * NW)

            def low(g, e, first=False):
                for m in range(2):
                    if m or e or not first:
                        pool.wait_ge(S["zl_out"], 2 * (g * E + e) + m)
                    pool.wait_ge(S["z_out"], 2 * (g * E + e) + m + 1)
                    nc.gpsimd.tensor_tensor(zl[e % 2][m][:], z[m][:], zh[e % 2][m][:].bitcast(F32),
                                            ALU.subtract).then_inc(S["zl_out"], 1)

            def factor(g, done):
                pool.wait_ge(S["zl_out"], done)
                pool.wait_ge(S["agg_out"], g + 1)
                nc.gpsimd.tensor_tensor(veps[:], agg[:, :, 1], eps5[:], ALU.add).then_inc(S["veps_out"], 1)
                pool.wait_ge(S["veps_out"], g + 1)
                nc.gpsimd.tensor_tensor(rst[:], veps[:], mhalf[:], ALU.pow).then_inc(S["rst_out"], 1)
                pool.wait_ge(S["rst_out"], g + 1)

            def times_gamma(g, done):
                pool.wait_ge(S["zl_out"], done)
                pool.wait_ge(S["nrm_out"], g + 1)
                nc.gpsimd.tensor_tensor(yf, yf, gam[:].unsqueeze(1).broadcast_to([T, TPC, D]),
                                        ALU.mult).then_inc(S["gam_out"], 1)
                pool.wait_ge(S["gam_out"], g + 1)

            def plus_beta(g, done):
                pool.wait_ge(S["zl_out"], done)
                nc.gpsimd.tensor_tensor(yf, yf, bet[:].unsqueeze(1).broadcast_to([T, TPC, D]),
                                        ALU.add).then_inc(S["yf_out"], 1)
                pool.wait_ge(S["yf_out"], g + 1)

            def chunk(g, first=False):
                done = 2 * E * g
                for e in range(E):
                    low(g, e, first)
                    if not first and e == 2:
                        factor(g - 1, done + 6)
                    if not first and e == 3:
                        times_gamma(g - 1, done + 8)
                    if not first and e == 4:
                        plus_beta(g - 1, done + 10)

            chunk(0, first=True)
            with pool.Fori(1, NC) as g:
                chunk(g)
            factor(NC - 1, 2 * E * NC)
            times_gamma(NC - 1, 2 * E * NC)
            plus_beta(NC - 1, 2 * E * NC)

        @block.tensor
        def _(pe):
            pe.wait_ge(S["w_in"], 16 * NW)
            pe.wait_ge(S["w_ready"], 3)

            def split_product(dst, wh, wl, cols):
                steps = ((wh[:, 0], xth[:, 0, :]), (wh[:, 0], xtl[:]), (wl[:, 0], xth[:, 0, :]),
                         (wh[:, 1], xth[:, 1, :]), (wl[0:64, 1], xth[0:64, 1, :]))
                for n, (w, x) in enumerate(steps):
                    mm = pe.matmul(dst, w[:, cols], x, start=(n == 0), stop=(n == 4))
                return mm

            def front(g):
                pe.wait_ge(S["xn_ready"], g + 1)
                for q in range(TPC):
                    for c in range(2):
                        mm = pe.transpose(ptr[:, c, q * T:(q + 1) * T], xn[:, q, c * 128:(c + 1) * 128], eye[0:T, 0:T])
                mm.then_inc(S["xtr_mm"], 1)

            def router(g):
                pe.wait_ge(S["xL_out"], g + 1)
                if isinstance(g, int) and g == 0:
                    pe.wait_ge(S["split"], 10)
                split_product(prt[:, 0:CH], w1h, w1l, slice(0, KC)).then_inc(S["r1_mm"], 1)

            def logits(g):
                pe.wait_ge(S["r1_out"], g + 1)
                for q in range(TPC):
                    mm = pe.matmul(plg[:, q * E:(q + 1) * E], r1[:, q * T:(q + 1) * T], w2[:], start=True, stop=True,
                                   skip_group_check=True)
                mm.then_inc(S["lg_mm"], 1)

            def down_e(g, e, m, first=False):
                if e >= 1 or not first:
                    pe.wait_ge(S["z_out"], 2 * (g * E + e) - 1 + m)
                split_product(pz[m][:, 0:CH], downh[:, :, e], downl[:, :, e],
                              slice(m * 128, (m + 1) * 128)).then_inc(S["down_mm"], 1)

            def up_e(g, e, first):
                pe.wait_ge(S["zl_out"], 2 * (g * E + e) + 2)
                for q in range(TPC):
                    if q % 2 == 0 and (e >= 1 or not first):
                        pe.wait_ge(S["acc_out"], 2 * (g * E + e) - 1 + q // 2)
                    cols = slice(q * T, (q + 1) * T)
                    for m in range(2):
                        for n, (zz, w) in enumerate(((zh, uph), (zl, uph), (zh, upl))):
                            mm = pe.matmul(py[:, q // 2, (q % 2) * D:(q % 2 + 1) * D], zz[e % 2][m][:, cols],
                                           w[:, e, m, :], start=(m + n == 0), stop=(m + n == 3), skip_group_check=True)
                    if q % 2 == 1:
                        mm.then_inc(S["up_mm"], 1)

            def chunk(g, first=False, last=False):
                for e in range(1, E):
                    down_e(g, e, 0)
                    down_e(g, e, 1)
                    if e == 5 and not last:
                        front(g + 1)
                    up_e(g, e - 1, first)
                if not last:
                    router(g + 1)
                    down_e(g + 1, 0, 0)
                    logits(g + 1)
                    down_e(g + 1, 0, 1)
                up_e(g, E - 1, first)

            front(0)
            router(0)
            down_e(0, 0, 0, first=True)
            logits(0)
            down_e(0, 0, 1, first=True)
            chunk(0, first=True)
            with pe.Fori(1, NC - 1) as g:
                chunk(g)
            chunk(NC - 1, last=True)

        @block.scalar
        def _(act):
            def take_x(g):
                if not isinstance(g, int) or g > 0:
                    act.wait_ge(S["down_mm"], 2 * E * g)
                act.wait_ge(S["xtr_mm"], g + 1)
                nc.scalar.copy(xth[:, :, :], ptr[:, :, 0:CH]).then_inc(S["xT_out"], 1)

            def take_r1(g):
                act.wait_ge(S["r1_mm"], g + 1)
                nc.scalar.activation(r1[0:KC], prt[:, 0:CH], ACT.Gelu, bias=b1[:]).then_inc(S["r1_out"], 1)

            def gelu_e(g, e, first=False):
                for m in range(2):
                    if e or not first:
                        act.wait_ge(S["zl_out"], 2 * (g * E + e) - 1 + m)
                    act.wait_ge(S["down_mm"], 2 * (g * E + e) + m + 1)
                    nc.scalar.activation(z[m][:], pz[m][:, 0:CH], ACT.Gelu, bias=downb[:, 2 * e + m:2 * e + m + 1])
                    if m == 0 and (e >= 2 or not first):
                        act.wait_ge(S["up_mm"], 2 * (g * E + e) - 2)
                    nc.scalar.activation(zh[e % 2][m][:], pz[m][:, 0:CH], ACT.Gelu,
                                         bias=downb[:, 2 * e + m:2 * e + m + 1]).then_inc(S["z_out"], 1)

            def chunk(g, first=False, last=False):
                take_r1(g)
                gelu_e(g, 0, first)
                act.wait_ge(S["lg_out"], g + 1)
                nc.scalar.activation(ex[:], lg[:], ACT.Exp).then_inc(S["ex_out"], 1)
                gelu_e(g, 1, first)
                for e in range(2, E - 1):
                    gelu_e(g, e)
                if not last:
                    take_x(g + 1)
                gelu_e(g, E - 1)

            act.wait_ge(S["w_in"], 16 * NW)
            take_x(0)
            chunk(0, first=True)
            with act.Fori(1, NC - 1) as g:
                chunk(g)
            chunk(NC - 1, last=True)

        @block.vector
        def _(dve):
            dve.wait_ge(S["w_in"], 16 * NW)
            CHAIN = 11

            def normalise(g):
                for q in range(TPC):
                    t = g * TPC + q
                    nc.vector.tensor_scalar(xn[:, q, 0:D], h[:, t, :], mean[:, bass.ds(t, 1)],
                                            rstd[:, bass.ds(t, 1)], ALU.subtract, ALU.mult)
                for q in range(TPC):
                    t = g * TPC + q
                    ts = nc.vector.tensor_scalar(xn[:, q, D:256], h[:, t, 128:D], mean[:, bass.ds(t, 1)],
                                                 rstd[:, bass.ds(t, 1)], ALU.subtract, ALU.mult)
                ts.then_inc(S["xn_ready"], 1)

            def take_low(g):
                dve.wait_ge(S["xT_out"], g + 1)
                nc.vector.tensor_tensor(xtl[:], ptr[:, 0, 0:CH], xth[:, 0, :].bitcast(F32), ALU.subtract)
                nc.vector.tensor_tensor(xth[64:128, 1, :], ptr[64:128, 1, 0:CH], xth[64:128, 1, :].bitcast(F32),
                                        ALU.subtract).then_inc(S["xL_out"], 1)

            def softmax_head(g, first=False):
                logit = plg[:].rearrange("p (q e) -> p q e", q=TPC)
                if not first:
                    dve.wait_ge(S["gates_out"], g)
                dve.wait_ge(S["lg_mm"], g + 1)
                nc.vector.tensor_reduce(small[:, :, 0], logit, AX.X, ALU.max).then_inc(S["mx_out"], 1)
                dve.wait_ge(S["mx_out"], g + 1)
                nc.vector.tensor_tensor(lg[:], logit, small[:].broadcast_to([T, TPC, E]),
                                        ALU.subtract).then_inc(S["lg_out"], 1)

            def top2(g, first):
                step = [g * CHAIN]

                def link(ins):
                    step[0] = step[0] + 1
                    ins.then_inc(S["dvec"], 1)
                    dve.wait_ge(S["dvec"], step[0])

                dve.wait_ge(S["lg_out"], g + 1)
                dve.wait_ge(S["ex_out"], g + 1)
                link(nc.vector.tensor_reduce(small[:, :, 0], ex[:], AX.X, ALU.add))
                link(nc.vector.reciprocal(small[:], small[:]))
                link(nc.vector.tensor_tensor(ex[:], ex[:], small[:].broadcast_to([T, TPC, E]), ALU.mult))
                pe_ = ex[:].unsqueeze(3).broadcast_to([T, TPC, E, E])
                pj = ex[:].unsqueeze(2).broadcast_to([T, TPC, E, E])
                nc.vector.tensor_tensor(gt[:].rearrange("p (q e) j -> p q e j", q=TPC), pj, pe_, ALU.is_gt)
                link(nc.vector.tensor_tensor(eq[:].rearrange("p (q e) j -> p q e j", q=TPC), pj, pe_, ALU.is_equal))
                link(nc.vector.tensor_tensor(eq[:].rearrange("p (q e) j -> p q (e j)", q=TPC),
                                             eq[:].rearrange("p (q e) j -> p q (e j)", q=TPC),
                                             tri[:].rearrange("p e j -> p (e j)").unsqueeze(1).broadcast_to(
                                                 [T, TPC, E * E]), ALU.mult))
                link(nc.vector.tensor_tensor(gt[:], gt[:], eq[:], ALU.add))
                link(nc.vector.tensor_reduce(lg[:].rearrange("p q e -> p (q e)"), gt[:], AX.X, ALU.add))
                link(nc.vector.scalar_tensor_tensor(ex[:], lg[:], 2.0, ex[:], ALU.is_lt, ALU.mult))
                link(nc.vector.tensor_reduce(small[:, :, 0], ex[:], AX.X, ALU.add))
                link(nc.vector.tensor_scalar(small[:], small[:], 1e-8, None, ALU.add))
                link(nc.vector.reciprocal(small[:], small[:]))
                nc.vector.tensor_tensor(gates[:], ex[:], small[:].broadcast_to([T, TPC, E]),
                                        ALU.mult).then_inc(S["gates_out"], 1)
                dve.wait_ge(S["gates_out"], g + 1)

            def combine(g, e, pair):
                if e >= 1:
                    dve.wait_ge(S["acc_out"], 2 * (g * E + e) + pair)
                dve.wait_ge(S["up_mm"], 2 * (g * E + e) + 1 + pair)
                for i in range(2):
                    q = 2 * pair + i
                    src = xn[:, q, 0:D] if e <= 2 else acc[:, q, :]
                    dst = xn[:, q, 0:D] if e < 2 else acc[:, q, :]
                    st = nc.vector.scalar_tensor_tensor(dst, py[:, pair, i * D:(i + 1) * D],
                                                        gates[:, q, e:e + 1], src, ALU.mult, ALU.add)
                st.then_inc(S["acc_out"], 1)

            def stat(g):
                dve.wait_ge(S["acc_out"], 2 * E * (g + 1))
                for q in range(TPC):
                    bs = nc.vector.bn_stats(bn[:, q, :], acc[:, q, :])
                bs.then_inc(S["stat_out"], 1)

            def aggregate(g):
                for q in range(TPC):
                    ag = nc.vector.bn_aggr(agg[:, q, :], bn[:, q, :])
                ag.then_inc(S["agg_out"], 1)

            def norm_out(g):
                dve.wait_ge(S["rst_out"], g + 1)
                for q in range(TPC):
                    ts = nc.vector.tensor_scalar(yf[:, q, :], acc[:, q, :], agg[:, q, 0:1], rst[:, q:q + 1],
                                                 ALU.subtract, ALU.mult)
                ts.then_inc(S["nrm_out"], 1)

            def add_out(g):
                dve.wait_ge(S["yf_out"], g + 1)
                hs = h[:, bass.ds(g * TPC, TPC), :]
                nc.vector.tensor_tensor(hs, hs, yf[:], ALU.add).then_inc(S["h_out"], 1)

            def take_stats(g):
                for q in range(TPC):
                    nc.vector.bn_stats(bns[:, g * TPC + q, :], h[:, g * TPC + q, :])

            def chunk(g, first=False, last=False):
                top2(g, first)
                combine(g, 0, 0)
                combine(g, 0, 1)
                if not first:
                    stat(g - 1)
                    dve.wait_ge(S["stat_out"], g)
                combine(g, 1, 0)
                if not first:
                    aggregate(g - 1)
                combine(g, 1, 1)
                if not first:
                    norm_out(g - 1)
                    dve.wait_ge(S["nrm_out"], g)
                combine(g, 2, 0)
                combine(g, 2, 1)
                if not last:
                    dve.wait_ge(S["acc_out"], 2 * g * E + 6)
                    normalise(g + 1)
                for e in (3, 4, 5):
                    combine(g, e, 0)
                    combine(g, e, 1)
                if not first:
                    add_out(g - 1)
                    dve.wait_ge(S["h_out"], g)
                combine(g, 6, 0)
                if not last:
                    take_low(g + 1)
                combine(g, 6, 1)
                if not first:
                    take_stats(g - 1)
                if not last:
                    softmax_head(g + 1)
                combine(g, 7, 0)
                combine(g, 7, 1)

            dve.wait_ge(S["w_in"], 16 * NW)
            pieces = [(downh[:, half].rearrange("p e d -> p (e d)"), downl[:, half].rearrange("p e d -> p (e d)"),
                       stage[:, half, :]) for half in range(2)]
            pieces += [(uph[:, half * E // 2:(half + 1) * E // 2].rearrange("p e m d -> p (e m d)"),
                        upl[:, half * E // 2:(half + 1) * E // 2].rearrange("p e m d -> p (e m d)"),
                        stage[:, half, 0:UPH]) for half in range(2)]
            pieces += [(w1h[:], w1l[:], w1s[:])]
            for n, (high, low, src) in enumerate(pieces):
                if n < 4:
                    dve.wait_ge(S["stage_in"], 32 if n < 2 else 64)
                nc.vector.tensor_copy(high, src).then_inc(S["split"], 1)
                dve.wait_ge(S["split"], 2 * n + 1)
                nc.vector.tensor_tensor(low, src, high.bitcast(F32), ALU.subtract).then_inc(S["split"], 1)
            dve.wait_ge(S["split"], 10)
            normalise(0)
            take_low(0)
            softmax_head(0, first=True)
            chunk(0, first=True)
            with dve.Fori(1, NC - 1) as g:
                chunk(g)
            chunk(NC - 1, last=True)
            stat(NC - 1)
            dve.wait_ge(S["stat_out"], NC)
            aggregate(NC - 1)
            norm_out(NC - 1)
            add_out(NC - 1)
            dve.wait_ge(S["h_out"], NC)
            take_stats(NC - 1)


def linear_attention_phase(nc, ins, h, bns, mean, rstd, eye):
    with ExitStack() as ctx:
        sb, ps, sem = allocator(nc, ctx)
        wT = sb("wT4", [KC, 2, 3 * D])
        wq = sb("wq4", [KC, 2, D])
        wpT = sb("wpT4", [KC, 2, D])
        heads = sb("heads4", [KC, KC])
        xn = [sb(f"xn4_{i}", [T, TPC, D]) for i in range(2)]
        xT = sb("xT4", [KC + 1, 2, TOK])
        junk = sb("junk4", [KC, CH])
        sums = sb("sums4", [KC, 4, CPI])
        nrm = sb("nrm4", [KC, 4])
        scale = sb("scale4", [KC, 2])
        gsb = sb("gsb4", [KC, 2, D])
        t2 = sb("t2_4", [KC, 2, D])
        kvT = sb("kvT4", [KC, 2, D])
        m1 = sb("m1_4", [KC, 2, D])
        wimg = sb("wimg4", [KC + 1, 2, D])
        ptr = ps("ptr4", [KC, 2, 512])
        pqk = [ps(f"pqk4_{i}", [KC, 512]) for i in range(2)]
        pg = [ps(f"pg4_{i}", [KC, 512]) for i in range(2)]
        po = ps("po4", [T, 2, 512])
        names = ("w_in", "w_ready", "xn_ready", "xtr_mm", "xT_out", "qk_mm", "k_sum", "q_sum", "g_mm", "g_out",
                 "t2_mm", "t2_out", "kv_mm", "kv_out", "m1_mm", "m1_out", "wi_mm", "wi_out", "o_mm", "h_out", "dvec")
        S = {n: sem(f"{n}_4") for n in names}
        block = ctx.enter_context(nc.Block())
        NW = 5

        @block.sync
        def _(sp):
            for dst, name in ((wT[:], "wT4"), (wq[:], "wq4"), (wpT[:], "wpT4"), (heads[:], "heads"),
                              (wimg[KC:KC + 1, 0, :], "bproj4")):
                sp.dma_start(dst, ins[name]).then_inc(S["w_in"], 16)

        @block.gpsimd
        def _(pool):
            nc.gpsimd.memset(xT[KC:KC + 1], 1.0).then_inc(S["w_ready"], 1)

        @block.tensor
        def _(pe):
            pe.wait_ge(S["w_in"], 16 * NW)
            pe.wait_ge(S["w_ready"], 1)
            pe.sem_inc(S["o_mm"], 1)

            def gather(b, c):
                g = b * CPI + c
                pe.wait_ge(S["xn_ready"], g + 1)
                for q in range(TPC):
                    for i in range(2):
                        mm = pe.transpose(ptr[:, i, q * T:(q + 1) * T], xn[c % 2][:, q, i * KC:(i + 1) * KC],
                                          eye[0:T, 0:T])
                mm.then_inc(S["xtr_mm"], 1)
                for q in range(TPC):
                    for i in range(2):
                        mm = pe.matmul(pg[i][:, 0:D], xn[c % 2][:, q, i * KC:(i + 1) * KC], xn[c % 2][:, q, :],
                                       start=(c == 0 and q == 0), stop=(c == CPI - 1 and q == TPC - 1),
                                       skip_group_check=True)
                mm.then_inc(S["g_mm"], 1)
                pe.wait_ge(S["xT_out"], g + 1)
                for m in range(4):
                    if m == 0:
                        pe.wait_ge(S["q_sum"], 2 * g + 1)
                    elif m == 1:
                        pe.wait_ge(S["k_sum"], 2 * g + 1)
                    elif m == 2:
                        pe.wait_ge(S["q_sum"], 2 * g + 2)
                    else:
                        pe.wait_ge(S["k_sum"], 2 * g + 2)
                    piece = (0, 2, 1, 3)[m]
                    for i in range(2):
                        mm = pe.matmul(pqk[m % 2][:, 0:CH], wT[:, i, piece * KC:(piece + 1) * KC],
                                       xT[0:KC, i, c * CH:(c + 1) * CH], start=(i == 0), stop=(i == 1))
                    mm.then_inc(S["qk_mm"], 1)

            def square(dst, lhs, rhs):
                for i in range(2):
                    for c in range(2):
                        mm = pe.matmul(dst[i][:, 0:D], lhs(c, i), rhs(c), start=(c == 0), stop=(c == 1))
                return mm

            def image(b):
                for c in range(CPI):
                    gather(b, c)
                pe.wait_ge(S["g_out"], b + 1)
                pe.wait_ge(S["k_sum"], 2 * CPI * (b + 1) + 1)
                pe.wait_ge(S["q_sum"], 2 * CPI * (b + 1) + 1)
                square(pqk, lambda c, i: gsb[:, c, i * KC:(i + 1) * KC],
                       lambda c: wT[:, c, D:2 * D]).then_inc(S["t2_mm"], 1)
                pe.wait_ge(S["t2_out"], b + 1)
                square(pg, lambda c, i: wT[:, c, 2 * D + i * KC:2 * D + (i + 1) * KC],
                       lambda c: t2[:, c, :]).then_inc(S["kv_mm"], 1)
                pe.wait_ge(S["kv_out"], b + 1)
                square(pqk, lambda c, i: kvT[:, c, i * KC:(i + 1) * KC],
                       lambda c: wpT[:, c, :]).then_inc(S["m1_mm"], 1)
                pe.wait_ge(S["m1_out"], b + 1)
                square(pg, lambda c, i: wq[:, c, i * KC:(i + 1) * KC],
                       lambda c: m1[:, c, :]).then_inc(S["wi_mm"], 1)
                pe.wait_ge(S["wi_out"], b + 1)
                for t in range(TPI):
                    if t % 2 == 0:
                        pe.wait_ge(S["h_out"], TPI // 2 * b + t // 2 + 1)
                    for i in range(2):
                        k = KC + 1 if i == 0 else KC
                        mm = pe.matmul(po[:, (t // 2) % 2, (t % 2) * D:(t % 2 + 1) * D], xT[0:k, i, t * T:(t + 1) * T],
                                       wimg[0:k, i, :], start=(i == 0), stop=(i == 1), skip_group_check=True)
                    if t % 2 == 1:
                        mm.then_inc(S["o_mm"], 1)

            with pe.Fori(0, B) as b:
                image(b)

        @block.scalar
        def _(act):
            act.wait_ge(S["w_in"], 16 * NW)
            nc.scalar.preload_act_table(ACT.Abs)
            act.sem_inc(S["q_sum"], 1)

            def image(b):
                for c in range(CPI):
                    g = b * CPI + c
                    act.wait_ge(S["xtr_mm"], g + 1)
                    if c == 0:
                        act.wait_ge(S["o_mm"], TPI // 2 * b + 1)
                    nc.scalar.copy(xT[0:KC, :, c * CH:(c + 1) * CH], ptr[:, :, 0:CH]).then_inc(S["xT_out"], 1)
                    for m in range(2):
                        act.wait_ge(S["qk_mm"], 4 * g + 2 * m + 1)
                        nc.scalar.activation(junk[:], pqk[0][:, 0:CH], ACT.Abs,
                                             accum_out=sums[:, m, c:c + 1]).then_inc(S["q_sum"], 1)
                act.wait_ge(S["g_mm"], CPI * (b + 1))
                for i in range(2):
                    cp = nc.scalar.copy(gsb[:, i, :], pg[i][:, 0:D])
                cp.then_inc(S["g_out"], 1)

            with act.Fori(0, B) as b:
                image(b)

        @block.vector
        def _(dve):
            dve.wait_ge(S["w_in"], 16 * NW)
            dve.sem_inc(S["k_sum"], 1)
            dve.sem_inc(S["h_out"], 2)

            def normalise(b, c):
                g = b * CPI + c
                if c >= 2:
                    dve.wait_ge(S["g_mm"], g - 1)
                for q in range(TPC):
                    t = g * TPC + q
                    ts = nc.vector.tensor_scalar(xn[c % 2][:, q, :], h[:, t, :],
                                                 mean[:, bass.ds(t, 1)], rstd[:, bass.ds(t, 1)],
                                                 ALU.subtract, ALU.mult)
                ts.then_inc(S["xn_ready"], 1)

            def image(b):
                normalise(b, 0)
                for c in range(CPI):
                    g = b * CPI + c
                    if c + 1 < CPI:
                        normalise(b, c + 1)
                    for m in range(2):
                        dve.wait_ge(S["qk_mm"], 4 * g + 2 * m + 2)
                        nc.vector.tensor_reduce(sums[:, 2 + m, c:c + 1], pqk[1][:, 0:CH], AX.X, ALU.add,
                                                apply_absolute_value=True).then_inc(S["k_sum"], 1)
                dve.wait_ge(S["k_sum"], 2 * CPI * (b + 1) + 1)
                dve.wait_ge(S["q_sum"], 2 * CPI * (b + 1) + 1)
                step = [4 * b]

                def link(ins):
                    step[0] = step[0] + 1
                    ins.then_inc(S["dvec"], 1)
                    dve.wait_ge(S["dvec"], step[0])

                link(nc.vector.tensor_reduce(nrm[:], sums[:], AX.X, ALU.add))
                link(nc.vector.tensor_scalar(nrm[:], nrm[:], 1e-12, None, ALU.max))
                link(nc.vector.reciprocal(nrm[:], nrm[:]))
                link(nc.vector.tensor_tensor(scale[:], nrm[:, 0:2], nrm[:, 2:4], ALU.mult))
                dve.wait_ge(S["t2_mm"], b + 1)
                for i in range(2):
                    cp = nc.vector.tensor_copy(t2[:, i, :], pqk[i][:, 0:D])
                cp.then_inc(S["t2_out"], 1)
                dve.wait_ge(S["kv_mm"], b + 1)
                for i in range(2):
                    nc.vector.tensor_tensor(kvT[:, i, i * KC:(i + 1) * KC], pg[i][:, i * KC:(i + 1) * KC], heads[:],
                                            ALU.mult)
                    ms = nc.vector.memset(kvT[:, i, (1 - i) * KC:(2 - i) * KC], 0.0)
                ms.then_inc(S["kv_out"], 1)
                dve.wait_ge(S["m1_mm"], b + 1)
                for i in range(2):
                    ts = nc.vector.tensor_scalar(m1[:, i, :], pqk[i][:, 0:D], scale[:, i:i + 1], None, ALU.mult)
                ts.then_inc(S["m1_out"], 1)
                dve.wait_ge(S["wi_mm"], b + 1)
                for i in range(2):
                    cp = nc.vector.tensor_copy(wimg[0:KC, i, :], pg[i][:, 0:D])
                cp.then_inc(S["wi_out"], 1)
                for p in range(TPI // 2):
                    n = TPI // 2 * b + p
                    t = b * TPI + 2 * p
                    dve.wait_ge(S["o_mm"], n + 2)
                    if p >= 1:
                        dve.wait_ge(S["h_out"], n + 2)
                    two = h[:, bass.ds(t, 2), :]
                    nc.vector.tensor_tensor(two, two, po[:, p % 2, 0:2 * D].rearrange("p (q d) -> p q d", q=2),
                                            ALU.add).then_inc(S["h_out"], 1)
                    if p >= 1:
                        stats_of(t - 2)
                dve.wait_ge(S["h_out"], TPI // 2 * (b + 1) + 2)
                nc.vector.tensor_copy(scale[:], nrm[:, 0:2])
                stats_of(b * TPI + TPI - 2)

            def stats_of(t):
                for q in range(2):
                    nc.vector.bn_stats(bns[:, t + q, :],
                                       h[:, t + q, :])

            with dve.Fori(0, B) as b:
                image(b)


def bit_ffn_phase(nc, ins, h, bns, mean, rstd, var, eye, out):
    HID = 512
    MAGIC = 12582912.0
    with ExitStack() as ctx:
        sb, ps, sem = allocator(nc, ctx)
        win = sb("win5", [KC, 2, 2 * HID])
        wout = sb("wout5", [128, 4, D])
        winq = sb("winq5", [KC, 2, 2 * HID], BF16)
        woutq = sb("woutq5", [128, 4, D], BF16)
        gin = sb("gin5", [T, D])
        gout = sb("gout5", [T, HID])
        ones = sb("ones5", [128, 128])
        eyeb = sb("eyeb5", [128, 128], BF16)
        wsum = sb("wsum5", [128, 4])
        wsc = sb("wsc5", [128, 4])
        mhalf = sb("mhalf5", [T, NT])
        fac = sb("fac5", [T, NT])
        tmp = sb("tmp5", [T, NT])
        xg = sb("xg5", [T, TPC, D])
        xr = sb("xr5", [T, TPC, D])
        xq = sb("xq5", [T, TPC, D], BF16)
        xT = sb("xT5", [KC, 2, CH], BF16)
        am = sb("am5", [T, TPC])
        sx = sb("sx5", [T, TPC])
        dx = sb("dx5", [T, TPC])
        sg = [sb(f"sg5_{i}", [T, HID]) for i in range(2)]
        junk = sb("junk5", [T, HID])
        y = sb("y5", [T, TPC, HID])
        yg = sb("yg5", [T, TPC, HID])
        yr = sb("yr5", [T, TPC, HID])
        yq = sb("yq5", [T, TPC, HID], BF16)
        yT = sb("yT5", [128, 4, CH], BF16)
        ssq = sb("ssq5", [T, TPC])
        am2 = sb("am2_5", [T, TPC])
        ms2 = sb("ms2_5", [T, TPC])
        r2 = sb("r2_5", [T, TPC])
        s2 = sb("s2_5", [T, TPC])
        d2 = sb("d2_5", [T, TPC])
        ho = sb("ho5", [T, TPC, D])
        pxt = ps("pxt5", [KC, 2, CH], BF16)
        pyt = ps("pyt5", [128, 2, 1024], BF16)
        pup = [ps(f"pup5_{i}", [128, 512]) for i in range(2)]
        pga = [ps(f"pga5_{i}", [128, 512]) for i in range(2)]
        po = ps("po5", [T, 512])
        names = ("w_in", "w_ready", "wc", "wsum_mm", "xq_out", "xtr_mm", "xT_out", "in_mm", "sg_out", "y_out", "yg_out",
                 "ssq_out", "r2_in", "r2_out", "yq_out", "ytr_mm", "yT_out", "o_mm", "o_out", "stored", "dvec",
                 "dvec2", "fac_in", "fac_out", "poolc", "d2_out", "dx_out", "xr_out", "yr_out")
        S = {n: sem(f"{n}_5") for n in names}
        block = ctx.enter_context(nc.Block())
        NW = 4
        out_t = out.rearrange("b (t p) d -> p (b t) d", p=T)

        @block.sync
        def _(sp):
            for dst, name in ((win[:], "win5"), (wout[:], "wout5"), (gin[:], "gin5"), (gout[:], "gout5")):
                sp.dma_start(dst, ins[name]).then_inc(S["w_in"], 16)

            def store(g):
                sp.wait_ge(S["o_out"], 2 * g + 2)
                sp.dma_start(out_t[:, bass.ds(g * TPC, TPC), :], ho[:]).then_inc(S["stored"], 16)

            with sp.Fori(0, NC) as g:
                store(g)
            sp.wait_ge(S["stored"], 16 * NC)

        @block.gpsimd
        def _(pool):
            nc.gpsimd.memset(ones[:], 1.0).then_inc(S["w_ready"], 1)
            pool.wait_ge(S["w_ready"], 1)
            nc.gpsimd.memset(mhalf[:], -0.5).then_inc(S["w_ready"], 1)
            pool.wait_ge(S["w_ready"], 2)
            pool.wait_ge(S["fac_in"], 1)
            nc.gpsimd.tensor_tensor(fac[:], tmp[:], mhalf[:], ALU.pow).then_inc(S["fac_out"], 1)
            pool.wait_ge(S["w_in"], 16 * NW)
            pool.wait_ge(S["fac_out"], 1)

            def chunk(g, first=False):
                for q in range(TPC):
                    if q == 0 and not first:
                        pool.wait_ge(S["r2_out"], g)
                        pool.wait_ge(S["yr_out"], g)
                    elif q:
                        pool.wait_ge(S["yg_out"], g * TPC + q)
                    pool.wait_ge(S["y_out"], g * TPC + q + 1)
                    nc.gpsimd.tensor_tensor(yg[:, q, :], y[:, q, :], gout[:], ALU.mult).then_inc(S["yg_out"], 1)
                pool.wait_ge(S["yg_out"], (g + 1) * TPC)
                pool.wait_ge(S["r2_in"], g + 1)
                nc.gpsimd.tensor_tensor(r2[:], ms2[:], mhalf[:, 0:TPC], ALU.pow).then_inc(S["r2_out"], 1)

            chunk(0, first=True)
            with pool.Fori(1, NC) as g:
                chunk(g)

        @block.tensor
        def _(pe):
            pe.wait_ge(S["w_ready"], 2)
            pe.wait_ge(S["wc"], 1)
            pe.matmul(pup[0][:, 0:1], ones[:], wsum[:, 1:2], start=True, stop=True)
            pe.matmul(pga[0][:, 0:1], ones[:], wsum[:, 0:1], start=True, stop=True).then_inc(
                S["wsum_mm"], 1)
            pe.wait_ge(S["w_ready"], 2 + 3)

            def transpose_in(g):
                pe.wait_ge(S["xq_out"], g + 1)
                for q in range(TPC):
                    for c in range(2):
                        mm = pe.transpose(pxt[:, c, q * T:(q + 1) * T], xq[:, q, c * KC:(c + 1) * KC], eyeb[0:T, 0:T])
                mm.then_inc(S["xtr_mm"], 1)

            def into(g, q, first=False):
                if not first:
                    pe.wait_ge(S["y_out"], g * TPC + q - 1)
                for dst, o in ((pga, HID), (pup, 0)):
                    for c in range(2):
                        mm = pe.matmul(dst[q % 2][0:T], xT[:, c, q * T:(q + 1) * T], winq[:, c, o:o + HID],
                                       start=(c == 0), stop=(c == 1))
                mm.then_inc(S["in_mm"], 1)

            def transpose_y(g):
                pe.wait_ge(S["yq_out"], 2 * g + 2)
                for half in range(2):
                    for k in range(2):
                        for q in range(TPC):
                            mm = pe.transpose(pyt[:, half, k * CH + q * T:k * CH + (q + 1) * T],
                                              yq[:, q, (2 * half + k) * 128:(2 * half + k + 1) * 128], eyeb[0:T, 0:T])
                    mm.then_inc(S["ytr_mm"], 1)

            def enter(g, first=False):
                pe.wait_ge(S["xT_out"], g + 1)
                into(g, 0, first)
                into(g, 1, first)

            def outof(g, pair):
                if pair or not isinstance(g, int) or g > 0:
                    pe.wait_ge(S["o_out"], 2 * g + pair)
                pe.wait_ge(S["yT_out"], 2 * g + 2)
                for i in range(2):
                    q = 2 * pair + i
                    for k in range(4):
                        mm = pe.matmul(po[:, i * D:(i + 1) * D], yT[:, k, q * T:(q + 1) * T], woutq[:, k, :],
                                       start=(k == 0), stop=(k == 3), skip_group_check=True)
                mm.then_inc(S["o_mm"], 1)

            def step(g, first=False, last=False):
                into(g, 2)
                into(g, 3)
                if not first:
                    transpose_y(g - 1)
                    outof(g - 1, 0)
                if not last:
                    transpose_in(g + 1)
                if not first:
                    outof(g - 1, 1)
                if not last:
                    enter(g + 1)

            transpose_in(0)
            enter(0, first=True)
            step(0, first=True)
            with pe.Fori(1, NC - 1) as g:
                step(g)
            step(NC - 1, last=True)
            transpose_y(NC - 1)
            outof(NC - 1, 0)
            outof(NC - 1, 1)

        @block.scalar
        def _(act):
            nc.scalar.preload_act_table(ACT.Silu)
            act.wait_ge(S["w_ready"], 2 + 3)

            def take_x(g):
                act.wait_ge(S["xtr_mm"], g + 1)
                nc.scalar.copy(xT[:, :, :], pxt[:, :, :]).then_inc(S["xT_out"], 1)

            def silu(g, q):
                act.wait_ge(S["in_mm"], g * TPC + q + 1)
                nc.scalar.activation(sg[q % 2][:], pga[q % 2][0:T], ACT.Silu, scale=dx[:, q:q + 1]).then_inc(
                    S["sg_out"], 1)

            def squares(g, q, first=False):
                if q or not first:
                    act.wait_ge(S["ssq_out"], g * TPC + q)
                if q == 0 and not first:
                    act.wait_ge(S["r2_in"], g)
                act.wait_ge(S["y_out"], g * TPC + q + 1)
                nc.scalar.activation(junk[:], y[:, q, :], ACT.Square, accum_out=ssq[:, q:q + 1]).then_inc(
                    S["ssq_out"], 1)

            def whole_y(g, pair):
                act.wait_ge(S["yr_out"], g + 1)
                nc.scalar.activation(yq[:, 2 * pair:2 * pair + 2, :], yr[:, 2 * pair:2 * pair + 2, :],
                                     ACT.Copy, bias=-MAGIC).then_inc(S["yq_out"], 1)

            def take_y(g):
                for half in range(2):
                    act.wait_ge(S["ytr_mm"], 2 * g + half + 1)
                    nc.scalar.copy(yT[:, 2 * half:2 * half + 2, :],
                                   pyt[:, half, 0:2 * CH].rearrange("p (k c) -> p k c", k=2)).then_inc(S["yT_out"], 1)

            def step(g, first=False, last=False):
                if not first:
                    whole_y(g - 1, 0)
                silu(g, 2)
                if not first:
                    whole_y(g - 1, 1)
                silu(g, 3)
                for q in (0, 1):
                    squares(g, q, first)
                if not first:
                    take_y(g - 1)
                for q in (2, 3):
                    squares(g, q)
                if not last:
                    take_x(g + 1)
                    silu(g + 1, 0)
                    silu(g + 1, 1)

            take_x(0)
            silu(0, 0)
            silu(0, 1)
            step(0, first=True)
            with act.Fori(1, NC - 1) as g:
                step(g)
            step(NC - 1, last=True)
            whole_y(NC - 1, 0)
            whole_y(NC - 1, 1)
            take_y(NC - 1)

        @block.vector
        def _(dve):
            step = [0]

            def link(ins):
                step[0] = step[0] + 1
                ins.then_inc(S["dvec"], 1)
                dve.wait_ge(S["dvec"], step[0])

            dve.wait_ge(S["w_in"], 16 * NW)
            link(nc.vector.memset(wsum[:], 0.0))
            link(nc.vector.tensor_reduce(wsum[0:KC, 0:1], win[:], AX.XY, ALU.add, apply_absolute_value=True))
            nc.vector.tensor_reduce(wsum[:, 1:2], wout[:], AX.XY, ALU.add, apply_absolute_value=True).then_inc(S["wc"], 1)
            link(nc.vector.tensor_copy(eyeb[:], eye[:]))
            dve.wait_ge(S["wsum_mm"], 1)
            nc.vector.tensor_scalar(wsc[:, 0:1], pga[0][:, 0:1], 1.0 / (2 * HID * D), 1e-5, ALU.mult, ALU.max)
            link(nc.vector.tensor_scalar(wsc[:, 1:2], pup[0][:, 0:1], 1.0 / (HID * D), 1e-5, ALU.mult, ALU.max))
            link(nc.vector.reciprocal(wsc[:, 2:4], wsc[:, 0:2]))
            link(nc.vector.tensor_scalar(win[:], win[:], wsc[0:KC, 2:3], MAGIC, ALU.mult, ALU.add))
            link(nc.vector.tensor_scalar(win[:], win[:], MAGIC, 1.0, ALU.subtract, ALU.min))
            nc.vector.tensor_scalar(winq[:], win[:], -1.0, None, ALU.max).then_inc(S["w_ready"], 1)
            link(nc.vector.tensor_scalar(wout[:], wout[:], wsc[:, 3:4], MAGIC, ALU.mult, ALU.add))
            link(nc.vector.tensor_scalar(wout[:], wout[:], MAGIC, 1.0, ALU.subtract, ALU.min))
            nc.vector.tensor_scalar(woutq[:], wout[:], -1.0, None, ALU.max).then_inc(S["w_ready"], 1)
            link(nc.vector.tensor_tensor(tmp[:], var[:], rstd[:], ALU.mult))
            link(nc.vector.tensor_tensor(tmp[:], tmp[:], rstd[:], ALU.mult))
            link(nc.vector.tensor_scalar(tmp[:], tmp[:], 1e-6, None, ALU.add))
            dve.sem_inc(S["fac_in"], 1)
            dve.wait_ge(S["fac_out"], 1)
            nc.vector.tensor_tensor(fac[:], fac[:], rstd[:], ALU.mult).then_inc(S["w_ready"], 1)
            dve.wait_ge(S["w_ready"], 5)

            L1, L2 = 6, 5

            def quant_in(g):
                st = [g * L1]

                def link(ins):
                    st[0] = st[0] + 1
                    ins.then_inc(S["poolc"], 1)
                    dve.wait_ge(S["poolc"], st[0])

                for q in range(TPC):
                    t = g * TPC + q
                    ins_ = nc.vector.scalar_tensor_tensor(xg[:, q, :], h[:, t, :], mean[:, bass.ds(t, 1)], gin[:],
                                                          ALU.subtract, ALU.mult)
                link(ins_)
                link(nc.vector.tensor_reduce(am[:], xg[:], AX.X, ALU.max, apply_absolute_value=True))
                link(nc.vector.tensor_tensor(am[:], am[:], fac[:, bass.ds(g * TPC, TPC)], ALU.mult))
                link(nc.vector.tensor_scalar(am[:], am[:], 1e-5, 1.0 / 127, ALU.max, ALU.mult))
                nc.vector.tensor_scalar(dx[:], am[:], wsc[0:T, 0:1], None, ALU.mult).then_inc(S["dx_out"], 1)
                link(nc.vector.reciprocal(sx[:], am[:]))
                link(nc.vector.tensor_tensor(sx[:], sx[:], fac[:, bass.ds(g * TPC, TPC)], ALU.mult))
                for q in range(TPC):
                    ins_ = nc.vector.tensor_scalar(xr[:, q, :], xg[:, q, :], sx[:, q:q + 1], MAGIC, ALU.mult, ALU.add)
                ins_.then_inc(S["xr_out"], 1)
                dve.wait_ge(S["xr_out"], g + 1)
                nc.vector.tensor_scalar(xq[:], xr[:], MAGIC, None, ALU.subtract).then_inc(S["xq_out"], 1)

            def gated(g, q, first=False):
                if not first:
                    dve.wait_ge(S["yg_out"], (g - 1) * TPC + q + 1)
                dve.wait_ge(S["sg_out"], g * TPC + q + 1)
                nc.vector.scalar_tensor_tensor(y[:, q, :], pup[q % 2][0:T], dx[:, q:q + 1], sg[q % 2][:],
                                               ALU.mult, ALU.mult).then_inc(S["y_out"], 1)

            def mean_square(g):
                dve.wait_ge(S["ssq_out"], (g + 1) * TPC)
                nc.vector.tensor_scalar(ms2[:], ssq[:], 1.0 / HID, 1e-6, ALU.mult, ALU.add).then_inc(S["r2_in"], 1)

            def quant_y(g, first=False):
                st = [g * L2]

                def link(ins):
                    st[0] = st[0] + 1
                    ins.then_inc(S["dvec2"], 1)
                    dve.wait_ge(S["dvec2"], st[0])

                dve.wait_ge(S["yg_out"], (g + 1) * TPC)
                nc.vector.tensor_reduce(am2[:], yg[:], AX.X, ALU.max, apply_absolute_value=True)
                if not first:
                    result(g - 1, 1)
                dve.wait_ge(S["r2_out"], g + 1)
                dve.wait_ge(S["r2_in"], g + 1)
                link(nc.vector.tensor_copy(s2[:], r2[:]))
                link(nc.vector.tensor_tensor(am2[:], am2[:], r2[:], ALU.mult))
                if not first:
                    dve.wait_ge(S["o_out"], 2 * g)
                link(nc.vector.tensor_scalar(am2[:], am2[:], 1e-5, 1.0 / 127, ALU.max, ALU.mult))
                link(nc.vector.reciprocal(s2[:], am2[:]))
                nc.vector.tensor_scalar(d2[:], am2[:], wsc[0:T, 1:2], None, ALU.mult).then_inc(S["d2_out"], 1)
                link(nc.vector.tensor_tensor(s2[:], s2[:], r2[:], ALU.mult))
                if not first:
                    dve.wait_ge(S["yq_out"], 2 * g)
                for q in range(TPC):
                    ins_ = nc.vector.tensor_scalar(yr[:, q, :], yg[:, q, :], s2[:, q:q + 1], MAGIC, ALU.mult, ALU.add)
                ins_.then_inc(S["yr_out"], 1)

            def result(g, pair):
                if pair == 0 and (not isinstance(g, int) or g > 0):
                    dve.wait_ge(S["stored"], 16 * g)
                dve.wait_ge(S["d2_out"], g + 1)
                dve.wait_ge(S["o_mm"], 2 * g + pair + 1)
                for i in range(2):
                    q = 2 * pair + i
                    st = nc.vector.scalar_tensor_tensor(ho[:, q, :], po[:, i * D:(i + 1) * D], d2[:, q:q + 1],
                                                        h[:, g * TPC + q, :], ALU.mult, ALU.add)
                st.then_inc(S["o_out"], 1)

            def step(g, first=False, last=False):
                for q in range(TPC):
                    gated(g, q, first)
                if not last:
                    quant_in(g + 1)
                mean_square(g)
                if not first:
                    result(g - 1, 0)
                quant_y(g, first)

            quant_in(0)
            step(0, first=True)
            with dve.Fori(1, NC - 1) as g:
                step(g)
            step(NC - 1, last=True)
            result(NC - 1, 0)
            result(NC - 1, 1)


def vit_tower(nc, ins, out):
    with ExitStack() as ctx:
        sb, ps, sem = allocator(nc, ctx)
        h = sb("h", [T, NT, D])
        bns = sb("bns", [T, NT, 6])
        eye = sb("eye", [128, 128])
        mean = sb("mean", [T, NT])
        rstd = sb("rstd", [T, NT])
        var = sb("var", [T, NT])
        mixer_phase(nc, ins, h, bns, eye)
        finish_stats(nc, "ln1", bns, mean, rstd, var, 1e-5)
        retention_phase(nc, ins, h, bns, mean, rstd, eye)
        finish_stats(nc, "ln2", bns, mean, rstd, var, 1e-5)
        expert_phase(nc, ins, h, bns, mean, rstd, eye)
        finish_stats(nc, "ln3", bns, mean, rstd, var, 1e-5)
        linear_attention_phase(nc, ins, h, bns, mean, rstd, eye)
        finish_stats(nc, "ln4", bns, mean, rstd, var, 1e-5)
        bit_ffn_phase(nc, ins, h, bns, mean, rstd, var, eye, out)


def kernel(**inputs):
    import numpy as np
    import concourse.bacc as bacc
    from concourse.bass_utils import run_bass_kernel_spmd as run

    f = {k: np.ascontiguousarray(v) for k, v in inputs.items()}
    lay = {}
    x = f["x"].reshape(B, 3, 56, 4, 56, 4).transpose(0, 1, 3, 5, 2, 4).reshape(B, 48, TOK)
    x1 = np.ones((B, X1, TOK), np.float32)
    x1[:, 0:48] = x
    lay["xT"] = x1
    keys = np.zeros((B, KT * 128, LO), np.float32)
    keys[:, 0:TOK, 0:X1] = x1.transpose(0, 2, 1)
    lay["xkey"] = keys.reshape(B, KT, 128, LO).transpose(0, 2, 1, 3)
    conv = np.zeros((D, X1), np.float32)
    conv[:, 0:48] = f["L0_tok_conv_w"].reshape(D, 48)
    conv[:, 48] = f["L0_tok_conv_b"]
    lay["conv"] = conv.reshape(2, KC, X1).transpose(1, 0, 2)
    w = np.stack([f["L0_tok_q_w"].T, f["L0_tok_k_w"].T, f["L0_tok_v_w"].T])
    lay["wqkv"] = w.reshape(3, 2, KC, 96).transpose(2, 0, 1, 3)
    lay["bqkv"] = np.stack([f["L0_tok_q_b"], f["L0_tok_k_b"], f["L0_tok_v_b"]])[None]
    projT = np.zeros((96, D + 1), np.float32)
    projT[:, 0:D] = f["L0_tok_proj_w"].T
    lay["projT"] = projT
    projb = np.ones((1, D + 1), np.float32)
    projb[0, 0:D] = f["L0_tok_proj_b"]
    lay["projb"] = projb
    e48 = np.zeros((1, 128), np.float32)
    e48[0, 48] = e48[0, LO + 48] = 1.0
    lay["e48"] = e48
    lay["eye"] = np.eye(128, dtype=np.float32)

    def pieces(w, n=2):
        return w.reshape(n, w.shape[0] // n, -1).transpose(1, 0, 2)

    lay["wqk"] = pieces(np.concatenate([f["L0_attn_Wq"], f["L0_attn_Wk"]], 1))
    lay["wff"] = pieces(np.concatenate([f["L0_attn_Wf"], f["L0_attn_Wf"]], 1))
    lay["bff"] = np.concatenate([f["L0_attn_bf"], f["L0_attn_bf"]])[:, None]
    lay["wv"] = pieces(f["L0_attn_Wv"])
    lay["wo2"] = pieces(f["L0_attn_Wo"])
    lay["gam2"] = f["L0_attn_gamma"].reshape(2, KC).T
    lay["bet2"] = f["L0_attn_beta"].reshape(2, KC).T
    lay["sgn"] = np.repeat(np.float32([1.0, -1.0]), 64)[:, None]
    lay["mask"] = np.triu(np.ones((T, T), np.float32))

    E = 8

    def parts(w):
        return np.stack([w[0:128], np.concatenate([w[128:D], w[128:D]], 0)], 1)

    lay["w1"] = parts(f["L0_ffn_w1"])
    lay["b1"] = f["L0_ffn_b1"][:, None]
    lay["w2"] = np.concatenate([f["L0_ffn_w2"], f["L0_ffn_b2"][None]], 0)
    lay["down"] = parts(f["L0_ffn_down_w"].transpose(1, 0, 2).reshape(D, E * 256)).reshape(128, 2, E, 256)
    lay["downb"] = f["L0_ffn_down_b"].reshape(E * 2, 128).T
    lay["up"] = f["L0_ffn_up_w"].reshape(E, 2, 128, D).transpose(2, 0, 1, 3)
    lay["gam3"] = np.broadcast_to(f["L0_ffn_gamma"], (T, D))
    lay["bet3"] = np.broadcast_to(f["L0_ffn_beta"], (T, D))
    lay["tri"] = np.broadcast_to(np.tril(np.ones((E, E), np.float32), -1), (T, E, E))
    lay["wT4"] = pieces(f["L1_attn_w_qkv"].T)
    lay["wq4"] = pieces(f["L1_attn_w_qkv"][0:D])
    lay["wpT4"] = pieces(f["L1_attn_w_proj"].T)
    lay["heads"] = np.kron(np.eye(6, dtype=np.float32), np.ones((16, 16), np.float32))
    lay["bproj4"] = f["L1_attn_b_proj"][None]
    lay["win5"] = pieces(f["L1_ffn_w_in"].T)
    lay["wout5"] = pieces(f["L1_ffn_w_out"].T, 4)
    lay["gin5"] = np.broadcast_to(f["L1_ffn_g_in"], (T, D))
    lay["gout5"] = np.broadcast_to(f["L1_ffn_g_out"], (T, 512))

    nc = bacc.Bacc("TRN2", target_bir_lowering=False, num_devices=1)
    arrays, ins = {}, {}
    for name, a in lay.items():
        a = np.ascontiguousarray(a)
        arrays[f"in_{name}"] = a
        ins[name] = nc.dram_tensor(f"in_{name}", a.shape, mybir.dt.from_np(a.dtype), kind="ExternalInput").ap()
    out = nc.dram_tensor("out_0", (B, TOK, D), F32, kind="ExternalOutput").ap()
    vit_tower(nc, ins, out)
    r = run(nc, [arrays], core_ids=[0])
    return r.results[0]["out_0"]
```

```python
from contextlib import ExitStack

import concourse.bass as bass
from concourse import mybir

F32 = mybir.dt.float32
F32R = mybir.dt.float32r
BF16 = mybir.dt.bfloat16
ACT = mybir.ActivationFunctionType
ALU = mybir.AluOpType
AX = mybir.AxisListType

B = 4
TOK = 3136
D = 192
KC = 96
T = 112
TPI = TOK // T
NT = B * TPI
CH = 448
TPC = CH // T
CPI = TOK // CH
NC = B * CPI
X1 = 49
LO = 64
XS = LO + X1
KT = 25
KEYS = KT * 128
ZMIN = -13.815509557963773
SHIFT_SLOT = 11
PROJECT_SLOTS = (2, 4)
SLOTS = 13



def allocator(nc, ctx):
    def sb(name, shape, dt=F32):
        return ctx.enter_context(nc.sbuf_tensor(name, shape, dt))

    def ps(name, shape, dt=F32):
        return ctx.enter_context(nc.psum_tensor(name, shape, dt))

    def sem(name):
        return ctx.enter_context(nc.semaphore(name))
    return sb, ps, sem


def mixer_phase(nc, ins, h, bns, eye):
    with ExitStack() as ctx:
        sb, ps, sem = allocator(nc, ctx)
        conv = sb("conv", [KC, 2, X1])
        wqkv = sb("wqkv", [KC, 3, 2, 96])
        bqkv = sb("bqkv", [1, 3, 96])
        projT = sb("projT", [96, D + 1])
        projb = sb("projb", [1, D + 1])
        e48 = sb("e48", [1, 128])
        wT = sb("wT", [96, 3, 128])
        A2 = sb("A2", [X1, XS])
        W2 = sb("W2", [128, D + 1])
        eyer = sb("eyer", [T, T], F32R)
        x32 = [sb(f"x32_{i}", [XS, KEYS]) for i in range(2)]
        xhl = [sb(f"xhl_{i}", [XS, KEYS], F32R) for i in range(2)]
        xkey = [sb(f"xkey_{i}", [128, KT, LO]) for i in range(2)]
        y32 = sb("y32", [XS, CH])
        ysum = sb("ysum", [XS, CH])
        yh1 = sb("yh1", [XS, CH], F32R)
        yh = sb("yh", [XS, CH], F32R)
        yl = sb("yl", [XS, CH], F32R)
        pmax = sb("pmax", [T, TPC, CPI])
        negmax = sb("negmax", [T, TPC, XS], F32R)
        prob = [sb(f"prob{i}", [128, 2, CH]) for i in range(3)]
        oT = sb("oT", [128, CH])
        rden = sb("rden", [T, TPC, 1])

        pscore = [ps(f"pscore{i}", [128, 2, 512]) for i in range(2)]
        ppre = [ps(f"ppre{i}", [T, 512]) for i in range(2)]
        pout = ps("pout", [128, 512])
        pmisc = ps("pmisc", [128, 512])

        w_in = sem("w_in")
        x_in = [sem(f"x_in{i}") for i in range(2)]
        zeroed = sem("zeroed")
        x_split = sem("x_split")
        fold_mm = sem("fold_mm")
        folded = sem("folded")
        y_mm = sem("y_mm")
        y_out = sem("y_out")
        pre_mm = sem("pre_mm")
        pre_max = sem("pre_max")
        max_ready = sem("max_ready")
        shift_mm = sem("shift_mm")
        y_shifted = sem("y_shifted")
        scores = sem("scores")
        exped = sem("exped")
        pv = sem("pv")
        o_out = sem("o_out")
        proj_mm = sem("proj_mm")
        proj_out = sem("proj_out")
        dvec = sem("dvec")
        proj_rden = sem("proj_rden")
        stat_out = sem("stat_out")
        block = ctx.enter_context(nc.Block())

        @block.sync
        def _(sp):
            sp.dma_start(conv[:], ins["conv"]).then_inc(w_in, 16)
            sp.dma_start(wqkv[:], ins["wqkv"]).then_inc(w_in, 16)
            sp.dma_start(bqkv[:], ins["bqkv"]).then_inc(w_in, 16)
            sp.dma_start(projT[:], ins["projT"]).then_inc(w_in, 16)
            sp.dma_start(projb[:], ins["projb"]).then_inc(w_in, 16)
            sp.dma_start(e48[:], ins["e48"]).then_inc(w_in, 16)
            sp.dma_start(eye[:], ins["eye"]).then_inc(w_in, 16)
            for b in range(B):
                if b < 2:
                    sp.wait_ge(zeroed, b + 1)
                else:
                    sp.wait_ge(pv, SLOTS * CPI * (b - 1))
                sp.dma_start(x32[b % 2][0:X1, 0:TOK], ins["xT"][b]).then_inc(x_in[b % 2], 16)
                sp.dma_start(x32[b % 2][LO:XS, 0:TOK], ins["xT"][b]).then_inc(x_in[b % 2], 16)
                sp.dma_start(xkey[b % 2][:], ins["xkey"][b]).then_inc(x_in[b % 2], 16)

        @block.gpsimd
        def _(pool):
            nc.gpsimd.memset(x32[0][:], 0.0).then_inc(zeroed, 1)
            nc.gpsimd.memset(x32[1][:], 0.0).then_inc(zeroed, 1)
            nc.gpsimd.memset(negmax[:].bitcast(F32), 0.0).then_inc(zeroed, 1)
            nc.gpsimd.memset(wT[:], 0.0).then_inc(zeroed, 1)
            pool.wait_ge(zeroed, 4)
            for b in range(1, B):
                pool.wait_ge(x_in[b % 2], 48 * (b // 2 + 1))
                pool.wait_ge(x_split, 2 * b)
                if b >= 2:
                    pool.wait_ge(pv, SLOTS * CPI * (b - 1))
                nc.gpsimd.tensor_copy(xhl[b % 2][:], x32[b % 2][:]).then_inc(x_split, 1)
                pool.wait_ge(x_split, 2 * b + 1)
                nc.gpsimd.tensor_tensor(xhl[b % 2][LO:XS, :], x32[b % 2][LO:XS, :],
                                        xhl[b % 2][LO:XS, :].bitcast(F32), ALU.subtract).then_inc(x_split, 1)

        @block.scalar
        def _(act):
            def slots(g):
                for j in range(SLOTS):
                    act.wait_ge(scores, g * SLOTS + j + 1)
                    if j >= 3:
                        act.wait_ge(pv, g * SLOTS + j - 2)
                    elif j == 0 and not (isinstance(g, int) and g == 0):
                        act.wait_ge(pv, g * SLOTS)
                    if j < SLOTS - 1:
                        nc.scalar.activation(prob[j % 3][:, :, :], pscore[j % 2][:, :, 0:CH],
                                             ACT.Exp).then_inc(exped, 1)
                    else:
                        nc.scalar.activation(prob[j % 3][:, 0, :], pscore[j % 2][:, 0, 0:CH],
                                             ACT.Exp).then_inc(exped, 1)

            act.wait_ge(x_in[0], 48)
            nc.scalar.copy(xhl[0][:], x32[0][:]).then_inc(x_split, 1)
            nc.scalar.preload_act_table(ACT.Exp)
            slots(0)
            with act.Fori(1, NC) as g:
                slots(g)

        @block.tensor
        def _(pe):
            pe.wait_ge(w_in, 16 * 7)
            for i in range(3):
                for c in range(2):
                    pe.matmul(pmisc[0:96, i * 64:i * 64 + X1], wqkv[:, i, c, :], conv[:, c, :],
                              start=(c == 0), stop=False)
                pe.matmul(pmisc[0:96, i * 64:i * 64 + X1], bqkv[:, i, :], e48[:, 0:X1],
                          start=False, stop=True).then_inc(fold_mm, 1)
            pe.wait_ge(folded, 5)
            pe.matmul(ppre[0][0:X1, 0:XS], wT[:, 0, 0:X1], wT[:, 1, 0:XS], start=True, stop=True).then_inc(fold_mm, 1)
            pe.matmul(pout[:, 0:D + 1], wT[:, 2, :], projT[:], start=True, stop=False)
            pe.matmul(pout[:, 0:D + 1], e48[:], projb[:], start=False, stop=True).then_inc(fold_mm, 1)
            pe.wait_ge(folded, 8)

            def make_y(g, b, c):
                pe.matmul(pmisc[0:XS, 0:CH], A2[:], x32[b % 2][0:X1, bass.ds(c * CH, CH)],
                          start=True, stop=True).then_inc(y_mm, 1)

            def first_scores(g, b, k):
                q, kc = k // CPI, k % CPI
                pe.wait_ge(pre_max, g * TPC * CPI + k - 1) if k >= 2 else pe.wait_ge(pre_max, g * TPC * CPI)
                pe.matmul(ppre[k % 2][:, 0:CH], yh1[:, q * T:(q + 1) * T],
                          xhl[b % 2][:, kc * CH:(kc + 1) * CH], start=True, stop=True).then_inc(pre_mm, 1)

            def shift(g):
                pe.wait_ge(max_ready, (g + 1) * TPC)
                for q in range(TPC):
                    mm = pe.matmul(pmisc[0:XS, q * T:(q + 1) * T], negmax[:, q, :], eyer[:],
                                   start=True, stop=True)
                mm.then_inc(shift_mm, 1)

            def slot_scores(g, b, j, between=lambda: None):
                if j >= 2:
                    pe.wait_ge(exped, g * SLOTS + j - 1)
                elif j == 0:
                    pe.wait_ge(exped, g * SLOTS)
                if j == 0:
                    pe.wait_ge(y_shifted, 2 * g + 1)
                    for i in range(2):
                        pe.matmul(pscore[0][:, i, 0:CH], xhl[b % 2][:, i * 128:(i + 1) * 128], yh[:],
                                  start=True, stop=False)
                    pe.wait_ge(y_shifted, 2 * g + 2)
                    for i in range(2):
                        mm = pe.matmul(pscore[0][:, i, 0:CH], xhl[b % 2][:, i * 128:(i + 1) * 128], yl[:],
                                       start=False, stop=True)
                    mm.then_inc(scores, 1)
                    return
                for i in range(2 if j < SLOTS - 1 else 1):
                    k = 2 * j + i
                    out, keys = pscore[j % 2][:, i, 0:CH], xhl[b % 2][:, k * 128:(k + 1) * 128]
                    pe.matmul(out, keys, yh[:], start=True, stop=False)
                    mm = pe.matmul(out, keys, yl[:], start=False, stop=True)
                    if j == SLOTS - 1 or i == 1:
                        mm.then_inc(scores, 1)
                    between()

            def slot_pv(g, b, j):
                pe.wait_ge(exped, g * SLOTS + j + 1)
                if j == 0:
                    pe.wait_ge(o_out, g)
                if j < SLOTS - 1:
                    for i in range(2):
                        mm = pe.matmul(pout[i * LO:(i + 1) * LO, 0:CH], xkey[b % 2][:, 2 * j + i, :],
                                       prob[j % 3][:, i, :], start=(j == 0), stop=(i == 1 and j == SLOTS - 2),
                                       tile_position=(0, i * LO))
                else:
                    mm = pe.matmul(pout[0:LO, 0:CH], xkey[b % 2][:, 2 * j, :], prob[j % 3][:, 0, :],
                                   start=False, stop=True, tile_position=(0, 0))
                mm.then_inc(pv, 1)

            def project(g, r):
                for i in range(2):
                    q = 2 * r + i
                    mm = pe.matmul(pmisc[0:T, i * (D + 1):(i + 1) * (D + 1)], oT[:, q * T:(q + 1) * T], W2[:],
                                   start=True, stop=True, skip_group_check=True)
                mm.then_inc(proj_mm, 1)

            def chunk(g, b, nxt, first=False, last=False):
                todo = list(range(TPC * CPI)) if nxt is not None else []

                def first_pass():
                    if todo:
                        first_scores(g + 1, nxt[0], todo.pop(0))

                slot_scores(g, b, 0)
                for j in range(SLOTS):
                    if j == 1 and nxt is not None:
                        pe.wait_ge(y_out, 2 * (g + 2) - 1)
                    run = first_pass if 1 <= j < SHIFT_SLOT else lambda: None
                    if j < SLOTS - 1:
                        slot_scores(g, b, j + 1, run)
                    if j == 0 and nxt is not None:
                        if not first:
                            pe.wait_ge(y_shifted, 2 * g + 2)
                        if nxt[0] != b:
                            pe.wait_ge(x_split, 2 * (nxt[0] + 1))
                        make_y(g + 1, *nxt)
                    if j in PROJECT_SLOTS and not first:
                        if j == PROJECT_SLOTS[0]:
                            pe.wait_ge(o_out, g)
                            if nxt is not None:
                                pe.wait_ge(y_out, 2 * (g + 2))
                        else:
                            pe.wait_ge(proj_out, 4 * g - 2)
                        project(g - 1, PROJECT_SLOTS.index(j))
                    if j == SHIFT_SLOT and nxt is not None:
                        if not first:
                            pe.wait_ge(proj_out, 4 * g)
                        shift(g + 1)
                    slot_pv(g, b, j)
                    run()

            pe.wait_ge(x_split, 2)
            make_y(0, 0, 0)
            pe.wait_ge(y_out, 2)
            for k in range(TPC * CPI):
                first_scores(0, 0, k)
            shift(0)
            for b in range(B):
                chunk(b * CPI, b, (b, 1), first=(b == 0))
                with pe.Fori(1, CPI - 1) as c:
                    chunk(b * CPI + c, b, (b, c + 1))
                chunk(b * CPI + CPI - 1, b, (b + 1, 0) if b + 1 < B else None)
            pe.wait_ge(o_out, NC)
            project(NC - 1, 0)
            pe.wait_ge(proj_out, 4 * NC - 2)
            project(NC - 1, 1)

        @block.vector
        def _(dve):
            dve.wait_ge(w_in, 16 * 7)
            nc.vector.tensor_copy(eyer[:], eye[0:T, 0:T]).then_inc(folded, 1)
            dve.wait_ge(zeroed, 4)
            dve.wait_ge(fold_mm, 3)
            nc.vector.tensor_scalar(wT[:, 0, 0:X1], pmisc[0:96, 0:X1], 96 ** -0.5, None,
                                    ALU.mult).then_inc(folded, 1)
            nc.vector.tensor_copy(wT[:, 1:3, 0:X1],
                                  pmisc[0:96, 64:192].rearrange("p (i c) -> p i c", i=2)[:, :, 0:X1]).then_inc(folded, 1)
            nc.vector.tensor_copy(wT[:, 1, LO:XS], pmisc[0:96, 64:64 + X1]).then_inc(folded, 1)
            nc.vector.tensor_copy(wT[:, 2, LO:XS], pmisc[0:96, 128:128 + X1]).then_inc(folded, 1)
            dve.wait_ge(fold_mm, 5)
            nc.vector.tensor_copy(A2[:], ppre[0][0:X1, 0:XS]).then_inc(folded, 1)
            nc.vector.tensor_copy(W2[:], pout[:, 0:D + 1]).then_inc(folded, 1)
            nc.vector.memset(pmax[:], 0.0).then_inc(folded, 1)
            dve.wait_ge(x_split, 1)
            nc.vector.tensor_tensor(xhl[0][LO:XS, :], x32[0][LO:XS, :], xhl[0][LO:XS, :].bitcast(F32),
                                    ALU.subtract).then_inc(x_split, 1)

            def take_y(g):
                dve.wait_ge(y_mm, g + 1)
                nc.vector.tensor_copy(yh1[:], pmisc[0:XS, 0:CH]).then_inc(y_out, 1)
                nc.vector.tensor_copy(y32[:], pmisc[0:XS, 0:CH]).then_inc(y_out, 1)

            def take_max(g, k):
                q, kc = k // CPI, k % CPI
                dve.wait_ge(pre_mm, g * TPC * CPI + k + 1)
                nc.vector.reduce_max(pmax[:, q, kc:kc + 1], ppre[k % 2][:, 0:CH], AX.X).then_inc(pre_max, 1)
                if kc == CPI - 1:
                    dve.wait_ge(pre_max, g * TPC * CPI + k + 1)
                    nc.vector.tensor_reduce(negmax[:, q, X1 - 1:XS:LO],
                                            pmax[:, q:q + 1, :].broadcast_to([T, 2, CPI]),
                                            AX.X, ALU.max, negate=True).then_inc(max_ready, 1)

            def shift_y(g, first=False):
                dve.wait_ge(shift_mm, g + 1)
                dve.wait_ge(y_out, 2 * (g + 1))
                nc.vector.tensor_tensor(ysum[:], y32[:], pmisc[0:XS, 0:CH], ALU.add).then_inc(dvec, 1)
                dve.wait_ge(dvec, g + 1)
                if not first:
                    dve.wait_ge(scores, g * SLOTS)
                nc.vector.tensor_copy(yh[:], ysum[:]).then_inc(y_shifted, 1)
                dve.wait_ge(y_shifted, 2 * g + 1)
                nc.vector.tensor_tensor(yl[:], ysum[:], yh[:].bitcast(F32), ALU.subtract).then_inc(y_shifted, 1)

            def take_o(g):
                dve.wait_ge(pv, (g + 1) * SLOTS)
                nc.vector.tensor_copy(oT[:], pout[:, 0:CH]).then_inc(o_out, 1)

            def take_projected(g, r):
                dve.wait_ge(proj_mm, 2 * g + r + 1)
                two = pmisc[0:T, 0:2 * (D + 1)].rearrange("p (i c) -> p i c", i=2)
                nc.vector.reciprocal(rden[:, 2 * r:2 * r + 2, :], two[:, :, D:D + 1]).then_inc(proj_rden, 1)
                dve.wait_ge(proj_rden, 2 * g + r + 1)
                for i in range(2):
                    nc.vector.tensor_scalar(h[:, g * TPC + 2 * r + i, :], two[:, i, 0:D], rden[:, 2 * r + i, :], None,
                                            ALU.mult).then_inc(proj_out, 1)

            def take_stats(g):
                for q in range(TPC):
                    nc.vector.bn_stats(bns[:, g * TPC + q, :], h[:, g * TPC + q, :]).then_inc(stat_out, 1)

            def chunk(g, first=False, last=False):
                if not last:
                    take_y(g + 1)
                    for k in range(TPC * CPI):
                        if not first and k in (5, 11):
                            take_projected(g - 1, (5, 11).index(k))
                        if not first and k == 14:
                            dve.wait_ge(proj_out, 4 * g)
                        take_max(g + 1, k)
                        if not first and k == 14:
                            take_stats(g - 1)
                    shift_y(g + 1)
                else:
                    take_projected(g - 1, 0)
                    take_projected(g - 1, 1)
                    dve.wait_ge(proj_out, 4 * g)
                    take_stats(g - 1)
                take_o(g)

            take_y(0)
            for k in range(TPC * CPI):
                take_max(0, k)
            shift_y(0, first=True)
            chunk(0, first=True)
            with dve.Fori(1, NC - 1) as g:
                chunk(g)
            chunk(NC - 1, last=True)
            take_projected(NC - 1, 0)
            take_projected(NC - 1, 1)
            dve.wait_ge(proj_out, 4 * NC)
            take_stats(NC - 1)


def inverse_root(nc, dve, link, out, var, root, t):
    link(nc.vector.reciprocal(root, root))
    link(nc.vector.tensor_tensor(t, root, root, ALU.mult))
    link(nc.vector.tensor_tensor(t, t, var, ALU.mult))
    link(nc.vector.tensor_scalar(t, t, -0.5, 1.5, ALU.mult, ALU.add))
    return nc.vector.tensor_tensor(out, root, t, ALU.mult)


def finish_stats(nc, name, bns, mean, rstd, vtok, eps):
    with ExitStack() as ctx:
        sb, ps, sem = allocator(nc, ctx)
        dif = sb(f"dif_{name}", [T, NT])
        var = sb(f"var_{name}", [T, NT])
        root = sb(f"root_{name}", [T, NT])
        done = sem(f"stats_{name}")
        ready = sem(f"var_{name}_ready")
        rooted = sem(f"root_{name}_ready")
        block = ctx.enter_context(nc.Block())

        @block.scalar
        def _(act):
            nc.scalar.preload_act_table(ACT.Sqrt)
            act.wait_ge(ready, 1)
            nc.scalar.activation(root[:], var[:], ACT.Sqrt).then_inc(rooted, 1)

        @block.vector
        def _(dve):
            nc.vector.tensor_tensor(mean[:], bns[:, :, 1], bns[:, :, 4], ALU.add).then_inc(done, 1)
            nc.vector.tensor_tensor(dif[:], bns[:, :, 1], bns[:, :, 4], ALU.subtract).then_inc(done, 1)
            nc.vector.tensor_tensor(var[:], bns[:, :, 2], bns[:, :, 5], ALU.add).then_inc(done, 1)
            dve.wait_ge(done, 3)
            nc.vector.tensor_scalar(mean[:], mean[:], 0.5, None, ALU.mult).then_inc(done, 1)
            nc.vector.scalar_tensor_tensor(dif[:], dif[:], D / 4, dif[:], ALU.mult, ALU.mult).then_inc(done, 1)
            dve.wait_ge(done, 5)
            nc.vector.tensor_tensor(var[:], var[:], dif[:], ALU.add).then_inc(done, 1)
            dve.wait_ge(done, 6)
            nc.vector.tensor_scalar(vtok[:], var[:], 1.0 / D, None, ALU.mult).then_inc(done, 1)
            dve.wait_ge(done, 7)
            nc.vector.tensor_scalar(var[:], vtok[:], eps, None, ALU.add).then_inc(ready, 1)
            count = [7]

            def link(ins):
                count[0] = count[0] + 1
                ins.then_inc(done, 1)
                dve.wait_ge(done, count[0])

            dve.wait_ge(ready, 1)
            dve.wait_ge(rooted, 1)
            inverse_root(nc, dve, link, rstd[:], var[:], root[:], dif[:])


def retention_phase(nc, ins, h, bns, mean, rstd, eye):
    M = 64
    V1 = D + 1
    with ExitStack() as ctx:
        sb, ps, sem = allocator(nc, ctx)
        wqk = sb("wqk", [KC, 2, 128])
        wff = sb("wff", [KC, 2, 128])
        bff = sb("bff", [128, 1])
        wv = sb("wv", [KC, 2, D])
        wo = sb("wo", [KC, 2, D])
        betb = sb("betb", [KC, 2, T])
        brow = sb("brow2", [T, D])
        spare = sb("spare2", [T, 1])
        gam = sb("gam", [KC, 2])
        bet = sb("bet", [KC, 2])
        sgn = sb("sgn", [128, 1])
        mask = sb("mask", [T, T])
        ones = sb("ones_scan", [128, CH])
        eps5 = sb("eps5", [T, TPC])
        mhalf = sb("mhalf4", [T, TPC])
        xn = sb("xn2", [T, TPC, D])
        xT = sb("xT2", [KC, 2, CH])
        gate = sb("gate2", [128, CH])
        elu = sb("elu2", [128, CH])
        cum = sb("cum2", [128, CH])
        dec = sb("dec2", [128, CH])
        tail = sb("tail2", [128, 1])
        qt = sb("qt2", [M, CH])
        kt = sb("kt2", [M, CH])
        ktok = sb("ktok2", [T, TPC, M])
        vt = sb("vt2", [T, TPC, V1])
        at = sb("at2", [T, TPC, T])
        snap = sb("snap2", [M, TPC, V1])
        den = sb("den2", [T, TPC, 1])
        hh = sb("hh2", [T, TPC, D])
        bn = sb("bn2", [T, TPC, 6])
        agg = sb("agg2", [T, TPC, 2])
        veps = sb("veps2", [T, TPC])
        rst = sb("rst2", [T, TPC])
        nT = sb("nT2", [KC, 2, CH])
        ptr = ps("ptr2", [KC, 2, 512])
        pqk = ps("pqk2", [128, 512])
        pff = ps("pff2", [128, 512])
        pvo = ps("pvo2", [T, 2, 512])
        pat = ps("pat2", [T, 512])
        pst = ps("pst2", [M, 512])

        names = ("w_in", "w_ready", "brow_mm", "xn_ready", "xtr_mm", "xT_out", "qk_mm", "ff_mm", "v_mm", "v_out",
                 "bias_out", "ntr_mm", "nT_out", "wo_mm", "h_out", "gate_in", "gate_out", "elu_in", "elu_out",
                 "cum_out", "dec_out", "qk_out", "ktr_mm", "ktok_out", "at_mm", "at_out", "st_mm", "snap_out",
                 "num_mm", "hhc", "hh_out", "agg_out", "rst_out", "dvec", "poolc")
        S = {n: sem(f"{n}_2") for n in names}
        block = ctx.enter_context(nc.Block())

        @block.sync
        def _(sp):
            for dst, name in ((wqk, "wqk"), (wff, "wff"), (bff, "bff"), (wv, "wv"), (gam, "gam2"),
                              (bet, "bet2"), (sgn, "sgn"), (mask, "mask")):
                sp.dma_start(dst[:], ins[name]).then_inc(S["w_in"], 16)
            sp.dma_start(wo[:], ins["wo2"]).then_inc(S["w_in"], 16)

        @block.gpsimd
        def _(pool):
            for n, (buf, value) in enumerate(((ones[:], 1.0), (eps5[:], 1e-5), (mhalf[:], -0.5),
                                              (vt[:, :, D:V1], 1.0))):
                nc.gpsimd.memset(buf, value).then_inc(S["w_ready"], 1)
                pool.wait_ge(S["w_ready"], n + 1)

            def chunk(g, first=False):
                if not first:
                    pool.wait_ge(S["rst_out"], g)
                pool.wait_ge(S["agg_out"], g + 1)
                nc.gpsimd.tensor_tensor(veps[:], agg[:, :, 1], eps5[:], ALU.add).then_inc(S["poolc"], 1)
                pool.wait_ge(S["poolc"], g + 1)
                nc.gpsimd.tensor_tensor(rst[:], veps[:], mhalf[:], ALU.pow).then_inc(S["rst_out"], 1)

            chunk(0, first=True)
            with pool.Fori(1, NC) as g:
                chunk(g)

        @block.tensor
        def _(pe):
            pe.wait_ge(S["w_in"], 16 * 9)
            pe.wait_ge(S["w_ready"], 5)
            for c in range(2):
                mm = pe.matmul(pat[:, 0:D], betb[:, c, :], wo[:, c, :], start=(c == 0), stop=(c == 1))
            mm.then_inc(S["brow_mm"], 1)
            pe.wait_ge(S["w_ready"], 6)
            for c in range(2):
                mm = pe.matmul(pqk[0:KC, 0:D], ones[0:KC, 0:KC], wo[:, c, :], start=(c == 0), stop=(c == 1))
            mm.then_inc(S["brow_mm"], 1)
            pe.wait_ge(S["w_ready"], 7)

            def transpose_x(g):
                pe.wait_ge(S["xn_ready"], g + 1)
                for q in range(TPC):
                    for c in range(2):
                        mm = pe.transpose(ptr[:, c, q * T:(q + 1) * T], xn[:, q, c * KC:(c + 1) * KC], eye[0:T, 0:T])
                mm.then_inc(S["xtr_mm"], 1)

            def project(g):
                pe.wait_ge(S["xT_out"], g + 1)
                for dst, w, done in ((pff, wff, "ff_mm"), (pqk, wqk, "qk_mm")):
                    for c in range(2):
                        mm = pe.matmul(dst[:, 0:CH], w[:, c, :], xT[:, c, :], start=(c == 0), stop=(c == 1))
                    mm.then_inc(S[done], 1)

            def values(g, first=False):
                if not first:
                    pe.wait_ge(S["hh_out"], g)
                for q in range(TPC):
                    for c in range(2):
                        mm = pe.matmul(pvo[:, q // 2, (q % 2) * V1:(q % 2) * V1 + D], xT[:, c, q * T:(q + 1) * T],
                                       wv[:, c, :], start=(c == 0), stop=(c == 1), skip_group_check=True)
                    if q % 2 == 1:
                        mm.then_inc(S["v_mm"], 1)

            def weights(g):
                pe.wait_ge(S["qk_out"], g + 1)
                for q in range(TPC):
                    mm = pe.matmul(pat[:, q * T:(q + 1) * T], kt[:, q * T:(q + 1) * T], qt[:, q * T:(q + 1) * T],
                                   start=True, stop=True)
                mm.then_inc(S["at_mm"], 1)
                for q in range(TPC):
                    mm = pe.transpose(pff[0:T, q * M:(q + 1) * M], kt[:, q * T:(q + 1) * T], eye[0:M, 0:M])
                mm.then_inc(S["ktr_mm"], 1)

            def attend(g, reset, first):
                if not first:
                    pe.wait_ge(S["h_out"], g)
                pe.wait_ge(S["v_out"], 2 * g + 2)
                pe.wait_ge(S["ktok_out"], g + 1)
                pe.wait_ge(S["at_out"], g + 1)
                for q in range(TPC):
                    if not (reset and q == 0):
                        pe.wait_ge(S["snap_out"], g * TPC + q)
                    num = pvo[:, q // 2, (q % 2) * V1:(q % 2 + 1) * V1]
                    pe.matmul(pst[:, 0:V1], ktok[:, q, :], vt[:, q, :], start=(reset and q == 0), stop=True,
                              skip_group_check=True).then_inc(S["st_mm"], 1)
                    mm = pe.matmul(num, at[:, q, :], vt[:, q, :], start=True, stop=(reset and q == 0),
                                   skip_group_check=True)
                    if not (reset and q == 0):
                        mm = pe.matmul(num, qt[:, q * T:(q + 1) * T], snap[:, q, :], start=False, stop=True,
                                       skip_group_check=True)
                mm.then_inc(S["num_mm"], 1)

            def transpose_n(g):
                pe.wait_ge(S["hh_out"], g + 1)
                for q in range(TPC):
                    for c in range(2):
                        mm = pe.transpose(ptr[:, c, q * T:(q + 1) * T], hh[:, q, c * KC:(c + 1) * KC], eye[0:T, 0:T])
                mm.then_inc(S["ntr_mm"], 1)

            def wo_out(g, last=False):
                pe.wait_ge(S["nT_out"], g + 1)
                for q in range(TPC):
                    if q % 2 == 0 and not last:
                        pe.wait_ge(S["v_out"], 2 * g + 3 + q // 2)
                    for c in range(2):
                        mm = pe.matmul(pvo[:, q // 2, (q % 2) * V1:(q % 2) * V1 + D], nT[:, c, q * T:(q + 1) * T],
                                       wo[:, c, :], start=(c == 0), stop=(c == 1), skip_group_check=True)
                    if q % 2 == 1:
                        mm.then_inc(S["wo_mm"], 1)

            def chunk(g, reset=False, first=False, last=False):
                weights(g)
                if not last:
                    transpose_x(g + 1)
                attend(g, reset, first)
                if not last:
                    project(g + 1)
                transpose_n(g)
                if not last:
                    values(g + 1)
                wo_out(g, last)

            transpose_x(0)
            project(0)
            values(0, first=True)
            chunk(0, reset=True, first=True)
            with pe.Fori(1, CPI) as c:
                chunk(c)
            with pe.Fori(1, B - 1) as b:
                chunk(b * CPI, reset=True)
                with pe.Fori(1, CPI) as c:
                    chunk(b * CPI + c)
            chunk((B - 1) * CPI, reset=True)
            with pe.Fori((B - 1) * CPI + 1, NC - 1) as g:
                chunk(g)
            chunk(NC - 1, last=True)

        @block.scalar
        def _(act):
            nc.scalar.preload_act_table_set("natural_log_exp_and_others")
            act.wait_ge(S["w_ready"], 7)

            def take_n(g):
                act.wait_ge(S["ntr_mm"], g + 1)
                nc.scalar.copy(nT[:, :, :], ptr[:, :, 0:CH]).then_inc(S["nT_out"], 1)

            def gate_and_values(g, first=False):
                act.wait_ge(S["gate_in"], g + 1)
                nc.scalar.activation(gate[:], gate[:], ACT.Exp, scale=-1.0).then_inc(S["gate_out"], 1)
                act.wait_ge(S["gate_out"], 2 * g + 1)
                nc.scalar.activation(gate[:], gate[:], ACT.Ln, bias=1.0).then_inc(S["gate_out"], 1)
                act.wait_ge(S["elu_in"], g + 1)
                nc.scalar.activation(elu[:], elu[:], ACT.Exp).then_inc(S["elu_out"], 1)
                if not first:
                    take_n(g - 1)
                for i in range(2):
                    act.wait_ge(S["v_mm"], 2 * g + i + 1)
                    nc.scalar.copy(vt[:, 2 * i:2 * i + 2, 0:D],
                                   pvo[:, i, 0:2 * V1].rearrange("p (q v) -> p q v", q=2)[:, :, 0:D]).then_inc(
                                       S["v_out"], 1)
                act.wait_ge(S["cum_out"], g + 1)
                nc.scalar.activation(dec[:], cum[:], ACT.Exp, scale=sgn[:]).then_inc(S["dec_out"], 1)

            def chunk(g, last=False):
                act.wait_ge(S["ktr_mm"], g + 1)
                nc.scalar.copy(ktok[:, :, :], pff[0:T, 0:TPC * M].rearrange("p (q m) -> p q m", q=TPC)).then_inc(
                    S["ktok_out"], 1)
                for q in range(TPC):
                    act.wait_ge(S["st_mm"], g * TPC + q + 1)
                    nc.scalar.copy(snap[:, (q + 1) % TPC, :], pst[:, 0:V1]).then_inc(S["snap_out"], 1)
                if not last:
                    gate_and_values(g + 1)
                else:
                    take_n(g)

            gate_and_values(0, first=True)
            with act.Fori(0, NC - 1) as g:
                chunk(g)
            chunk(NC - 1, last=True)

        @block.vector
        def _(dve):
            dve.wait_ge(S["w_in"], 16 * 9)
            dve.wait_ge(S["w_ready"], 4)
            for c in range(2):
                ts = nc.vector.tensor_scalar(betb[:, c, :], ones[0:KC, 0:T], bet[:, c:c + 1], None, ALU.mult)
            ts.then_inc(S["w_ready"], 1)
            dve.wait_ge(S["brow_mm"], 1)
            nc.vector.tensor_copy(brow[:], pat[:, 0:D])
            for c in range(2):
                ts = nc.vector.tensor_scalar(wo[:, c, :], wo[:, c, :], gam[:, c:c + 1], None, ALU.mult)
            ts.then_inc(S["w_ready"], 1)
            dve.wait_ge(S["brow_mm"], 2)
            for c in range(2):
                ts = nc.vector.scalar_tensor_tensor(wo[:, c, :], pqk[0:KC, 0:D], -1.0 / D, wo[:, c, :],
                                                    ALU.mult, ALU.add)
            ts.then_inc(S["w_ready"], 1)

            def normalise(g):
                for q in range(TPC):
                    t = g * TPC + q
                    ts = nc.vector.tensor_scalar(xn[:, q, :], h[:, t, :], mean[:, bass.ds(t, 1)], rstd[:, bass.ds(t, 1)],
                                                 ALU.subtract, ALU.mult)
                ts.then_inc(S["xn_ready"], 1)

            def take_x(g):
                dve.wait_ge(S["xtr_mm"], g + 1)
                nc.vector.tensor_copy(xT[:, :, :], ptr[:, :, 0:CH]).then_inc(S["xT_out"], 1)

            def sums_out(g):
                dve.wait_ge(S["num_mm"], g + 1)
                step = [g * 3]

                def link(ins):
                    step[0] = step[0] + 1
                    ins.then_inc(S["hhc"], 1)
                    dve.wait_ge(S["hhc"], step[0])

                two = [pvo[:, i, 0:2 * V1].rearrange("p (q v) -> p q v", q=2) for i in range(2)]
                for i in range(2):
                    ts = nc.vector.tensor_scalar(den[:, 2 * i:2 * i + 2, :], two[i][:, :, D:V1], 1e-6, None, ALU.add)
                link(ts)
                link(nc.vector.reciprocal(den[:], den[:]))
                for q in range(TPC):
                    ts = nc.vector.tensor_scalar(hh[:, q, :], two[q // 2][:, q % 2, 0:D], den[:, q, :], None, ALU.mult)
                ts.then_inc(S["hh_out"], 1)

            def sums_stats(g):
                dve.wait_ge(S["hh_out"], g + 1)
                for q in range(TPC):
                    bs = nc.vector.bn_stats(bn[:, q, :], hh[:, q, :])
                bs.then_inc(S["hhc"], 1)
                dve.wait_ge(S["hhc"], 3 * g + 3)

            def sums_aggr(g):
                for q in range(TPC):
                    ag = nc.vector.bn_aggr(agg[:, q, :], bn[:, q, :])
                ag.then_inc(S["agg_out"], 1)

            def gate_in(g):
                dve.wait_ge(S["ff_mm"], g + 1)
                nc.vector.tensor_scalar(gate[:], pff[:, 0:CH], bff[:], ZMIN, ALU.add, ALU.max).then_inc(S["gate_in"], 1)

            def elu_in(g):
                dve.wait_ge(S["qk_mm"], g + 1)
                nc.vector.tensor_scalar(elu[:], pqk[:, 0:CH], 0.0, None, ALU.min).then_inc(S["elu_in"], 1)

            def scan(g, reset, sums=None):
                dve.wait_ge(S["gate_out"], 2 * g + 2)
                nc.vector.tensor_tensor_scan(cum[:], ones[:], gate[:], 0.0 if reset else tail[:],
                                             ALU.mult, ALU.subtract).then_inc(S["dvec"], 1)
                if sums is not None:
                    sums_aggr(sums)
                dve.wait_ge(S["dvec"], 3 * g + 1)
                nc.vector.tensor_copy(tail[:], cum[:, CH - 1:CH]).then_inc(S["dvec"], 1)
                dve.wait_ge(S["dvec"], 3 * g + 2)
                nc.vector.tensor_scalar(cum[:], cum[:], -20.0, 20.0, ALU.max, ALU.min).then_inc(S["cum_out"], 1)

            def q_and_k(g):
                dve.wait_ge(S["elu_out"], g + 1)
                nc.vector.scalar_tensor_tensor(elu[:], pqk[:, 0:CH], 0.0, elu[:], ALU.max, ALU.add).then_inc(S["dvec"], 1)
                dve.wait_ge(S["dvec"], 3 * g + 3)
                dve.wait_ge(S["dec_out"], g + 1)
                nc.vector.scalar_tensor_tensor(qt[:], elu[0:M, :], M ** -0.5, dec[0:M, :], ALU.mult, ALU.mult)
                nc.vector.tensor_tensor(kt[:], elu[M:128, :], dec[M:128, :], ALU.mult).then_inc(S["qk_out"], 1)

            def add_out(g):
                dve.wait_ge(S["rst_out"], g + 1)
                for r in range(2):
                    dve.wait_ge(S["wo_mm"], 2 * g + r + 1)
                    for i in range(2):
                        hs = h[:, g * TPC + 2 * r + i, :]
                        tt = nc.vector.scalar_tensor_tensor(hs, pvo[:, r, i * V1:i * V1 + D],
                                                            rst[:, 2 * r + i:2 * r + i + 1], hs, ALU.mult, ALU.add)
                tt.then_inc(S["h_out"], 1)

            def add_bias(g):
                hs = h[:, bass.ds(g * TPC, TPC), :]
                nc.vector.tensor_tensor(hs, hs, brow[:].unsqueeze(1).broadcast_to([T, TPC, D]),
                                        ALU.add).then_inc(S["bias_out"], 1)

            def take_stats(g):
                for q in range(TPC):
                    nc.vector.bn_stats(bns[:, g * TPC + q, :], h[:, g * TPC + q, :])

            def chunk(g, reset_next=False, first=False, last=False, enter=True):
                if not first:
                    dve.wait_ge(S["h_out"], g)
                dve.wait_ge(S["at_mm"], g + 1)
                nc.vector.tensor_tensor(at[:, :, :], pat[:, 0:CH].rearrange("p (q t) -> p q t", q=TPC),
                                        mask[:, :].unsqueeze(1).broadcast_to([T, TPC, T]), ALU.mult).then_inc(S["at_out"], 1)
                if not last:
                    take_x(g + 1)
                if not first:
                    add_bias(g - 1)
                if enter:
                    normalise(g + 2)
                if not first:
                    dve.wait_ge(S["bias_out"], g)
                    nc.vector.tensor_copy(spare[:], eye[0:T, 0:1])
                    take_stats(g - 1)
                sums_out(g)
                if not last:
                    gate_in(g + 1)
                    elu_in(g + 1)
                sums_stats(g)
                if last:
                    sums_aggr(g)
                else:
                    scan(g + 1, reset_next, g)
                    q_and_k(g + 1)
                add_out(g)

            normalise(0)
            take_x(0)
            normalise(1)
            gate_in(0)
            elu_in(0)
            scan(0, True)
            q_and_k(0)
            chunk(0, first=True)
            with dve.Fori(1, CPI - 1) as c:
                chunk(c)
            chunk(CPI - 1, reset_next=True)
            with dve.Fori(1, B - 1) as b:
                with dve.Fori(0, CPI - 1) as c:
                    chunk(b * CPI + c)
                chunk(b * CPI + CPI - 1, reset_next=True)
            with dve.Fori((B - 1) * CPI, NC - 2) as g:
                chunk(g)
            chunk(NC - 2, enter=False)
            chunk(NC - 1, last=True, enter=False)
            dve.wait_ge(S["h_out"], NC)
            add_bias(NC - 1)
            dve.wait_ge(S["bias_out"], NC)
            take_stats(NC - 1)


def expert_phase(nc, ins, h, bns, mean, rstd, eye):
    E, HID = 8, 256
    with ExitStack() as ctx:
        sb, ps, sem = allocator(nc, ctx)
        w1h = sb("w1h", [128, 2, KC], F32R)
        w1l = sb("w1l", [128, 2, KC], F32R)
        w1s = sb("w1s", [128, 2, KC])
        b1 = sb("b1_3", [KC, 1])
        w2 = sb("w2_3", [KC + 1, E])
        downh = sb("downh", [128, 2, E, HID], F32R)
        downl = sb("downl", [128, 2, E, HID], F32R)
        downb = sb("downb", [128, 2 * E])
        uph = sb("uph", [128, E, 2, D], F32R)
        upl = sb("upl", [128, E, 2, D], F32R)
        gam = sb("gam3", [T, D])
        bet = sb("bet3", [T, D])
        tri = sb("tri", [T, E, E])
        eps5 = sb("eps5_3", [T, TPC])
        mhalf = sb("mhalf_3", [T, TPC])
        xth = sb("xth3", [128, 2, CH], F32R)
        xtl = sb("xtl3", [128, CH], F32R)
        r1 = sb("r1", [KC + 1, CH])
        lg = sb("lg", [T, TPC, E])
        ex = sb("ex", [T, TPC, E])
        small = sb("small3", [T, TPC, 1])
        gt = sb("gt3", [T, TPC * E, E])
        eq = sb("eq3", [T, TPC * E, E])
        gates = sb("gates", [T, TPC, E])
        zh = [[sb(f"zh{i}{m}", [128, CH], F32R) for m in range(2)] for i in range(2)]
        zl = [[sb(f"zl{i}{m}", [128, CH], F32R) for m in range(2)] for i in range(2)]
        stage = sb("stage3", [128, 2, 2048])
        z = [stage[:, 0, m * CH:(m + 1) * CH] for m in range(2)]
        acc = stage[0:T, 0, 1024:1024 + TPC * D].rearrange("p (q d) -> p q d", q=TPC)
        xn = sb("xn3", [T, TPC, 256])
        yf = stage[0:T, 1, 1024:1024 + TPC * D].rearrange("p (q d) -> p q d", q=TPC)
        bn = sb("bn3", [T, TPC, 6])
        agg = sb("agg3", [T, TPC, 2])
        veps = sb("veps3", [T, TPC])
        rst = sb("rst3", [T, TPC])
        ptr = ps("ptr3", [128, 2, 512])
        prt = ps("prt3", [KC, 512])
        plg = ps("plg3", [T, TPC * E])
        pz = [ps(f"pz{m}", [128, 512]) for m in range(2)]
        py = ps("py3", [T, 2, 512])
        names = ("w_in", "w_ready", "xn_ready", "xtr_mm", "xT_out", "r1_mm", "r1_out", "lg_mm", "dvec", "lg_out",
                 "ex_out", "gates_out", "down_mm", "z_out", "zl_out", "xL_out", "split", "high", "veps_out", "gam_out", "mx_out", "up_mm", "acc_out", "stat_out", "agg_out", "rst_out",
                 "nrm_out", "poolc", "yf_out", "h_out")
        S = {n: sem(f"{n}_3") for n in names}
        stage_in = [sem(f"stage{i}_in_3") for i in range(2)]
        block = ctx.enter_context(nc.Block())
        NW = 7
        UPH = E // 2 * 2 * D
        pieces = [(w1h[:], w1l[:], w1s[:])]
        pieces += [(downh[:, half].rearrange("p e d -> p (e d)"), downl[:, half].rearrange("p e d -> p (e d)"),
                    stage[:, half, :]) for half in range(2)]
        pieces += [(uph[:, half * E // 2:(half + 1) * E // 2].rearrange("p e m d -> p (e m d)"),
                    upl[:, half * E // 2:(half + 1) * E // 2].rearrange("p e m d -> p (e m d)"),
                    stage[:, half, 0:UPH]) for half in range(2)]

        @block.sync
        def _(sp):
            for dst, name in ((w1s[:], "w1"), (b1[:], "b1"), (w2[:], "w2"), (downb[:], "downb"), (gam[:], "gam3"),
                              (bet[:], "bet3"), (tri[:], "tri")):
                sp.dma_start(dst, ins[name]).then_inc(S["w_in"], 16)
            for half in range(2):
                sp.dma_start(stage[:, half, :], ins["down"][:, half].rearrange("p e d -> p (e d)")).then_inc(
                    stage_in[half], 16)
            for half in range(2):
                sp.wait_ge(S["split"], 2 + half)
                sp.dma_start(stage[:, half, 0:UPH],
                             ins["up"][:, half * E // 2:(half + 1) * E // 2].rearrange("p e m d -> p (e m d)")
                             ).then_inc(stage_in[half], 16)

        @block.gpsimd
        def _(pool):
            for n, (buf, value) in enumerate(((eps5[:], 1e-5), (mhalf[:], -0.5), (r1[KC:KC + 1], 1.0))):
                nc.gpsimd.memset(buf, value).then_inc(S["w_ready"], 1)
                pool.wait_ge(S["w_ready"], n + 1)
            pool.wait_ge(S["w_in"], 16 * NW)

            def low(g, e, first=False):
                for m in range(2):
                    if m or e or not first:
                        pool.wait_ge(S["zl_out"], 2 * (g * E + e) + m)
                    pool.wait_ge(S["z_out"], 2 * (g * E + e) + m + 1)
                    nc.gpsimd.tensor_tensor(zl[e % 2][m][:], z[m][:], zh[e % 2][m][:].bitcast(F32),
                                            ALU.subtract).then_inc(S["zl_out"], 1)

            def factor(g, done):
                pool.wait_ge(S["zl_out"], done)
                pool.wait_ge(S["agg_out"], g + 1)
                nc.gpsimd.tensor_tensor(veps[:], agg[:, :, 1], eps5[:], ALU.add).then_inc(S["veps_out"], 1)
                pool.wait_ge(S["veps_out"], g + 1)
                nc.gpsimd.tensor_tensor(rst[:], veps[:], mhalf[:], ALU.pow).then_inc(S["rst_out"], 1)
                pool.wait_ge(S["rst_out"], g + 1)

            def times_gamma(g, done):
                pool.wait_ge(S["zl_out"], done)
                pool.wait_ge(S["nrm_out"], g + 1)
                nc.gpsimd.tensor_tensor(yf, yf, gam[:].unsqueeze(1).broadcast_to([T, TPC, D]),
                                        ALU.mult).then_inc(S["gam_out"], 1)
                pool.wait_ge(S["gam_out"], g + 1)

            def plus_beta(g, done):
                pool.wait_ge(S["zl_out"], done)
                nc.gpsimd.tensor_tensor(yf, yf, bet[:].unsqueeze(1).broadcast_to([T, TPC, D]),
                                        ALU.add).then_inc(S["yf_out"], 1)
                pool.wait_ge(S["yf_out"], g + 1)

            def chunk(g, first=False):
                done = 2 * E * g
                for e in range(E):
                    low(g, e, first)
                    if not first and e == 2:
                        factor(g - 1, done + 6)
                    if not first and e == 3:
                        times_gamma(g - 1, done + 8)
                    if not first and e == 4:
                        plus_beta(g - 1, done + 10)

            chunk(0, first=True)
            with pool.Fori(1, NC) as g:
                chunk(g)
            factor(NC - 1, 2 * E * NC)
            times_gamma(NC - 1, 2 * E * NC)
            plus_beta(NC - 1, 2 * E * NC)

        @block.tensor
        def _(pe):
            pe.wait_ge(S["w_in"], 16 * NW)
            pe.wait_ge(S["w_ready"], 3)

            def split_product(dst, wh, wl, cols):
                steps = ((wh[:, 0], xth[:, 0, :]), (wh[:, 0], xtl[:]), (wl[:, 0], xth[:, 0, :]),
                         (wh[:, 1], xth[:, 1, :]), (wl[0:64, 1], xth[0:64, 1, :]))
                for n, (w, x) in enumerate(steps):
                    mm = pe.matmul(dst, w[:, cols], x, start=(n == 0), stop=(n == 4))
                return mm

            def front(g):
                pe.wait_ge(S["xn_ready"], g + 1)
                for q in range(TPC):
                    for c in range(2):
                        mm = pe.transpose(ptr[:, c, q * T:(q + 1) * T], xn[:, q, c * 128:(c + 1) * 128], eye[0:T, 0:T])
                mm.then_inc(S["xtr_mm"], 1)

            def router(g):
                pe.wait_ge(S["xL_out"], g + 1)
                if isinstance(g, int) and g == 0:
                    pe.wait_ge(S["split"], 1)
                split_product(prt[:, 0:CH], w1h, w1l, slice(0, KC)).then_inc(S["r1_mm"], 1)

            def logits(g):
                pe.wait_ge(S["r1_out"], g + 1)
                for q in range(TPC):
                    mm = pe.matmul(plg[:, q * E:(q + 1) * E], r1[:, q * T:(q + 1) * T], w2[:], start=True, stop=True,
                                   skip_group_check=True)
                mm.then_inc(S["lg_mm"], 1)

            def down_e(g, e, m, first=False):
                if first:
                    pe.wait_ge(S["split"], 5)
                else:
                    pe.wait_ge(S["z_out"], 2 * (g * E + e) - 1 + m)
                split_product(pz[m][:, 0:CH], downh[:, :, e], downl[:, :, e],
                              slice(m * 128, (m + 1) * 128)).then_inc(S["down_mm"], 1)

            def up_e(g, e, first):
                pe.wait_ge(S["zl_out"], 2 * (g * E + e) + 2)
                for q in range(TPC):
                    if q % 2 == 0 and (e >= 1 or not first):
                        pe.wait_ge(S["acc_out"], 2 * (g * E + e) - 1 + q // 2)
                    cols = slice(q * T, (q + 1) * T)
                    for m in range(2):
                        for n, (zz, w) in enumerate(((zh, uph), (zl, uph), (zh, upl))):
                            mm = pe.matmul(py[:, q // 2, (q % 2) * D:(q % 2 + 1) * D], zz[e % 2][m][:, cols],
                                           w[:, e, m, :], start=(m + n == 0), stop=(m + n == 3), skip_group_check=True)
                    if q % 2 == 1:
                        mm.then_inc(S["up_mm"], 1)

            def chunk(g, first=False, last=False):
                for e in range(1, E):
                    down_e(g, e, 0)
                    down_e(g, e, 1)
                    if e == 5 and not last:
                        front(g + 1)
                    up_e(g, e - 1, first)
                if not last:
                    router(g + 1)
                    down_e(g + 1, 0, 0)
                    logits(g + 1)
                    down_e(g + 1, 0, 1)
                up_e(g, E - 1, first)

            front(0)
            router(0)
            down_e(0, 0, 0, first=True)
            logits(0)
            down_e(0, 0, 1, first=True)
            chunk(0, first=True)
            with pe.Fori(1, NC - 1) as g:
                chunk(g)
            chunk(NC - 1, last=True)

        @block.scalar
        def _(act):
            def take_x(g):
                if not isinstance(g, int) or g > 0:
                    act.wait_ge(S["down_mm"], 2 * E * g)
                act.wait_ge(S["xtr_mm"], g + 1)
                nc.scalar.copy(xth[:, :, :], ptr[:, :, 0:CH]).then_inc(S["xT_out"], 1)

            def take_r1(g):
                act.wait_ge(S["r1_mm"], g + 1)
                nc.scalar.activation(r1[0:KC], prt[:, 0:CH], ACT.Gelu, bias=b1[:]).then_inc(S["r1_out"], 1)

            def gelu_e(g, e, first=False):
                for m in range(2):
                    if e or not first:
                        act.wait_ge(S["zl_out"], 2 * (g * E + e) - 1 + m)
                    act.wait_ge(S["down_mm"], 2 * (g * E + e) + m + 1)
                    nc.scalar.activation(z[m][:], pz[m][:, 0:CH], ACT.Gelu, bias=downb[:, 2 * e + m:2 * e + m + 1])
                    if m == 0 and (e >= 2 or not first):
                        act.wait_ge(S["up_mm"], 2 * (g * E + e) - 2)
                    nc.scalar.activation(zh[e % 2][m][:], pz[m][:, 0:CH], ACT.Gelu,
                                         bias=downb[:, 2 * e + m:2 * e + m + 1]).then_inc(S["z_out"], 1)

            def chunk(g, first=False, last=False):
                take_r1(g)
                gelu_e(g, 0, first)
                act.wait_ge(S["lg_out"], g + 1)
                nc.scalar.activation(ex[:], lg[:], ACT.Exp).then_inc(S["ex_out"], 1)
                gelu_e(g, 1, first)
                for e in range(2, E - 1):
                    gelu_e(g, e)
                if not last:
                    take_x(g + 1)
                gelu_e(g, E - 1)

            act.wait_ge(S["w_in"], 16 * NW)
            for n, (high, low, src) in enumerate(pieces):
                if n >= 1:
                    act.wait_ge(stage_in[(n - 1) % 2], 16 if n <= 2 else 32)
                nc.scalar.copy(high, src).then_inc(S["high"], 1)
                if n == 0:
                    take_x(0)
            chunk(0, first=True)
            with act.Fori(1, NC - 1) as g:
                chunk(g)
            chunk(NC - 1, last=True)

        @block.vector
        def _(dve):
            CHAIN = 11

            def normalise(g):
                for q in range(TPC):
                    t = g * TPC + q
                    nc.vector.tensor_scalar(xn[:, q, 0:D], h[:, t, :], mean[:, bass.ds(t, 1)],
                                            rstd[:, bass.ds(t, 1)], ALU.subtract, ALU.mult)
                for q in range(TPC):
                    t = g * TPC + q
                    ts = nc.vector.tensor_scalar(xn[:, q, D:256], h[:, t, 128:D], mean[:, bass.ds(t, 1)],
                                                 rstd[:, bass.ds(t, 1)], ALU.subtract, ALU.mult)
                ts.then_inc(S["xn_ready"], 1)

            def take_low(g):
                dve.wait_ge(S["xT_out"], g + 1)
                nc.vector.tensor_tensor(xtl[:], ptr[:, 0, 0:CH], xth[:, 0, :].bitcast(F32), ALU.subtract)
                nc.vector.tensor_tensor(xth[64:128, 1, :], ptr[64:128, 1, 0:CH], xth[64:128, 1, :].bitcast(F32),
                                        ALU.subtract).then_inc(S["xL_out"], 1)

            def softmax_head(g, first=False):
                logit = plg[:].rearrange("p (q e) -> p q e", q=TPC)
                if not first:
                    dve.wait_ge(S["gates_out"], g)
                dve.wait_ge(S["lg_mm"], g + 1)
                nc.vector.tensor_reduce(small[:, :, 0], logit, AX.X, ALU.max).then_inc(S["mx_out"], 1)
                dve.wait_ge(S["mx_out"], g + 1)
                nc.vector.tensor_tensor(lg[:], logit, small[:].broadcast_to([T, TPC, E]),
                                        ALU.subtract).then_inc(S["lg_out"], 1)

            def top2(g, first):
                step = [g * CHAIN]

                def link(ins):
                    step[0] = step[0] + 1
                    ins.then_inc(S["dvec"], 1)
                    dve.wait_ge(S["dvec"], step[0])

                dve.wait_ge(S["lg_out"], g + 1)
                dve.wait_ge(S["ex_out"], g + 1)
                link(nc.vector.tensor_reduce(small[:, :, 0], ex[:], AX.X, ALU.add))
                link(nc.vector.reciprocal(small[:], small[:]))
                link(nc.vector.tensor_tensor(ex[:], ex[:], small[:].broadcast_to([T, TPC, E]), ALU.mult))
                pe_ = ex[:].unsqueeze(3).broadcast_to([T, TPC, E, E])
                pj = ex[:].unsqueeze(2).broadcast_to([T, TPC, E, E])
                nc.vector.tensor_tensor(gt[:].rearrange("p (q e) j -> p q e j", q=TPC), pj, pe_, ALU.is_gt)
                link(nc.vector.tensor_tensor(eq[:].rearrange("p (q e) j -> p q e j", q=TPC), pj, pe_, ALU.is_equal))
                link(nc.vector.tensor_tensor(eq[:].rearrange("p (q e) j -> p q (e j)", q=TPC),
                                             eq[:].rearrange("p (q e) j -> p q (e j)", q=TPC),
                                             tri[:].rearrange("p e j -> p (e j)").unsqueeze(1).broadcast_to(
                                                 [T, TPC, E * E]), ALU.mult))
                link(nc.vector.tensor_tensor(gt[:], gt[:], eq[:], ALU.add))
                link(nc.vector.tensor_reduce(lg[:].rearrange("p q e -> p (q e)"), gt[:], AX.X, ALU.add))
                link(nc.vector.scalar_tensor_tensor(ex[:], lg[:], 2.0, ex[:], ALU.is_lt, ALU.mult))
                link(nc.vector.tensor_reduce(small[:, :, 0], ex[:], AX.X, ALU.add))
                link(nc.vector.tensor_scalar(small[:], small[:], 1e-8, None, ALU.add))
                link(nc.vector.reciprocal(small[:], small[:]))
                nc.vector.tensor_tensor(gates[:], ex[:], small[:].broadcast_to([T, TPC, E]),
                                        ALU.mult).then_inc(S["gates_out"], 1)
                dve.wait_ge(S["gates_out"], g + 1)

            def combine(g, e, pair):
                if e >= 1:
                    dve.wait_ge(S["acc_out"], 2 * (g * E + e) + pair)
                dve.wait_ge(S["up_mm"], 2 * (g * E + e) + 1 + pair)
                for i in range(2):
                    q = 2 * pair + i
                    src = xn[:, q, 0:D] if e <= 2 else acc[:, q, :]
                    dst = xn[:, q, 0:D] if e < 2 else acc[:, q, :]
                    st = nc.vector.scalar_tensor_tensor(dst, py[:, pair, i * D:(i + 1) * D],
                                                        gates[:, q, e:e + 1], src, ALU.mult, ALU.add)
                st.then_inc(S["acc_out"], 1)

            def stat(g):
                dve.wait_ge(S["acc_out"], 2 * E * (g + 1))
                for q in range(TPC):
                    bs = nc.vector.bn_stats(bn[:, q, :], acc[:, q, :])
                bs.then_inc(S["stat_out"], 1)

            def aggregate(g):
                for q in range(TPC):
                    ag = nc.vector.bn_aggr(agg[:, q, :], bn[:, q, :])
                ag.then_inc(S["agg_out"], 1)

            def norm_out(g):
                dve.wait_ge(S["rst_out"], g + 1)
                for q in range(TPC):
                    ts = nc.vector.tensor_scalar(yf[:, q, :], acc[:, q, :], agg[:, q, 0:1], rst[:, q:q + 1],
                                                 ALU.subtract, ALU.mult)
                ts.then_inc(S["nrm_out"], 1)

            def add_out(g):
                dve.wait_ge(S["yf_out"], g + 1)
                hs = h[:, bass.ds(g * TPC, TPC), :]
                nc.vector.tensor_tensor(hs, hs, yf[:], ALU.add).then_inc(S["h_out"], 1)

            def take_stats(g):
                for q in range(TPC):
                    nc.vector.bn_stats(bns[:, g * TPC + q, :], h[:, g * TPC + q, :])

            def chunk(g, first=False, last=False):
                top2(g, first)
                combine(g, 0, 0)
                combine(g, 0, 1)
                if not first:
                    stat(g - 1)
                    dve.wait_ge(S["stat_out"], g)
                combine(g, 1, 0)
                if not first:
                    aggregate(g - 1)
                combine(g, 1, 1)
                if not first:
                    norm_out(g - 1)
                    dve.wait_ge(S["nrm_out"], g)
                combine(g, 2, 0)
                combine(g, 2, 1)
                if not last:
                    dve.wait_ge(S["acc_out"], 2 * g * E + 6)
                    normalise(g + 1)
                for e in (3, 4, 5):
                    combine(g, e, 0)
                    combine(g, e, 1)
                if not first:
                    add_out(g - 1)
                    dve.wait_ge(S["h_out"], g)
                combine(g, 6, 0)
                if not last:
                    take_low(g + 1)
                combine(g, 6, 1)
                if not first:
                    take_stats(g - 1)
                if not last:
                    softmax_head(g + 1)
                combine(g, 7, 0)
                combine(g, 7, 1)

            def split_low(n):
                high, low, src = pieces[n]
                dve.wait_ge(S["high"], n + 1)
                nc.vector.tensor_tensor(low, src, high.bitcast(F32), ALU.subtract).then_inc(S["split"], 1)

            normalise(0)
            split_low(0)
            take_low(0)
            for n in range(1, 5):
                split_low(n)
            softmax_head(0, first=True)
            chunk(0, first=True)
            with dve.Fori(1, NC - 1) as g:
                chunk(g)
            chunk(NC - 1, last=True)
            stat(NC - 1)
            dve.wait_ge(S["stat_out"], NC)
            aggregate(NC - 1)
            norm_out(NC - 1)
            add_out(NC - 1)
            dve.wait_ge(S["h_out"], NC)
            take_stats(NC - 1)


def linear_attention_phase(nc, ins, h, bns, mean, rstd, eye):
    RB = D - 128
    COLS = (slice(0, 128), slice(128, D))
    ROWS = (128, RB)
    with ExitStack() as ctx:
        sb, ps, sem = allocator(nc, ctx)
        wT = sb("wT4", [128, 2, 3 * D])
        wh = sb("wh4", [128, 2, 2 * D], F32R)
        wl = sb("wl4", [128, 2, 2 * D], F32R)
        wq = sb("wq4", [128, 2, D])
        wpT = sb("wpT4", [128, 2, D])
        heads = sb("heads4", [128, 128])
        xn = [sb(f"xn4_{i}", [T, TPC, 256]) for i in range(2)]
        xTA = sb("xTA4", [128, TOK])
        xTB = sb("xTB4", [RB + 1, TOK])
        xh = sb("xh4", [128, 2, CH], F32R)
        xl = sb("xl4", [128, CH], F32R)
        junk = sb("junk4", [128, CH])
        sums = sb("sums4", [128, 3, CPI])
        nrm = sb("nrm4", [128, 3])
        knrm = sb("knrm4", [RB, 1])
        spare = sb("spare4", [RB, 1])
        scale = sb("scale4", [128, 2])
        gsb = sb("gsb4", [128, 2, D])
        t2 = sb("t2_4", [128, 2, D])
        kvT = [sb(f"kvT4_{i}", [r, r]) for i, r in enumerate(ROWS)]
        m1 = sb("m1_4", [128, 2, D])
        wimg = sb("wimg4", [128, 2, D])
        ptr = ps("ptr4", [128, 2, 512])
        pqk = [ps(f"pqk4_{i}", [128, 512]) for i in range(2)]
        pg = [ps(f"pg4_{i}", [128, 512]) for i in range(2)]
        po = ps("po4", [T, 2, 512])
        names = ("w_in", "w_ready", "xn_ready", "xtr_mm", "xH_out", "xL_out", "xT_out", "qk_mm", "b_sum", "a_sum",
                 "g_mm", "g_out", "gt_mm", "gt_out", "t2_mm", "t2_out", "kv_mm", "kv_out", "m1_mm", "m1_out",
                 "wi_mm", "wi_out", "o_mm", "h_out", "dvec", "split")
        S = {n: sem(f"{n}_4") for n in names}
        block = ctx.enter_context(nc.Block())
        NW = 5
        PAIRS = TPI // 2

        @block.sync
        def _(sp):
            for dst, name in ((wT[:], "wT4"), (wq[:], "wq4"), (wpT[:], "wpT4"), (heads[:], "heads"),
                              (wimg[RB:RB + 1, 1, :], "bproj4")):
                sp.dma_start(dst, ins[name]).then_inc(S["w_in"], 16)

        @block.gpsimd
        def _(pool):
            nc.gpsimd.memset(xTB[RB:RB + 1], 1.0).then_inc(S["w_ready"], 1)

        @block.tensor
        def _(pe):
            pe.wait_ge(S["w_in"], 16 * NW)
            pe.wait_ge(S["w_ready"], 1)

            def gather(g, c):
                pe.wait_ge(S["xn_ready"], g + 1)
                if c or not isinstance(g, int):
                    pe.wait_ge(S["xT_out"], g)
                    pe.wait_ge(S["xL_out"], g)
                for q in range(TPC):
                    for i in range(2):
                        mm = pe.transpose(ptr[:, i, q * T:(q + 1) * T], xn[c % 2][:, q, i * 128:(i + 1) * 128],
                                          eye[0:T, 0:T])
                mm.then_inc(S["xtr_mm"], 1)
                for q in range(TPC):
                    for i in range(2):
                        mm = pe.matmul(pg[i][0:ROWS[i], 0:(D, RB)[i]], xn[c % 2][:, q, COLS[i]],
                                       xn[c % 2][:, q, (0, 128)[i]:D], start=(c == 0 and q == 0),
                                       stop=(c == CPI - 1 and q == TPC - 1), skip_group_check=True)
                mm.then_inc(S["g_mm"], 1)

            def q_and_k(g, c):
                first = isinstance(g, int) and g == 0
                for m in range(3):
                    if m == 0:
                        pe.wait_ge(S["xL_out"], g + 1)
                    if m == 0 and not first:
                        pe.wait_ge(S["a_sum"], 2 * g)
                    elif m == 1 and not first:
                        pe.wait_ge(S["b_sum"], g)
                    elif m == 2:
                        pe.wait_ge(S["a_sum"], 2 * g + 1)
                    cols = slice(m * 128, (m + 1) * 128)
                    steps = ((wh[:, 0, cols], xh[:, 0, :]), (wh[:, 0, cols], xl[:]), (wl[:, 0, cols], xh[:, 0, :]),
                             (wh[:, 1, cols], xh[:, 1, :]), (wl[0:64, 1, cols], xh[0:64, 1, :]))
                    for n, (w, x) in enumerate(steps):
                        mm = pe.matmul(pqk[m % 2][:, 0:CH], w, x, start=(n == 0), stop=(n == 4))
                    mm.then_inc(S["qk_mm"], 1)

            def map_out(b, c):
                for r in range(2):
                    n = b * PAIRS + 2 * c + r
                    pe.wait_ge(S["h_out"], n + 1)
                    for i in range(2):
                        ts = slice((4 * c + 2 * r + i) * T, (4 * c + 2 * r + i + 1) * T)
                        dst = po[:, r, i * D:(i + 1) * D]
                        pe.matmul(dst, xTA[:, ts], wimg[:, 0, :], start=True, stop=False, skip_group_check=True)
                        mm = pe.matmul(dst, xTB[:, ts], wimg[0:RB + 1, 1, :], start=False, stop=True,
                                       skip_group_check=True)
                    mm.then_inc(S["o_mm"], 1)

            def solve(b):
                pe.wait_ge(S["g_out"], b + 1)
                pe.transpose(pg[1][:, 256:384], gsb[:, 0, D - 128:D], eye[:]).then_inc(S["gt_mm"], 1)
                pe.wait_ge(S["a_sum"], 2 * CPI * (b + 1))
                pe.wait_ge(S["b_sum"], CPI * (b + 1))
                pe.wait_ge(S["gt_out"], b + 1)
                for i in range(2):
                    for c, k in enumerate(ROWS):
                        mm = pe.matmul(pqk[i][0:ROWS[i], 0:D], gsb[0:k, c, COLS[i]], wT[0:k, c, D:2 * D],
                                       start=(c == 0), stop=(c == 1))
                mm.then_inc(S["t2_mm"], 1)
                pe.wait_ge(S["t2_out"], b + 1)
                for i in range(2):
                    for c, k in enumerate(ROWS):
                        v = slice(2 * D + COLS[i].start, 2 * D + COLS[i].stop)
                        mm = pe.matmul(pg[i][0:ROWS[i], 0:ROWS[i]], wT[0:k, c, v], t2[0:k, c, COLS[i]],
                                       start=(c == 0), stop=(c == 1))
                mm.then_inc(S["kv_mm"], 1)
                pe.wait_ge(S["kv_out"], b + 1)
                for i, k in enumerate(ROWS):
                    mm = pe.matmul(pqk[i][0:k, 0:D], kvT[i][:], wpT[0:k, i, :], start=True, stop=True)
                mm.then_inc(S["m1_mm"], 1)
                pe.wait_ge(S["m1_out"], b + 1)
                for i in range(2):
                    for c, k in enumerate(ROWS):
                        mm = pe.matmul(pg[i][0:ROWS[i], 0:D], wq[0:k, c, COLS[i]], m1[0:k, c, :],
                                       start=(c == 0), stop=(c == 1))
                mm.then_inc(S["wi_mm"], 1)
                pe.wait_ge(S["wi_out"], b + 1)

            def image(b, first=False):
                for c in range(CPI):
                    gather(b * CPI + c, c)
                    if not first:
                        map_out(b - 1, c)
                    if first and c == 0:
                        pe.wait_ge(S["split"], 4)
                    q_and_k(b * CPI + c, c)
                solve(b)

            image(0, first=True)
            with pe.Fori(1, B) as b:
                image(b)
            for c in range(CPI):
                map_out(B - 1, c)

        @block.scalar
        def _(act):
            act.wait_ge(S["w_in"], 16 * NW)
            nc.scalar.preload_act_table(ACT.Abs)

            def image(b, first=False):
                for c in range(CPI):
                    g = b * CPI + c
                    act.wait_ge(S["xtr_mm"], g + 1)
                    nc.scalar.copy(xh[:, :, :], ptr[:, :, 0:CH]).then_inc(S["xH_out"], 1)
                    if not first:
                        act.wait_ge(S["o_mm"], (b - 1) * PAIRS + 2 * c + 2)
                    act.wait_ge(S["xL_out"], g + 1)
                    nc.scalar.copy(xTA[:, c * CH:(c + 1) * CH], ptr[:, 0, 0:CH])
                    nc.scalar.copy(xTB[0:RB, c * CH:(c + 1) * CH], ptr[0:RB, 1, 0:CH]).then_inc(S["xT_out"], 1)
                    for m in (0, 2):
                        act.wait_ge(S["qk_mm"], 3 * g + m + 1)
                        if not (first and c == 0 and m == 0):
                            act.wait_ge(S["a_sum"], 2 * g + m // 2)
                        nc.scalar.activation(junk[:], pqk[0][:, 0:CH], ACT.Abs,
                                             accum_out=sums[:, m, c:c + 1]).then_inc(S["a_sum"], 1)
                act.wait_ge(S["g_mm"], CPI * (b + 1))
                nc.scalar.copy(gsb[:, 0, :], pg[0][:, 0:D])
                nc.scalar.copy(gsb[0:RB, 1, 128:D], pg[1][0:RB, 0:RB]).then_inc(S["g_out"], 1)

            image(0, first=True)
            with act.Fori(1, B) as b:
                image(b)

        @block.vector
        def _(dve):

            def normalise(g, c):
                if c >= 2:
                    dve.wait_ge(S["g_mm"], g - 1)
                for cols, src in ((slice(0, D), slice(0, D)), (slice(D, 256), slice(128, D))):
                    for q in range(TPC):
                        t = g * TPC + q
                        ts = nc.vector.tensor_scalar(xn[c % 2][:, q, cols], h[:, t, src],
                                                     mean[:, bass.ds(t, 1)], rstd[:, bass.ds(t, 1)],
                                                     ALU.subtract, ALU.mult)
                ts.then_inc(S["xn_ready"], 1)

            def low(g):
                dve.wait_ge(S["xH_out"], g + 1)
                nc.vector.tensor_tensor(xl[:], ptr[:, 0, 0:CH], xh[:, 0, :].bitcast(F32), ALU.subtract)
                nc.vector.tensor_tensor(xh[64:128, 1, :], ptr[64:128, 1, 0:CH], xh[64:128, 1, :].bitcast(F32),
                                        ALU.subtract).then_inc(S["xL_out"], 1)

            def stats_of(t):
                for q in range(2):
                    nc.vector.bn_stats(bns[:, t + q, :], h[:, t + q, :])

            def add_out(b, c):
                for r in range(2):
                    n = b * PAIRS + 2 * c + r
                    if c or r:
                        dve.wait_ge(S["h_out"], n + 2)
                    dve.wait_ge(S["o_mm"], n + 1)
                    two = h[:, bass.ds(2 * n, 2), :]
                    nc.vector.tensor_tensor(two, two, po[:, r, 0:2 * D].rearrange("p (q d) -> p q d", q=2),
                                            ALU.add).then_inc(S["h_out"], 1)
                    if c or r:
                        stats_of(2 * n - 2)

            def last_stats(b):
                dve.wait_ge(S["h_out"], PAIRS * (b + 1) + 2)
                nc.vector.tensor_copy(spare[:], eye[0:RB, 0:1])
                stats_of(b * TPI + TPI - 2)

            def solve(b):
                dve.wait_ge(S["b_sum"], CPI * (b + 1))
                dve.wait_ge(S["a_sum"], 2 * CPI * (b + 1))
                step = [4 * b]

                def link(ins):
                    step[0] = step[0] + 1
                    ins.then_inc(S["dvec"], 1)
                    dve.wait_ge(S["dvec"], step[0])

                link(nc.vector.tensor_reduce(nrm[:], sums[:], AX.X, ALU.add))
                link(nc.vector.tensor_scalar(nrm[:], nrm[:], 1e-12, None, ALU.max))
                link(nc.vector.reciprocal(nrm[:], nrm[:]))
                dve.wait_ge(S["gt_mm"], b + 1)
                nc.vector.tensor_copy(gsb[0:RB, 1, 0:128], pg[1][128 - RB:128, 256:384]).then_inc(S["gt_out"], 1)
                nc.vector.tensor_tensor(scale[:, 0:1], nrm[:, 0:1], nrm[:, 2:3], ALU.mult)
                link(nc.vector.tensor_copy(knrm[:], nrm[64:128, 1:2]))
                nc.vector.tensor_tensor(scale[0:RB, 1:2], nrm[0:RB, 1:2], knrm[:], ALU.mult)
                dve.wait_ge(S["t2_mm"], b + 1)
                for i, r in enumerate(ROWS):
                    cp = nc.vector.tensor_copy(t2[0:r, i, :], pqk[i][0:r, 0:D])
                cp.then_inc(S["t2_out"], 1)
                dve.wait_ge(S["kv_mm"], b + 1)
                for i, r in enumerate(ROWS):
                    tt = nc.vector.tensor_tensor(kvT[i][:], pg[i][0:r, 0:r], heads[0:r, 0:r], ALU.mult)
                tt.then_inc(S["kv_out"], 1)
                dve.wait_ge(S["m1_mm"], b + 1)
                for i, r in enumerate(ROWS):
                    ts = nc.vector.tensor_scalar(m1[0:r, i, :], pqk[i][0:r, 0:D], scale[0:r, i:i + 1], None, ALU.mult)
                ts.then_inc(S["m1_out"], 1)
                dve.wait_ge(S["wi_mm"], b + 1)
                for i, r in enumerate(ROWS):
                    cp = nc.vector.tensor_copy(wimg[0:r, i, :], pg[i][0:r, 0:D])
                cp.then_inc(S["wi_out"], 1)

            def image(b, first=False, last=False):
                for c in range(CPI):
                    g = b * CPI + c
                    if c + 1 < CPI:
                        normalise(g + 1, c + 1)
                    low(g)
                    if not first:
                        add_out(b - 1, c)
                    dve.wait_ge(S["qk_mm"], 3 * g + 2)
                    nc.vector.tensor_reduce(sums[:, 1, c:c + 1], pqk[1][:, 0:CH], AX.X, ALU.add,
                                            apply_absolute_value=True).then_inc(S["b_sum"], 1)
                if not first:
                    last_stats(b - 1)
                if not last:
                    dve.wait_ge(S["g_mm"], (b + 1) * CPI)
                    normalise((b + 1) * CPI, 0)
                solve(b)

            dve.sem_inc(S["h_out"], 2)
            normalise(0, 0)
            dve.wait_ge(S["w_in"], 16 * NW)
            for dst, src in ((slice(0, D), slice(0, D)), (slice(D, 256), slice(D + 128, 2 * D)),
                             (slice(256, 2 * D), slice(D, D + 128))):
                nc.vector.tensor_copy(wh[:, :, dst], wT[:, :, src]).then_inc(S["split"], 1)
            dve.wait_ge(S["split"], 3)
            for dst, src in ((slice(0, D), slice(0, D)), (slice(D, 256), slice(D + 128, 2 * D)),
                             (slice(256, 2 * D), slice(D, D + 128))):
                tt = nc.vector.tensor_tensor(wl[:, :, dst], wT[:, :, src], wh[:, :, dst].bitcast(F32), ALU.subtract)
            tt.then_inc(S["split"], 1)
            image(0, first=True)
            with dve.Fori(1, B - 1) as b:
                image(b)
            image(B - 1, last=True)
            for c in range(CPI):
                add_out(B - 1, c)
            last_stats(B - 1)


def bit_ffn_phase(nc, ins, h, bns, mean, rstd, var, eye, out):
    HID = 512
    MAGIC = 12582912.0
    with ExitStack() as ctx:
        sb, ps, sem = allocator(nc, ctx)
        win = sb("win5", [KC, 2, 2 * HID])
        wout = sb("wout5", [128, 4, D])
        winq = sb("winq5", [KC, 2, 2 * HID], BF16)
        woutq = sb("woutq5", [128, 4, D], BF16)
        gin = sb("gin5", [T, D])
        gout = sb("gout5", [T, HID])
        ones = sb("ones5", [128, 128])
        eyeb = sb("eyeb5", [128, 128], BF16)
        wsum = sb("wsum5", [128, 4])
        wsc = sb("wsc5", [128, 4])
        mhalf = sb("mhalf5", [T, TPC])
        fac = sb("fac5", [T, NT])
        tmp = sb("tmp5", [T, NT])
        root = sb("root5", [T, NT])
        tmp2 = sb("tmp2_5", [T, NT])
        xg = sb("xg5", [T, TPC, D])
        xr = sb("xr5", [T, TPC, D])
        xq = sb("xq5", [T, TPC, D], BF16)
        xT = sb("xT5", [KC, 2, CH], BF16)
        am = sb("am5", [T, TPC])
        sx = sb("sx5", [T, TPC])
        dx = sb("dx5", [T, TPC])
        sg = [sb(f"sg5_{i}", [T, HID]) for i in range(2)]
        junk = sb("junk5", [T, HID])
        y = sb("y5", [T, TPC, HID])
        yg = sb("yg5", [T, TPC, HID])
        yr = sb("yr5", [T, TPC, HID])
        yq = sb("yq5", [T, TPC, HID], BF16)
        yT = sb("yT5", [128, 4, CH], BF16)
        ssq = sb("ssq5", [T, TPC])
        am2 = sb("am2_5", [T, TPC])
        ms2 = sb("ms2_5", [T, TPC])
        r2 = sb("r2_5", [T, TPC])
        s2 = sb("s2_5", [T, TPC])
        d2 = sb("d2_5", [T, TPC])
        ho = sb("ho5", [T, TPC, D])
        pxt = ps("pxt5", [KC, 2, CH], BF16)
        pyt = ps("pyt5", [128, 2, 1024], BF16)
        pup = [ps(f"pup5_{i}", [128, 512]) for i in range(2)]
        pga = [ps(f"pga5_{i}", [128, 512]) for i in range(2)]
        po = ps("po5", [T, 512])
        names = ("w_in", "w_ready", "wc", "wsum_mm", "xq_out", "xtr_mm", "xT_out", "in_mm", "sg_out", "y_out", "yg_out",
                 "ssq_out", "r2_in", "r2_out", "gin_in", "yq_out", "ytr_mm", "yT_out", "o_mm", "o_out", "stored", "dvec",
                 "dvec2", "fac_in", "fac_out", "poolc", "d2_out", "xr_out", "yr_out")
        S = {n: sem(f"{n}_5") for n in names}
        block = ctx.enter_context(nc.Block())
        NW = 3
        out_t = out.rearrange("b (t p) d -> p (b t) d", p=T)

        @block.sync
        def _(sp):
            sp.dma_start(gin[:], ins["gin5"]).then_inc(S["gin_in"], 16)
            for dst, name in ((win[:], "win5"), (wout[:], "wout5"), (gout[:], "gout5")):
                sp.dma_start(dst, ins[name]).then_inc(S["w_in"], 16)

            def store(g):
                sp.wait_ge(S["o_out"], 2 * g + 2)
                sp.dma_start(out_t[:, bass.ds(g * TPC, TPC), :], ho[:]).then_inc(S["stored"], 16)

            with sp.Fori(0, NC) as g:
                store(g)
            sp.wait_ge(S["stored"], 16 * NC)

        @block.gpsimd
        def _(pool):
            nc.gpsimd.memset(ones[:], 1.0).then_inc(S["w_ready"], 1)
            pool.wait_ge(S["w_ready"], 1)
            nc.gpsimd.memset(mhalf[:], -0.5).then_inc(S["w_ready"], 1)
            pool.wait_ge(S["w_ready"], 2)
            pool.wait_ge(S["w_in"], 16 * NW)

            def chunk(g, first=False):
                for q in range(TPC):
                    if q == 0 and not first:
                        pool.wait_ge(S["r2_out"], g)
                        pool.wait_ge(S["yr_out"], g)
                    elif q:
                        pool.wait_ge(S["yg_out"], g * TPC + q)
                    pool.wait_ge(S["y_out"], g * TPC + q + 1)
                    nc.gpsimd.tensor_tensor(yg[:, q, :], y[:, q, :], gout[:], ALU.mult).then_inc(S["yg_out"], 1)
                pool.wait_ge(S["yg_out"], (g + 1) * TPC)
                pool.wait_ge(S["r2_in"], g + 1)
                nc.gpsimd.tensor_tensor(r2[:], ms2[:], mhalf[:], ALU.pow).then_inc(S["r2_out"], 1)

            chunk(0, first=True)
            with pool.Fori(1, NC) as g:
                chunk(g)

        @block.tensor
        def _(pe):
            pe.wait_ge(S["w_ready"], 2)
            pe.wait_ge(S["wc"], 1)
            pe.matmul(pup[0][:, 0:1], ones[:], wsum[:, 1:2], start=True, stop=True)
            pe.matmul(pga[0][:, 0:1], ones[:], wsum[:, 0:1], start=True, stop=True).then_inc(
                S["wsum_mm"], 1)
            pe.wait_ge(S["w_ready"], 2 + 3)

            def transpose_in(g):
                pe.wait_ge(S["xq_out"], g + 1)
                for q in range(TPC):
                    for c in range(2):
                        mm = pe.transpose(pxt[:, c, q * T:(q + 1) * T], xq[:, q, c * KC:(c + 1) * KC], eyeb[0:T, 0:T])
                mm.then_inc(S["xtr_mm"], 1)

            def into(g, q, first=False):
                if not first:
                    pe.wait_ge(S["y_out"], g * TPC + q - 1)
                for dst, o in ((pga, HID), (pup, 0)):
                    for c in range(2):
                        mm = pe.matmul(dst[q % 2][0:T], xT[:, c, q * T:(q + 1) * T], winq[:, c, o:o + HID],
                                       start=(c == 0), stop=(c == 1))
                mm.then_inc(S["in_mm"], 1)

            def transpose_y(g):
                pe.wait_ge(S["yq_out"], 2 * g + 2)
                for half in range(2):
                    for k in range(2):
                        for q in range(TPC):
                            mm = pe.transpose(pyt[:, half, k * CH + q * T:k * CH + (q + 1) * T],
                                              yq[:, q, (2 * half + k) * 128:(2 * half + k + 1) * 128], eyeb[0:T, 0:T])
                    mm.then_inc(S["ytr_mm"], 1)

            def enter(g, first=False):
                pe.wait_ge(S["xT_out"], g + 1)
                into(g, 0, first)
                into(g, 1, first)

            def outof(g, pair):
                if pair or not isinstance(g, int) or g > 0:
                    pe.wait_ge(S["o_out"], 2 * g + pair)
                pe.wait_ge(S["yT_out"], 2 * g + 2)
                for i in range(2):
                    q = 2 * pair + i
                    for k in range(4):
                        mm = pe.matmul(po[:, i * D:(i + 1) * D], yT[:, k, q * T:(q + 1) * T], woutq[:, k, :],
                                       start=(k == 0), stop=(k == 3), skip_group_check=True)
                mm.then_inc(S["o_mm"], 1)

            def step(g, first=False, last=False):
                into(g, 2)
                into(g, 3)
                if not first:
                    transpose_y(g - 1)
                    outof(g - 1, 0)
                if not last:
                    transpose_in(g + 1)
                if not first:
                    outof(g - 1, 1)
                if not last:
                    enter(g + 1)

            transpose_in(0)
            enter(0, first=True)
            step(0, first=True)
            with pe.Fori(1, NC - 1) as g:
                step(g)
            step(NC - 1, last=True)
            transpose_y(NC - 1)
            outof(NC - 1, 0)
            outof(NC - 1, 1)

        @block.scalar
        def _(act):
            act.wait_ge(S["fac_in"], 1)
            nc.scalar.activation(root[:], tmp[:], ACT.Sqrt).then_inc(S["fac_out"], 1)
            nc.scalar.preload_act_table(ACT.Silu)
            act.wait_ge(S["w_ready"], 2 + 3)

            def take_x(g):
                act.wait_ge(S["xtr_mm"], g + 1)
                nc.scalar.copy(xT[:, :, :], pxt[:, :, :]).then_inc(S["xT_out"], 1)

            def silu(g, q):
                act.wait_ge(S["in_mm"], g * TPC + q + 1)
                nc.scalar.activation(sg[q % 2][:], pga[q % 2][0:T], ACT.Silu, scale=dx[:, q:q + 1]).then_inc(
                    S["sg_out"], 1)

            def squares(g, q, first=False):
                if q or not first:
                    act.wait_ge(S["ssq_out"], g * TPC + q)
                if q == 0 and not first:
                    act.wait_ge(S["r2_in"], g)
                act.wait_ge(S["y_out"], g * TPC + q + 1)
                nc.scalar.activation(junk[:], y[:, q, :], ACT.Square, accum_out=ssq[:, q:q + 1]).then_inc(
                    S["ssq_out"], 1)

            def whole_y(g, pair):
                act.wait_ge(S["yr_out"], g + 1)
                nc.scalar.activation(yq[:, 2 * pair:2 * pair + 2, :], yr[:, 2 * pair:2 * pair + 2, :],
                                     ACT.Copy, bias=-MAGIC).then_inc(S["yq_out"], 1)

            def take_y(g):
                for half in range(2):
                    act.wait_ge(S["ytr_mm"], 2 * g + half + 1)
                    nc.scalar.copy(yT[:, 2 * half:2 * half + 2, :],
                                   pyt[:, half, 0:2 * CH].rearrange("p (k c) -> p k c", k=2)).then_inc(S["yT_out"], 1)

            def step(g, first=False, last=False):
                if not first:
                    whole_y(g - 1, 0)
                silu(g, 2)
                if not first:
                    whole_y(g - 1, 1)
                silu(g, 3)
                for q in (0, 1):
                    squares(g, q, first)
                if not first:
                    take_y(g - 1)
                for q in (2, 3):
                    squares(g, q)
                if not last:
                    take_x(g + 1)
                    silu(g + 1, 0)
                    silu(g + 1, 1)

            take_x(0)
            silu(0, 0)
            silu(0, 1)
            step(0, first=True)
            with act.Fori(1, NC - 1) as g:
                step(g)
            step(NC - 1, last=True)
            whole_y(NC - 1, 0)
            whole_y(NC - 1, 1)
            take_y(NC - 1)

        @block.vector
        def _(dve):
            L1, L2 = 6, 5

            def weigh_in(g):
                for q in range(TPC):
                    t = g * TPC + q
                    ins_ = nc.vector.scalar_tensor_tensor(xg[:, q, :], h[:, t, :], mean[:, bass.ds(t, 1)], gin[:],
                                                          ALU.subtract, ALU.mult)
                ins_.then_inc(S["poolc"], 1)

            def largest_in(g):
                dve.wait_ge(S["poolc"], g * L1 + 1)
                nc.vector.tensor_reduce(am[:], xg[:], AX.X, ALU.max, apply_absolute_value=True).then_inc(S["poolc"], 1)

            step = [0]

            def link(ins):
                step[0] = step[0] + 1
                ins.then_inc(S["dvec"], 1)
                dve.wait_ge(S["dvec"], step[0])

            dve.wait_ge(S["w_ready"], 2)
            link(nc.vector.tensor_tensor(tmp[:], var[:], rstd[:], ALU.mult))
            link(nc.vector.tensor_tensor(tmp[:], tmp[:], rstd[:], ALU.mult))
            link(nc.vector.tensor_scalar(tmp[:], tmp[:], 1e-6, None, ALU.add))
            dve.sem_inc(S["fac_in"], 1)
            dve.wait_ge(S["fac_out"], 1)
            link(inverse_root(nc, dve, link, fac[:], tmp[:], root[:], tmp2[:]))
            nc.vector.tensor_tensor(fac[:], fac[:], rstd[:], ALU.mult).then_inc(S["w_ready"], 1)
            dve.wait_ge(S["gin_in"], 16)
            weigh_in(0)
            largest_in(0)
            dve.wait_ge(S["w_in"], 16 * NW)
            link(nc.vector.memset(wsum[:], 0.0))
            link(nc.vector.tensor_reduce(wsum[0:KC, 0:1], win[:], AX.XY, ALU.add, apply_absolute_value=True))
            nc.vector.tensor_reduce(wsum[:, 1:2], wout[:], AX.XY, ALU.add, apply_absolute_value=True).then_inc(S["wc"], 1)
            link(nc.vector.tensor_copy(eyeb[:], eye[:]))
            dve.wait_ge(S["wsum_mm"], 1)
            nc.vector.tensor_scalar(wsc[:, 0:1], pga[0][:, 0:1], 1.0 / (2 * HID * D), 1e-5, ALU.mult, ALU.max)
            link(nc.vector.tensor_scalar(wsc[:, 1:2], pup[0][:, 0:1], 1.0 / (HID * D), 1e-5, ALU.mult, ALU.max))
            link(nc.vector.reciprocal(wsc[:, 2:4], wsc[:, 0:2]))
            link(nc.vector.tensor_scalar(win[:], win[:], wsc[0:KC, 2:3], MAGIC, ALU.mult, ALU.add))
            link(nc.vector.tensor_scalar(win[:], win[:], MAGIC, 1.0, ALU.subtract, ALU.min))
            nc.vector.tensor_scalar(winq[:], win[:], -1.0, None, ALU.max).then_inc(S["w_ready"], 1)
            link(nc.vector.tensor_scalar(wout[:], wout[:], wsc[:, 3:4], MAGIC, ALU.mult, ALU.add))
            link(nc.vector.tensor_scalar(wout[:], wout[:], MAGIC, 1.0, ALU.subtract, ALU.min))
            nc.vector.tensor_scalar(woutq[:], wout[:], -1.0, None, ALU.max).then_inc(S["w_ready"], 1)
            dve.wait_ge(S["w_ready"], 5)

            def quant_in(g):
                st = [g * L1 + 2]

                def link(ins):
                    st[0] = st[0] + 1
                    ins.then_inc(S["poolc"], 1)
                    dve.wait_ge(S["poolc"], st[0])

                dve.wait_ge(S["poolc"], g * L1 + 2)
                link(nc.vector.tensor_tensor(am[:], am[:], fac[:, bass.ds(g * TPC, TPC)], ALU.mult))
                link(nc.vector.tensor_scalar(am[:], am[:], 1e-5, 1.0 / 127, ALU.max, ALU.mult))
                nc.vector.tensor_scalar(dx[:], am[:], wsc[0:T, 0:1], None, ALU.mult)
                link(nc.vector.reciprocal(sx[:], am[:]))
                link(nc.vector.tensor_tensor(sx[:], sx[:], fac[:, bass.ds(g * TPC, TPC)], ALU.mult))
                for q in range(TPC):
                    ins_ = nc.vector.tensor_scalar(xr[:, q, :], xg[:, q, :], sx[:, q:q + 1], MAGIC, ALU.mult, ALU.add)
                ins_.then_inc(S["xr_out"], 1)
                dve.wait_ge(S["xr_out"], g + 1)
                nc.vector.tensor_scalar(xq[:], xr[:], MAGIC, None, ALU.subtract).then_inc(S["xq_out"], 1)

            def gated(g, q, first=False):
                if not first:
                    dve.wait_ge(S["yg_out"], (g - 1) * TPC + q + 1)
                dve.wait_ge(S["sg_out"], g * TPC + q + 1)
                nc.vector.scalar_tensor_tensor(y[:, q, :], pup[q % 2][0:T], dx[:, q:q + 1], sg[q % 2][:],
                                               ALU.mult, ALU.mult).then_inc(S["y_out"], 1)

            def mean_square(g):
                dve.wait_ge(S["ssq_out"], (g + 1) * TPC)
                nc.vector.tensor_scalar(ms2[:], ssq[:], 1.0 / HID, 1e-6, ALU.mult, ALU.add).then_inc(S["r2_in"], 1)

            def largest_y(g, pair):
                dve.wait_ge(S["yg_out"], g * TPC + 2 * pair + 2)
                nc.vector.tensor_reduce(am2[:, 2 * pair:2 * pair + 2], yg[:, 2 * pair:2 * pair + 2, :], AX.X, ALU.max,
                                        apply_absolute_value=True)

            def quant_y(g, first=False):
                st = [g * L2]

                def link(ins):
                    st[0] = st[0] + 1
                    ins.then_inc(S["dvec2"], 1)
                    dve.wait_ge(S["dvec2"], st[0])

                largest_y(g, 1)
                if not first:
                    result(g - 1, 1)
                dve.wait_ge(S["r2_out"], g + 1)
                dve.wait_ge(S["r2_in"], g + 1)
                link(nc.vector.tensor_copy(s2[:], r2[:]))
                link(nc.vector.tensor_tensor(am2[:], am2[:], r2[:], ALU.mult))
                if not first:
                    dve.wait_ge(S["o_out"], 2 * g)
                link(nc.vector.tensor_scalar(am2[:], am2[:], 1e-5, 1.0 / 127, ALU.max, ALU.mult))
                link(nc.vector.reciprocal(s2[:], am2[:]))
                nc.vector.tensor_scalar(d2[:], am2[:], wsc[0:T, 1:2], None, ALU.mult).then_inc(S["d2_out"], 1)
                link(nc.vector.tensor_tensor(s2[:], s2[:], r2[:], ALU.mult))
                if not first:
                    dve.wait_ge(S["yq_out"], 2 * g)
                for q in range(TPC):
                    ins_ = nc.vector.tensor_scalar(yr[:, q, :], yg[:, q, :], s2[:, q:q + 1], MAGIC, ALU.mult, ALU.add)
                ins_.then_inc(S["yr_out"], 1)

            def result(g, pair):
                if pair == 0 and (not isinstance(g, int) or g > 0):
                    dve.wait_ge(S["stored"], 16 * g)
                dve.wait_ge(S["d2_out"], g + 1)
                dve.wait_ge(S["o_mm"], 2 * g + pair + 1)
                for i in range(2):
                    q = 2 * pair + i
                    st = nc.vector.scalar_tensor_tensor(ho[:, q, :], po[:, i * D:(i + 1) * D], d2[:, q:q + 1],
                                                        h[:, g * TPC + q, :], ALU.mult, ALU.add)
                st.then_inc(S["o_out"], 1)

            def step(g, first=False, last=False):
                gated(g, 0, first)
                gated(g, 1, first)
                if not last:
                    weigh_in(g + 1)
                gated(g, 2, first)
                if not last:
                    largest_in(g + 1)
                gated(g, 3, first)
                if not last:
                    quant_in(g + 1)
                largest_y(g, 0)
                mean_square(g)
                if not first:
                    result(g - 1, 0)
                quant_y(g, first)

            quant_in(0)
            step(0, first=True)
            with dve.Fori(1, NC - 1) as g:
                step(g)
            step(NC - 1, last=True)
            result(NC - 1, 0)
            result(NC - 1, 1)


def vit_tower(nc, ins, out):
    with ExitStack() as ctx:
        sb, ps, sem = allocator(nc, ctx)
        h = sb("h", [T, NT, D])
        bns = sb("bns", [T, NT, 6])
        eye = sb("eye", [128, 128])
        mean = sb("mean", [T, NT])
        rstd = sb("rstd", [T, NT])
        var = sb("var", [T, NT])
        mixer_phase(nc, ins, h, bns, eye)
        finish_stats(nc, "ln1", bns, mean, rstd, var, 1e-5)
        retention_phase(nc, ins, h, bns, mean, rstd, eye)
        finish_stats(nc, "ln2", bns, mean, rstd, var, 1e-5)
        expert_phase(nc, ins, h, bns, mean, rstd, eye)
        finish_stats(nc, "ln3", bns, mean, rstd, var, 1e-5)
        linear_attention_phase(nc, ins, h, bns, mean, rstd, eye)
        finish_stats(nc, "ln4", bns, mean, rstd, var, 1e-5)
        bit_ffn_phase(nc, ins, h, bns, mean, rstd, var, eye, out)


def kernel(**inputs):
    import numpy as np
    import concourse.bacc as bacc
    from concourse.bass_utils import run_bass_kernel_spmd as run

    f = {k: np.ascontiguousarray(v) for k, v in inputs.items()}
    lay = {}
    x = f["x"].reshape(B, 3, 56, 4, 56, 4).transpose(0, 1, 3, 5, 2, 4).reshape(B, 48, TOK)
    x1 = np.ones((B, X1, TOK), np.float32)
    x1[:, 0:48] = x
    lay["xT"] = x1
    keys = np.zeros((B, KT * 128, LO), np.float32)
    keys[:, 0:TOK, 0:X1] = x1.transpose(0, 2, 1)
    lay["xkey"] = keys.reshape(B, KT, 128, LO).transpose(0, 2, 1, 3)
    conv = np.zeros((D, X1), np.float32)
    conv[:, 0:48] = f["L0_tok_conv_w"].reshape(D, 48)
    conv[:, 48] = f["L0_tok_conv_b"]
    lay["conv"] = conv.reshape(2, KC, X1).transpose(1, 0, 2)
    w = np.stack([f["L0_tok_q_w"].T, f["L0_tok_k_w"].T, f["L0_tok_v_w"].T])
    lay["wqkv"] = w.reshape(3, 2, KC, 96).transpose(2, 0, 1, 3)
    lay["bqkv"] = np.stack([f["L0_tok_q_b"], f["L0_tok_k_b"], f["L0_tok_v_b"]])[None]
    projT = np.zeros((96, D + 1), np.float32)
    projT[:, 0:D] = f["L0_tok_proj_w"].T
    lay["projT"] = projT
    projb = np.ones((1, D + 1), np.float32)
    projb[0, 0:D] = f["L0_tok_proj_b"]
    lay["projb"] = projb
    e48 = np.zeros((1, 128), np.float32)
    e48[0, 48] = e48[0, LO + 48] = 1.0
    lay["e48"] = e48
    lay["eye"] = np.eye(128, dtype=np.float32)

    def pieces(w, n=2):
        return w.reshape(n, w.shape[0] // n, -1).transpose(1, 0, 2)

    lay["wqk"] = pieces(np.concatenate([f["L0_attn_Wq"], f["L0_attn_Wk"]], 1))
    lay["wff"] = pieces(np.concatenate([f["L0_attn_Wf"], f["L0_attn_Wf"]], 1))
    lay["bff"] = np.concatenate([f["L0_attn_bf"], f["L0_attn_bf"]])[:, None]
    lay["wv"] = pieces(f["L0_attn_Wv"])
    lay["wo2"] = pieces(f["L0_attn_Wo"])
    lay["gam2"] = f["L0_attn_gamma"].reshape(2, KC).T
    lay["bet2"] = f["L0_attn_beta"].reshape(2, KC).T
    lay["sgn"] = np.repeat(np.float32([1.0, -1.0]), 64)[:, None]
    lay["mask"] = np.triu(np.ones((T, T), np.float32))

    E = 8

    def parts(w):
        return np.stack([w[0:128], np.concatenate([w[128:D], w[128:D]], 0)], 1)

    lay["w1"] = parts(f["L0_ffn_w1"])
    lay["b1"] = f["L0_ffn_b1"][:, None]
    lay["w2"] = np.concatenate([f["L0_ffn_w2"], f["L0_ffn_b2"][None]], 0)
    lay["down"] = parts(f["L0_ffn_down_w"].transpose(1, 0, 2).reshape(D, E * 256)).reshape(128, 2, E, 256)
    lay["downb"] = f["L0_ffn_down_b"].reshape(E * 2, 128).T
    lay["up"] = f["L0_ffn_up_w"].reshape(E, 2, 128, D).transpose(2, 0, 1, 3)
    lay["gam3"] = np.broadcast_to(f["L0_ffn_gamma"], (T, D))
    lay["bet3"] = np.broadcast_to(f["L0_ffn_beta"], (T, D))
    lay["tri"] = np.broadcast_to(np.tril(np.ones((E, E), np.float32), -1), (T, E, E))
    lay["wT4"] = parts(f["L1_attn_w_qkv"].T)
    lay["wq4"] = parts(f["L1_attn_w_qkv"][0:D])
    lay["wpT4"] = parts(f["L1_attn_w_proj"].T)
    lay["heads"] = np.kron(np.eye(8, dtype=np.float32), np.ones((16, 16), np.float32))
    lay["bproj4"] = f["L1_attn_b_proj"][None]
    lay["win5"] = pieces(f["L1_ffn_w_in"].T)
    lay["wout5"] = pieces(f["L1_ffn_w_out"].T, 4)
    lay["gin5"] = np.broadcast_to(f["L1_ffn_g_in"], (T, D))
    lay["gout5"] = np.broadcast_to(f["L1_ffn_g_out"], (T, 512))

    nc = bacc.Bacc("TRN2", target_bir_lowering=False, num_devices=1)
    arrays, ins = {}, {}
    for name, a in lay.items():
        a = np.ascontiguousarray(a)
        arrays[f"in_{name}"] = a
        ins[name] = nc.dram_tensor(f"in_{name}", a.shape, mybir.dt.from_np(a.dtype), kind="ExternalInput").ap()
    out = nc.dram_tensor("out_0", (B, TOK, D), F32, kind="ExternalOutput").ap()
    vit_tower(nc, ins, out)
    r = run(nc, [arrays], core_ids=[0])
    return r.results[0]["out_0"]
```
